# Optimizing a Trainium2 kernel written in Bass

```python
import numpy as np
import jax
import jax.numpy as jnp

def _softmax(x, axis=-1):
    return jax.nn.softmax(x, axis=axis)

def _gelu(x):
    return jax.nn.gelu(x, approximate=True)

def _silu(x):
    return jax.nn.silu(x)

def _sigmoid(x):
    return jax.nn.sigmoid(x)

def _layernorm(x, axis=-1, eps=1e-05):
    m = jnp.mean(x, axis=axis, keepdims=True)
    v = jnp.var(x, axis=axis, keepdims=True)
    return (x - m) / jnp.sqrt(v + eps)

def _scatter_add(tgt, idx, src, axis=0):
    return tgt.at[idx].add(src)

def _segment_sum(src, seg, n):
    return jax.ops.segment_sum(src, seg, n)
kernel_name = 'mk_xattn_ffn_d2_seqx_r4_fcbc5c'

def setup_inputs(seed: int=0):
    np.random.seed(seed)
    _w = jnp.asarray

    def _rec_inputs():
        import jax
        import jax.numpy as jnp
        _rk = jax.random.key(seed)
        x = 0.002226 + 0.9996 * jax.random.normal(jax.random.fold_in(_rk, 1), (4, 512, 256), jnp.float32)
        _lenS = 512 - jax.random.randint(jax.random.fold_in(_rk, 7), (4,), 0, max(1, 512 // 4) + 1, jnp.int32)
        _lenS2 = 1601 - jax.random.randint(jax.random.fold_in(_rk, 8), (4,), 0, max(1, 1601 // 4) + 1, jnp.int32)
        _ctx_1024P = jax.random.normal(jax.random.fold_in(_rk, 11), (4, 16, 256), jnp.float32)
        _ctx_1024c = jax.random.dirichlet(jax.random.fold_in(_rk, 511), 0.3 * jnp.ones((16,), jnp.float32), (4, 1601))
        _ctx_1024t = jnp.einsum('bsk,bkd->bsd', _ctx_1024c, _ctx_1024P)
        _ctx_1024t = _ctx_1024t * jax.lax.rsqrt(jnp.mean(jnp.square(_ctx_1024t)) + 1e-12) * 0.953939
        ctx_1024 = -0.000125008 + 0.999885 * (_ctx_1024t + 0.3 * jax.random.normal(jax.random.fold_in(_rk, 611), (4, 1601, 256), jnp.float32))
        return (x, ctx_1024)
    x, ctx_1024 = _rec_inputs()

    def _L0_xattn_setup():
        import jax, jax.numpy as jnp
        import numpy as np
        B, M, N, DIM, DH, H = (8, 1024, 64, 256, 128, 8)
        INNER = DH * H
        EPS = 1e-05

        def _layernorm(x, g, b):
            mu = jnp.mean(x, axis=-1, keepdims=True)
            var = jnp.var(x, axis=-1, keepdims=True)
            return (x - mu) * jax.lax.rsqrt(var + EPS) * g + b
        key = jax.random.key(seed)
        ks = jax.random.split(key, 8)
        sd = 0.02
        return {'x': jax.random.normal(ks[0], (B, M, DIM), jnp.float32), 'latents': jax.random.normal(ks[1], (B, N, DIM), jnp.float32), 'gamma_media': jnp.ones((DIM,), jnp.float32), 'beta_media': jnp.zeros((DIM,), jnp.float32), 'gamma_lat': jnp.ones((DIM,), jnp.float32), 'beta_lat': jnp.zeros((DIM,), jnp.float32), 'Wq': jax.random.normal(ks[2], (DIM, INNER), jnp.float32) * sd, 'bq': jnp.zeros((INNER,), jnp.float32), 'Wkv': jax.random.normal(ks[3], (DIM, 2 * INNER), jnp.float32) * sd, 'bkv': jnp.zeros((2 * INNER,), jnp.float32), 'Wo': jax.random.normal(ks[4], (INNER, DIM), jnp.float32) * sd, 'bo': jnp.zeros((DIM,), jnp.float32)}
    _L0_xattn_all = _L0_xattn_setup()
    _L0_xattn_in = {k: v for k, v in _L0_xattn_all.items() if k in ('gamma_media', 'beta_media', 'gamma_lat', 'beta_lat', 'Wq', 'bq', 'Wkv', 'bkv', 'Wo', 'bo')}
    del _L0_xattn_all

    def _L0_ffn_setup():
        import jax, jax.numpy as jnp
        import numpy as np
        TOP_K = 2
        CAPACITY_FACTOR = 1.0
        key = jax.random.key(seed)
        ks = jax.random.split(key, 4)
        sl, bs, hs, ffn, E = (512, 8, 256, 1024, 8)
        x = jax.random.normal(ks[0], (sl, bs, hs), dtype=jnp.float32)
        w_router = jax.random.normal(ks[1], (hs, E), dtype=jnp.float32) * 0.02
        w1 = jax.random.normal(ks[2], (E, hs, ffn), dtype=jnp.float32) * 0.02
        w2 = jax.random.normal(ks[3], (E, ffn, hs), dtype=jnp.float32) * 0.02
        bias = jnp.zeros((1, 1, hs), dtype=jnp.float32)
        return {'x': x, 'w_router': w_router, 'w1': w1, 'w2': w2, 'bias': bias}
    _L0_ffn_all = _L0_ffn_setup()
    _L0_ffn_in = {k: v for k, v in _L0_ffn_all.items() if k in ('w_router', 'w1', 'w2', 'bias')}
    del _L0_ffn_all

    def _L1_xattn_setup():
        import jax, jax.numpy as jnp
        import numpy as np
        NUM_HEADS = 8

        def _split_heads(x, h):
            b, n, c = x.shape
            return x.reshape(b, n, h, c // h).transpose(0, 2, 1, 3)
        key = jax.random.key(seed)
        ks = jax.random.split(key, 5)
        B, N, K, C = (16, 1024, 64, 256)
        return {'img_fea': jax.random.normal(ks[0], (B, N, C), dtype=jnp.float32), 'aud_fea': jax.random.normal(ks[1], (B, K, C), dtype=jnp.float32), 'Wq': jax.random.normal(ks[2], (C, C), dtype=jnp.float32) * 0.02, 'Wk': jax.random.normal(ks[3], (C, C), dtype=jnp.float32) * 0.02, 'Wv': jax.random.normal(ks[4], (C, C), dtype=jnp.float32) * 0.02, 'aq': 1, 'sigmoid': 0, 'softmax': 1}
    _L1_xattn_all = _L1_xattn_setup()
    _L1_xattn_in = {k: v for k, v in _L1_xattn_all.items() if k in ('Wq', 'Wk', 'Wv')}
    del _L1_xattn_all

    def _L1_ffn_setup():
        import jax, jax.numpy as jnp
        import numpy as np
        from jax import lax
        D = 256
        H = 1024
        E = 8
        TOPK = 2
        key = jax.random.key(seed)
        ks = jax.random.split(key, 7)
        s = 0.02
        return {'x': jax.random.normal(ks[0], (2, 512, D), dtype=jnp.float32), 'W1': jax.random.normal(ks[1], (E, D, H), dtype=jnp.float32) * s, 'b1': jnp.zeros((E, H), dtype=jnp.float32), 'W2': jax.random.normal(ks[2], (E, H, D), dtype=jnp.float32) * s, 'b2': jnp.zeros((E, D), dtype=jnp.float32), 'Wr': jax.random.normal(ks[3], (D, E), dtype=jnp.float32) * s, 'br': jnp.zeros((E,), dtype=jnp.float32)}
    _L1_ffn_all = _L1_ffn_setup()
    _L1_ffn_in = {k: v for k, v in _L1_ffn_all.items() if k in ('W1', 'b1', 'W2', 'b2', 'Wr', 'br')}
    del _L1_ffn_all
    return {'x': x, 'ctx_1024': ctx_1024, 'L0_xattn_gamma_media': _L0_xattn_in['gamma_media'], 'L0_xattn_beta_media': _L0_xattn_in['beta_media'], 'L0_xattn_gamma_lat': _L0_xattn_in['gamma_lat'], 'L0_xattn_beta_lat': _L0_xattn_in['beta_lat'], 'L0_xattn_Wq': _L0_xattn_in['Wq'], 'L0_xattn_bq': _L0_xattn_in['bq'], 'L0_xattn_Wkv': _L0_xattn_in['Wkv'], 'L0_xattn_bkv': _L0_xattn_in['bkv'], 'L0_xattn_Wo': _L0_xattn_in['Wo'], 'L0_xattn_bo': _L0_xattn_in['bo'], 'L0_ffn_w_router': _L0_ffn_in['w_router'], 'L0_ffn_w1': _L0_ffn_in['w1'], 'L0_ffn_w2': _L0_ffn_in['w2'], 'L0_ffn_bias': _L0_ffn_in['bias'], 'L1_xattn_Wq': _L1_xattn_in['Wq'], 'L1_xattn_Wk': _L1_xattn_in['Wk'], 'L1_xattn_Wv': _L1_xattn_in['Wv'], 'L1_ffn_W1': _L1_ffn_in['W1'], 'L1_ffn_b1': _L1_ffn_in['b1'], 'L1_ffn_W2': _L1_ffn_in['W2'], 'L1_ffn_b2': _L1_ffn_in['b2'], 'L1_ffn_Wr': _L1_ffn_in['Wr'], 'L1_ffn_br': _L1_ffn_in['br']}

def reference(x, ctx_1024, L0_xattn_gamma_media, L0_xattn_beta_media, L0_xattn_gamma_lat, L0_xattn_beta_lat, L0_xattn_Wq, L0_xattn_bq, L0_xattn_Wkv, L0_xattn_bkv, L0_xattn_Wo, L0_xattn_bo, L0_ffn_w_router, L0_ffn_w1, L0_ffn_w2, L0_ffn_bias, L1_xattn_Wq, L1_xattn_Wk, L1_xattn_Wv, L1_ffn_W1, L1_ffn_b1, L1_ffn_W2, L1_ffn_b2, L1_ffn_Wr, L1_ffn_br):
    import jax
    import jax.numpy as jnp

    def _L0_xattn_ref(x, latents, gamma_media, beta_media, gamma_lat, beta_lat, Wq, bq, Wkv, bkv, Wo, bo):
        import jax, jax.numpy as jnp
        import numpy as np
        B, M, N, DIM, DH, H = (8, 1024, 64, 256, 128, 8)
        INNER = DH * H
        EPS = 1e-05

        def _layernorm(x, g, b):
            mu = jnp.mean(x, axis=-1, keepdims=True)
            var = jnp.var(x, axis=-1, keepdims=True)
            return (x - mu) * jax.lax.rsqrt(var + EPS) * g + b
        b = x.shape[0]
        xn = _layernorm(x, gamma_media, beta_media)
        ln = _layernorm(latents, gamma_lat, beta_lat)
        q = ln @ Wq + bq
        kv_input = jnp.concatenate([xn, ln], axis=1)
        kv = kv_input @ Wkv + bkv
        k, v = jnp.split(kv, 2, axis=-1)

        def to_heads(t):
            return t.reshape(b, t.shape[1], H, DH).transpose(0, 2, 1, 3)
        q, k, v = (to_heads(q), to_heads(k), to_heads(v))
        q = q * DH ** (-0.5)
        sim = jnp.einsum('bhid,bhjd->bhij', q, k)
        attn = jax.nn.softmax(sim, axis=-1)
        out = jnp.einsum('bhij,bhjd->bhid', attn, v)
        out = out.transpose(0, 2, 1, 3).reshape(b, -1, INNER)
        return out @ Wo + bo

    def _L0_ffn_ref(x, w_router, w1, w2, bias):
        import jax, jax.numpy as jnp
        import numpy as np
        TOP_K = 2
        CAPACITY_FACTOR = 1.0
        sl, bs, hs = x.shape
        E = w_router.shape[1]
        xf = x.reshape(-1, hs)
        T = xf.shape[0]
        capacity = int(CAPACITY_FACTOR * TOP_K * T / E)
        scores = jax.nn.softmax(xf @ w_router, axis=-1)
        expert_weights, top_experts = jax.lax.top_k(scores, TOP_K)
        flat_e = top_experts.reshape(-1)
        flat_w = expert_weights.reshape(-1)
        N = flat_e.shape[0]
        order = jnp.argsort(flat_e, stable=True)
        bin_ids = flat_e[order]
        tpe = jnp.zeros((E,), jnp.int32).at[flat_e].add(1)
        starts = jnp.cumsum(tpe) - tpe
        offsets = jnp.arange(N) - starts[bin_ids]
        valid = offsets < capacity
        slot = jnp.where(valid, bin_ids * capacity + offsets, E * capacity)
        src = order // TOP_K
        xb = jnp.zeros((E * capacity + 1, hs), x.dtype).at[slot].set(xf[src])
        xb = xb[:-1].reshape(E, capacity, hs)
        h = jax.nn.gelu(jnp.einsum('ech,ehf->ecf', xb, w1))
        y = jnp.einsum('ecf,efh->ech', h, w2).reshape(E * capacity, hs)
        yv = jnp.where(valid[:, None], y[jnp.minimum(slot, E * capacity - 1)], 0.0)
        out = jnp.zeros((T, hs), x.dtype).at[src].add(flat_w[order][:, None] * yv)
        return out.reshape(sl, bs, hs) + bias

    def _L1_xattn_ref(img_fea, aud_fea, Wq, Wk, Wv, aq, sigmoid, softmax):
        import jax, jax.numpy as jnp
        import numpy as np
        NUM_HEADS = 8

        def _split_heads(x, h):
            b, n, c = x.shape
            return x.reshape(b, n, h, c // h).transpose(0, 2, 1, 3)
        if aq:
            query, key, value = (aud_fea, img_fea, img_fea)
        else:
            query, key, value = (img_fea, aud_fea, aud_fea)
        B, Nq, C = query.shape
        h = NUM_HEADS
        scale = (C // h) ** (-0.5)
        q = _split_heads(query @ Wq.T, h)
        k = _split_heads(key @ Wk.T, h)
        v = _split_heads(value @ Wv.T, h)
        attn = jnp.einsum('bhnd,bhmd->bhnm', q, k) * scale
        if sigmoid:
            attn = jax.nn.sigmoid(attn)
        if softmax:
            attn = jax.nn.softmax(attn, axis=-1)
        x = jnp.einsum('bhnm,bhmd->bhnd', attn, v)
        return x.transpose(0, 2, 1, 3).reshape(B, Nq, C)

    def _L1_ffn_ref(x, W1, b1, W2, b2, Wr, br):
        import jax, jax.numpy as jnp
        import numpy as np
        from jax import lax
        D = 256
        H = 1024
        E = 8
        TOPK = 2
        B, S, _ = x.shape
        xf = x.reshape(-1, D)
        logits = xf @ Wr + br
        topv, _ = lax.top_k(logits, TOPK)
        thresh = topv[:, TOPK - 1:TOPK]
        masked = jnp.where(logits >= thresh, logits, -jnp.inf)
        weights = jax.nn.softmax(masked, axis=-1)
        h = jax.nn.gelu(jnp.einsum('td,edh->eth', xf, W1) + b1[:, None, :], approximate=False)
        expert_out = jnp.einsum('eth,ehd->etd', h, W2) + b2[:, None, :]
        out = jnp.einsum('etd,te->td', expert_out, weights)
        return out.reshape(B, S, D)
    x = x + _L0_xattn_ref(ctx_1024, _layernorm(x, axis=-1), L0_xattn_gamma_media, L0_xattn_beta_media, L0_xattn_gamma_lat, L0_xattn_beta_lat, L0_xattn_Wq, L0_xattn_bq, L0_xattn_Wkv, L0_xattn_bkv, L0_xattn_Wo, L0_xattn_bo)
    x = x + _L0_ffn_ref(_layernorm(x, axis=-1), L0_ffn_w_router, L0_ffn_w1, L0_ffn_w2, L0_ffn_bias)
    x = x + _L1_xattn_ref(ctx_1024, _layernorm(x, axis=-1), L1_xattn_Wq, L1_xattn_Wk, L1_xattn_Wv, 1, 0, 1)
    x = x + _L1_ffn_ref(_layernorm(x, axis=-1), L1_ffn_W1, L1_ffn_b1, L1_ffn_W2, L1_ffn_b2, L1_ffn_Wr, L1_ffn_br)
    return x

_drawn_inputs = setup_inputs


def setup_inputs(seed=0):
    import zlib

    import numpy as np

    out = dict(_drawn_inputs(seed))
    spreads = {'L0_xattn_gamma_media': (1.0, 0.6),
     'L0_xattn_beta_media': (0.0, 0.452),
     'L0_xattn_gamma_lat': (1.0, 0.6),
     'L0_xattn_beta_lat': (0.0, 0.8),
     'L0_xattn_bq': (0.0, 0.8),
     'L0_xattn_bkv': (0.0, 0.1),
     'L0_xattn_bo': (0.0, 0.1),
     'L0_ffn_bias': (0.0, 0.1),
     'L1_ffn_b1': (0.0, 0.32),
     'L1_ffn_b2': (0.0, 0.1),
     'L1_ffn_br': (0.0, 0.1)}
    factors = {'L0_xattn_Wq': 8.0, 'L1_xattn_Wq': 6.436, 'L1_xattn_Wk': 6.583}
    for name, (base, spread) in spreads.items():
        noise = np.random.default_rng([zlib.crc32(name.encode()), seed]).standard_normal(out[name].shape)
        drawn = base * np.exp(spread * noise) if base else spread * noise
        out[name] = jnp.asarray(drawn.astype(out[name].dtype))
    for name, factor in factors.items():
        out[name] = (out[name] * factor).astype(out[name].dtype)
    return out
```

```python
from contextlib import ExitStack

import concourse.bass as bass
from concourse import mybir

F32 = mybir.dt.float32
F16 = mybir.dt.float16
BF16 = mybir.dt.bfloat16
ALU = mybir.AluOpType
ACT = mybir.ActivationFunctionType
AX = mybir.AxisListType

P = 128
B, S, D = 4, 512, 256
M = 1601
KC = D // P
NT = B * S // P
ST = S // P
MT = -(-M // P)
MR = M - (MT - 1) * P
WS = 16.0
EPS = 1e-5

H0, DH0 = 8, 128
J0 = S + M
JT0 = -(-J0 // P)
JR0 = J0 - (JT0 - 1) * P
INNER = H0 * DH0


def done(per, n, k):
    return (n + 1) * per + k + 1


def rows(j, tiles, last):
    return last if j == tiles - 1 else P


class Chain:

    def __init__(self, eng, sem, base=0, ):
        self.eng, self.sem, self.count, self.base = eng, sem, 0, base

    def step(self, ins):
        ins.then_inc(self.sem, 1)
        self.count += 1

    def wait(self):
        self.eng.wait_ge(self.sem, self.base + self.count)


def chunks(total, size=512):
    return [(o, min(size, total - o)) for o in range(0, total, size)]


def attention0(nc, X, identf, io):
    KCH = chunks(J0)
    NA = 1 + len(KCH) + ST * len(KCH)
    NG = KC * -(-JT0 // 4)
    NV = JT0 * INNER // 512
    NW = NG + NV
    SCALE = DH0 ** -0.5 / (WS * WS)
    R = 3

    with ExitStack() as ctx:
        def sb(name, shape, dt):
            return ctx.enter_context(nc.sbuf_tensor("a_" + name, shape, dt))

        def pb(name, shape, dt=F32):
            return ctx.enter_context(nc.psum_tensor("a_" + name, shape, dt))

        def sem(name):
            return ctx.enter_context(nc.semaphore("a_" + name))

        wqh, wql = sb("wqh", [P, KC, INNER], F16), sb("wql", [P, KC, INNER], F16)
        wkvh, wkvl = sb("wkvh", [P, KC, 2 * INNER], F16), sb("wkvl", [P, KC, 2 * INNER], F16)
        woh, wol = sb("woh", [P, H0, D], F16), sb("wol", [P, H0, D], F16)
        vh, vl = sb("vh", [P, JT0, INNER], F16), sb("vl", [P, JT0, INNER], F16)
        stage_a = vh[:, 0:16, :].rearrange("p a b -> p (a b)").bitcast(F32)
        stage_b = vl[:, 0:16, :].rearrange("p a b -> p (a b)").bitcast(F32)
        wq_f = stage_a[:, 0:2048].rearrange("p (k n) -> p k n", k=KC)
        wkv_f = stage_a[:, 2048:6144].rearrange("p (k n) -> p k n", k=KC)
        wo_f = stage_b[:, 0:2048].rearrange("p (h n) -> p h n", h=H0)
        xth, xtl = sb("xth", [P, KC, J0], F16), sb("xtl", [P, KC, J0], F16)
        cx = sb("cx", [P, MT, D], F32)
        lat = sb("lat", [P, ST, D], F32)
        st = sb("st", [P, MT + ST, 6], F32)
        mv = sb("mv", [P, MT + ST, 2], F32)
        mhalf = sb("mhalf", [P, MT + ST], F32)
        rstd = sb("rstd", [P, MT + ST], F32)
        ve = sb("ve", [P, MT + ST], F32)
        tmp = sb("tmp", [P, 512], F32)
        gm, bm, gl, bl = (sb(n, [P, KC], F32) for n in ("gm", "bm", "gl", "bl"))
        bq, bkv = sb("bq", [P, H0], F32), sb("bkv", [P, 2 * H0], F32)
        bo = sb("bo", [1, D], F32)
        qh, ql = sb("qh", [P, 2, S], F16), sb("ql", [P, 2, S], F16)
        kh, kl = sb("kh", [P, 2, J0], F16), sb("kl", [P, 2, J0], F16)
        mx = sb("mx", [P, 2, ST, len(KCH)], F32)
        mc = sb("mc", [P, 2, ST], F32)
        mrow = sb("mrow", [1, 2, S], BF16)
        oneb = sb("oneb", [1, P], BF16)
        onef = sb("onef", [P, P], F32)
        four = sb("four", [P, 1], F32)
        pf = sb("pf", [P, R, S], F32)
        ph, pl = sb("ph", [P, R, S], F16), sb("pl", [P, R, S], F16)
        acc = sb("acc", [P, 2, S], F32)
        oh, ol = sb("oh", [P, S], F16), sb("ol", [P, S], F16)
        rl = sb("rl", [P, 2, ST], F32)
        brow = sb("brow", [1, D], F32)
        bb = sb("bb", [P, D], F32)

        psA = [pb(f"psA{i}", [P, 512]) for i in range(2)]
        psS = [pb(f"psS{i}", [P, 512]) for i in range(2)]
        psO = pb("psO", [P, 512])
        psW = pb("psW", [P, 2, D])
        psM = pb("psM", [P, 512])
        ring4 = psA + psS

        s_const = sem("const")
        s_small = sem("small")
        s_w = sem("w")
        s_wh = sem("wh")
        s_wl = sem("wl")
        s_b16 = sem("b16")
        s_br = sem("br")
        s_brow = sem("brow")
        s_cx = sem("cx")
        s_st = sem("st")
        s_mv = sem("mv")
        s_pool = sem("pool")
        s_rstd = sem("rstd")
        s_nt = sem("nt")
        s_wP = sem("wP")
        s_wH = sem("wH")
        s_wt = sem("wt")
        s_wL = sem("wL")
        s_aP = sem("aP")
        s_aH = sem("aH")
        s_aF = sem("aF")
        s_mc = sem("mc")
        s_mT = sem("mT")
        s_mrow = sem("mrow")
        s_sP = sem("sP")
        s_pF = sem("pF")
        s_pH = sem("pH")
        s_pL = sem("pL")
        s_pv = sem("pv")
        s_acc = sem("acc")
        s_oH = sem("oH")
        s_oL = sem("oL")
        s_lP = sem("lP")
        s_rl = sem("rl")
        s_yP = sem("yP")
        s_yF = sem("yF")
        s_fin = sem("fin")

        block = ctx.enter_context(nc.Block(no_gpsimd_drain=True))

        TAP, TMV = NG, NV

        @block.sync
        def _(sp):
            sp.dma_start(X[:, :, :], io["x"].rearrange("b (t p) c -> p (b t) c", p=P)).then_inc(s_small, 16)
            for name, t, k in (("L0_xattn_gamma_media", gm, KC), ("L0_xattn_beta_media", bm, KC),
                               ("L0_xattn_gamma_lat", gl, KC), ("L0_xattn_beta_lat", bl, KC),
                               ("L0_xattn_bq", bq, H0), ("L0_xattn_bkv", bkv, 2 * H0)):
                sp.dma_start(t[:, :], io[name].rearrange("(k p) -> p k", p=P),
                             allow_slow_non_contiguous=True).then_inc(s_small, 16)
            sp.dma_start(bo[:, :], io["L0_xattn_bo"].rearrange("(a n) -> a n", a=1)).then_inc(s_small, 16)
            with sp.Fori(0, B) as b:
                sp.wait_ge(s_wP, done(NW, b, -1) - NV)
                src = io["ctx_1024"][bass.ds(b, 1), :, :].rearrange("a m c -> (a m) c")
                sp.dma_start(cx[:, 0:MT - 1, :],
                             src[0:(MT - 1) * P, :].rearrange("(t p) c -> p t c", p=P)).then_inc(s_cx, 16)
                sp.dma_start(cx[0:MR, MT - 1, :], src[(MT - 1) * P:M, :]).then_inc(s_cx, 16)

        @block.gpsimd
        def _(g):
            for t, v in ((mhalf, -0.5), (onef, 1.0), (four, 4.0), (mv, 0.0), (oneb, 1.0)):
                g.memset(t[:], v).then_inc(s_const, 1)
            g.sem_inc(s_rstd, 3)
            g.sem_inc(s_acc, JT0)
            g.wait_ge(s_const, 5)
            sel = [(0, ST), (ST, ST + MT), (0, ST)]
            with g.Fori(0, B) as b:
                for r, (lo, hi) in enumerate(sel):
                    g.wait_ge(s_mv, b * 3 + r + 1)
                    g.nop(nofuse=True)
                    g.tensor_scalar(ve[:, lo:hi], mv[:, lo:hi, 1], EPS, None, ALU.add).then_inc(s_pool, 1)
                    g.wait_ge(s_pool, b * 3 + r + 1)
                    g.tensor_tensor(rstd[:, lo:hi], ve[:, lo:hi], mhalf[:, lo:hi], ALU.pow).then_inc(s_rstd, 1)

                def sums(h, p):
                    n = b * H0 + h
                    for j in range(JT0):
                        k = rows(j, JT0, JR0)
                        g.wait_ge(s_pF, done(JT0, n, j))
                        if j == 0:
                            g.wait_ge(s_lP, done(1, n, 0) - 2)
                            g.nop(nofuse=True)
                            g.tensor_copy(acc[:, p, :], pf[:, 0, :]).then_inc(s_acc, 1)
                        else:
                            g.wait_ge(s_acc, done(JT0, n, j - 1))
                            g.tensor_tensor(acc[0:k, p, :], acc[0:k, p, :], pf[0:k, j % R, :],
                                            ALU.add).then_inc(s_acc, 1)

                sums(0, 0)
                with g.Fori(0, 3) as t:
                    sums(t * 2 + 1, 1)
                    sums(t * 2 + 2, 0)
                sums(H0 - 1, 1)

        def ring_prev(j):
            if j >= R:
                return 0, j - R
            return -1, max(q for q in range(JT0) if q % R == j)

        def pre_slots():
            out = [[] for _ in range(JT0)]
            out[0] = ["A0", "A1"]
            out[1] = ["A2", "A3"]
            out[2] = ["A4", "A5"]
            for i in range(ST * len(KCH)):
                out[3 + i // 2].append(f"A{1 + len(KCH) + i}")
            out[13].append("mc")
            out[14].append("mT")
            return out

        SLOTS = pre_slots()

        @block.scalar
        def _(act):
            act.dma_start(wkv_f, io["L0_xattn_Wkv"].rearrange("(k p) n -> p k n", p=P)).then_inc(s_w, 16)
            act.dma_start(wq_f, io["L0_xattn_Wq"].rearrange("(k p) n -> p k n", p=P)).then_inc(s_w, 16)
            act.dma_start(wo_f, io["L0_xattn_Wo"].rearrange("(h p) n -> p h n", p=P)).then_inc(s_w, 16)
            act.sem_inc(s_wH, NW)
            act.sem_inc(s_aH, 1 + len(KCH))
            act.sem_inc(s_pF, JT0)
            act.sem_inc(s_pH, JT0)
            act.sem_inc(s_oH, 1)
            act.wait_ge(s_w, 48)
            act.wait_ge(s_small, 16 * 8)
            for hi, f in ((wkvh, wkv_f), (wqh, wq_f), (woh, wo_f)):
                act.activation(hi[:, :, :], f, ACT.Copy, scale=WS).then_inc(s_wh, 1)
            with act.Fori(0, B) as b:
                for i in range(NW):
                    act.wait_ge(s_wP, done(NW, b, i))
                    ps = ring4[i % 4]
                    if i < NG:
                        k, gidx = i % KC, i // KC
                        c0 = gidx * 512
                        n = min(512, J0 - c0)
                        gg, be = (gl, bl) if gidx == 0 else (gm, bm)
                        act.activation(xth[:, k, c0:c0 + n], ps[:, 0:n], ACT.Identity,
                                       bias=be[:, k:k + 1], scale=gg[:, k:k + 1]).then_inc(s_wH, 1)
                    else:
                        j, half = (i - NG) // 2, (i - NG) % 2
                        r = rows(j, JT0, JR0)
                        act.activation(vh[0:r, j, half * 512:half * 512 + 512], ps[0:r, :],
                                       ACT.Copy).then_inc(s_wH, 1)

                def pre(n, h, p, what):
                    if what[0] != "A":
                        return
                    a = int(what[1:])
                    if a > len(KCH):
                        return
                    act.wait_ge(s_aP, done(NA, n, a))
                    act.nop(nofuse=True)
                    if a == 0:
                        act.activation(qh[:, p, :], psA[0][:, :], ACT.Identity,
                                       bias=bq[:, bass.ds(h, 1)]).then_inc(s_aH, 1)
                    else:
                        c0, cn = KCH[a - 1]
                        act.activation(kh[:, p, c0:c0 + cn], psA[a % 2][:, 0:cn], ACT.Identity,
                                       bias=bkv[:, bass.ds(h, 1)]).then_inc(s_aH, 1)

                def out_hi(n):
                    act.wait_ge(s_pv, done(JT0, n, JT0 - 1))
                    act.wait_ge(s_yP, done(2, n, 1) - 2)
                    act.activation(oh[:, :], psO[:, :], ACT.Copy, scale=1.0 / 64).then_inc(s_oH, 1)

                def main(h, p, with_pre, with_tail):
                    n = b * H0 + h
                    if with_tail:
                        out_hi(n - 1)
                    for j in range(JT0):
                        r = rows(j, JT0, JR0)
                        dn, pj = ring_prev(j)
                        act.wait_ge(s_sP, done(JT0, n, j))
                        act.wait_ge(s_pL, done(JT0, n + dn, pj))
                        act.wait_ge(s_acc, done(JT0, n + dn, pj))
                        act.activation(pf[0:r, j % R, :], psS[j % 2][0:r, :], ACT.Exp,
                                       scale=SCALE).then_inc(s_pF, 1)
                        act.wait_ge(s_pv, done(JT0, n + dn, pj))
                        act.activation(ph[0:r, j % R, :], psS[j % 2][0:r, :], ACT.Exp,
                                       scale=SCALE).then_inc(s_pH, 1)
                        if with_pre:
                            for what in SLOTS[j]:
                                pre(n + 1, h + 1, 1 - p, what)

                for what in sum(SLOTS, []):
                    pre(b * H0, b * 0, 0, what)
                main(b * 0, 0, True, False)
                with act.Fori(0, 3) as t:
                    main(t * 2 + 1, 1, True, True)
                    main(t * 2 + 2, 0, True, True)
                main(b * 0 + (H0 - 1), 1, False, True)
                out_hi(b * H0 + (H0 - 1))

        @block.tensor
        def _(pe):
            pe.sem_inc(s_wP, NW)
            pe.sem_inc(s_aP, NA)
            pe.sem_inc(s_mT, 1)
            pe.sem_inc(s_sP, JT0)
            pe.sem_inc(s_pv, JT0)
            pe.sem_inc(s_lP, 2)
            pe.sem_inc(s_yP, 2)
            pe.wait_ge(s_const, 5)
            pe.wait_ge(s_small, 16 * 8)
            pe.wait_ge(s_w, 48)
            for h in range(H0):
                pe.matmul(psM[0:1, 0:D], bkv[:, H0 + h:H0 + h + 1], wo_f[:, h, :], start=(h == 0), stop=False)
            pe.matmul(psM[0:1, 0:D], onef[0:1, 0:1], bo[:, :], start=False, stop=True).then_inc(s_br, 1)
            pe.wait_ge(s_brow, 1)
            pe.matmul(psM[:, 0:D], onef[0:1, :], brow[:, :], start=True, stop=True).then_inc(s_br, 1)
            pe.wait_ge(s_brow, 2)

            def triple(out, hi, lo, xh_, xl_, first=True, last=True):
                pe.matmul(out, hi, xh_, start=first, stop=False)
                pe.matmul(out, hi, xl_, start=False, stop=False)
                return pe.matmul(out, lo, xh_, start=False, stop=last)

            with pe.Fori(0, B) as b:
                for i in range(NW):
                    if i < 4:
                        if i == 0:
                            pe.wait_ge(s_aF, (b * H0) * NA + NA)
                            pe.wait_ge(s_pH, (b * H0) * JT0 + JT0)
                    else:
                        pe.wait_ge(s_wL, done(NW, b, NG - 1 if i == NG else i - 4))
                    ps = ring4[i % 4]
                    if i < NG:
                        k, gidx = i % KC, i // KC
                        pe.wait_ge(s_nt, b * 2 + (1 if gidx == 0 else 2))
                        for u in range(4):
                            tl = gidx * 4 + u
                            if tl >= JT0:
                                break
                            r = rows(tl, JT0, JR0)
                            src = lat[:, tl, :] if tl < ST else cx[0:r, tl - ST, :]
                            ins = pe.transpose(ps[:, u * P:u * P + r], src[:, k * P:(k + 1) * P], identf[0:r, 0:r])
                        ins.then_inc(s_wP, 1)
                    else:
                        j, half = (i - NG) // 2, (i - NG) % 2
                        r = rows(j, JT0, JR0)
                        if i == NG:
                            pe.wait_ge(s_wl, 3)
                        for k in range(KC):
                            cs = slice(j * P, j * P + r)
                            ws = slice(INNER + half * 512, INNER + half * 512 + 512)
                            ins = triple(ps[0:r, :], xth[:, k, cs], xtl[:, k, cs], wkvh[:, k, ws], wkvl[:, k, ws],
                                         k == 0, k == KC - 1)
                        ins.then_inc(s_wP, 1)

                def pre(n, h, p, what):
                    if what == "mc":
                        return
                    if what == "mT":
                        pe.wait_ge(s_mc, done(1, n, 0))
                        pe.wait_ge(s_rl, done(1, n, 0) - 2)
                        for it in range(ST):
                            ins = pe.transpose(psM[0:1, it * P:(it + 1) * P], mc[:, p, it:it + 1], identf[:, :])
                        ins.then_inc(s_mT, 1)
                        return
                    a = int(what[1:])
                    ps = psA[a % 2]
                    pe.wait_ge(s_aF, done(NA, n, a - 2))
                    if a == 0:
                        for k in range(KC):
                            ws = bass.ds(h * DH0, DH0)
                            ins = triple(ps[:, 0:S], wqh[:, k, ws], wql[:, k, ws], xth[:, k, 0:S], xtl[:, k, 0:S],
                                         k == 0, k == KC - 1)
                    elif a <= len(KCH):
                        c0, cn = KCH[a - 1]
                        for k in range(KC):
                            ws = bass.ds(h * DH0, DH0)
                            ins = triple(ps[:, 0:cn], wkvh[:, k, ws], wkvl[:, k, ws], xth[:, k, c0:c0 + cn],
                                         xtl[:, k, c0:c0 + cn], k == 0, k == KC - 1)
                    else:
                        it, c = divmod(a - 1 - len(KCH), len(KCH))
                        c0, cn = KCH[c]
                        ins = pe.matmul(ps[:, 0:cn], qh[:, p, it * P:(it + 1) * P], kh[:, p, c0:c0 + cn],
                                        start=True, stop=True)
                    ins.then_inc(s_aP, 1)

                def pv(n, h, p, j):
                    r = rows(j, JT0, JR0)
                    s = j % R
                    vs = bass.ds(h * DH0, DH0)
                    pe.wait_ge(s_pL, done(JT0, n, j))
                    if j == 0:
                        pe.wait_ge(s_oL, done(1, n, 0) - 1)
                    pe.matmul(psO[:, :], vh[0:r, j, vs], ph[0:r, s, :], start=(j == 0), stop=False)
                    pe.matmul(psO[:, :], vh[0:r, j, vs], pl[0:r, s, :], start=False, stop=False)
                    pe.matmul(psO[:, :], vl[0:r, j, vs], ph[0:r, s, :], start=False,
                              stop=(j == JT0 - 1)).then_inc(s_pv, 1)

                def tail(n, h, p, step):
                    if step == 0:
                        pe.wait_ge(s_acc, done(JT0, n, JT0 - 1))
                        pe.wait_ge(s_mrow, done(1, n, 0))
                        for it in range(ST):
                            ins = pe.matmul(psM[:, it:it + 1], acc[:, p, it * P:(it + 1) * P], four[:, :],
                                            start=True, stop=True)
                        ins.then_inc(s_lP, 1)
                        return
                    pe.wait_ge(s_oL, done(1, n, 0))
                    pe.wait_ge(s_yF, done(2, n, step - 1) - 1)
                    for u in range(2):
                        it = 2 * (step - 1) + u
                        cs = slice(it * P, (it + 1) * P)
                        ins = triple(psW[:, u, :], oh[:, cs], ol[:, cs], woh[:, bass.ds(h, 1), :].rearrange("p a n -> p (a n)"),
                                     wol[:, bass.ds(h, 1), :].rearrange("p a n -> p (a n)"))
                    ins.then_inc(s_yP, 1)

                def main(h, p, with_pre, with_tail):
                    n = b * H0 + h
                    for j in range(JT0):
                        r = rows(j, JT0, JR0)
                        js = slice(j * P, j * P + r)
                        pe.wait_ge(s_pH, done(JT0, n, j - 2) if j >= 2 else done(JT0, n - 1, JT0 - 1 - (j + JT0 - 1) % 2))
                        if j == 0:
                            pe.wait_ge(s_mrow, done(1, n, 0))
                        ps = psS[j % 2][0:r, :]
                        triple(ps, kh[:, p, js], kl[:, p, js], qh[:, p, :], ql[:, p, :], True, False)
                        pe.matmul(ps, oneb[:, 0:r], mrow[:, p, :], start=False, stop=True).then_inc(s_sP, 1)
                        if j >= 1:
                            pv(n, h, p, j - 1)
                        if with_tail and j in (1, 2, 4):
                            tail(n - 1, h - 1, 1 - p, (1, 2, 4).index(j))
                        if with_pre:
                            for what in SLOTS[j]:
                                pre(n + 1, h + 1, 1 - p, what)
                    pv(n, h, p, JT0 - 1)

                pe.wait_ge(s_wL, done(NW, b, NW - 1))
                for what in sum(SLOTS, []):
                    pre(b * H0, b * 0, 0, what)
                main(b * 0, 0, True, False)
                with pe.Fori(0, 3) as t:
                    main(t * 2 + 1, 1, True, True)
                    main(t * 2 + 2, 0, True, True)
                main(b * 0 + (H0 - 1), 1, False, True)
                for step in range(3):
                    tail(b * H0 + (H0 - 1), b * 0 + (H0 - 1), 1, step)

        @block.vector
        def _(v):
            v.sem_inc(s_wL, NW)
            v.sem_inc(s_aF, NA)
            v.sem_inc(s_mc, 1)
            v.sem_inc(s_mrow, 1)
            v.sem_inc(s_pL, JT0)
            v.sem_inc(s_oL, 1)
            v.sem_inc(s_rl, 2)
            v.sem_inc(s_yF, 2)
            v.wait_ge(s_small, 16 * 8)
            v.tensor_scalar(bq[:, :], bq[:, :], WS, None, ALU.mult).then_inc(s_b16, 1)
            v.tensor_scalar(bkv[:, 0:H0], bkv[:, 0:H0], WS, None, ALU.mult).then_inc(s_b16, 1)
            v.wait_ge(s_br, 1)
            v.tensor_copy(brow[:, :], psM[0:1, 0:D]).then_inc(s_brow, 1)
            v.wait_ge(s_br, 2)
            v.tensor_copy(bb[:, :], psM[:, 0:D]).then_inc(s_brow, 1)
            for i, (lo, f, hi) in enumerate(((wkvl, wkv_f, wkvh), (wql, wq_f, wqh), (wol, wo_f, woh))):
                v.wait_ge(s_wh, i + 1)
                v.scalar_tensor_tensor(lo[:, :, :], f, WS, hi[:, :, :], ALU.mult, ALU.subtract).then_inc(s_wl, 1)
            v.wait_ge(s_const, 5)
            v.wait_ge(s_b16, 2)
            steps = [0]
            NST = 4 * ST + 2 * MT + 2 * ST + MT

            with v.Fori(0, B) as b:
                steps[0] = 0

                def step(ins):
                    ins.then_inc(s_st, 1)
                    steps[0] += 1

                def own():
                    v.wait_ge(s_st, b * NST + steps[0])

                def stats(src, slot, r=P):
                    step(v.bn_stats(st[0:r, slot, :], src))

                def aggr(slots, last_rows=P):
                    own()
                    v.nop(nofuse=True)
                    for q, s in enumerate(slots):
                        r = last_rows if q == len(slots) - 1 else P
                        step(v.bn_aggr(mv[0:r, s, :], st[0:r, s, :]))

                for u in range(ST):
                    stats(X[:, bass.ds(b * ST + u, 1), :].rearrange("p a c -> p (a c)"), u)
                aggr(range(ST))
                own()
                v.sem_inc(s_mv, 1)
                v.wait_ge(s_cx, b * 32 + 32)
                for u in range(MT):
                    r = rows(u, MT, MR)
                    stats(cx[0:r, u, :], ST + u, r)
                aggr(range(ST, ST + MT), MR)
                own()
                v.sem_inc(s_mv, 1)
                v.wait_ge(s_rstd, b * 3 + 3 + 1)
                for u in range(ST):
                    step(v.tensor_scalar(lat[:, u, :], X[:, bass.ds(b * ST + u, 1), :].rearrange("p a c -> p (a c)"),
                                         mv[:, u, 0:1], rstd[:, u:u + 1], ALU.subtract, ALU.mult))
                own()
                for u in range(ST):
                    stats(lat[:, u, :], u)
                aggr(range(ST))
                own()
                v.sem_inc(s_mv, 1)
                v.wait_ge(s_rstd, b * 3 + 3 + 2)
                for u in range(MT):
                    r = rows(u, MT, MR)
                    step(v.tensor_scalar(cx[0:r, u, :], cx[0:r, u, :], mv[0:r, ST + u, 0:1],
                                         rstd[0:r, ST + u:ST + u + 1], ALU.subtract, ALU.mult))
                v.wait_ge(s_rstd, b * 3 + 3 + 3)
                for u in range(ST):
                    step(v.tensor_scalar(lat[:, u, :], lat[:, u, :], mv[:, u, 0:1], rstd[:, u:u + 1],
                                         ALU.subtract, ALU.mult))
                own()
                v.sem_inc(s_nt, 2)

                for i in range(NW):
                    v.wait_ge(s_wH, done(NW, b, i))
                    ps = ring4[i % 4]
                    if i < NG:
                        k, gidx = i % KC, i // KC
                        c0 = gidx * 512
                        n = min(512, J0 - c0)
                        gg, be = (gl, bl) if gidx == 0 else (gm, bm)
                        if i >= 1:
                            v.wait_ge(s_wL, done(NW, b, i - 1))
                        v.tensor_scalar(tmp[:, 0:n], ps[:, 0:n], gg[:, k:k + 1], be[:, k:k + 1],
                                        ALU.mult, ALU.add).then_inc(s_wt, 1)
                        v.wait_ge(s_wt, b * NG + i + 1)
                        v.tensor_tensor(xtl[:, k, c0:c0 + n], tmp[:, 0:n], xth[:, k, c0:c0 + n],
                                        ALU.subtract).then_inc(s_wL, 1)
                    else:
                        j, half = (i - NG) // 2, (i - NG) % 2
                        r = rows(j, JT0, JR0)
                        cs = slice(half * 512, half * 512 + 512)
                        v.tensor_tensor(vl[0:r, j, cs], ps[0:r, :], vh[0:r, j, cs], ALU.subtract).then_inc(s_wL, 1)

                def pre(n, h, p, what):
                    if what == "mc":
                        v.wait_ge(s_aF, done(NA, n, NA - 1))
                        v.tensor_reduce(mc[:, p, :], mx[:, p, :, :], AX.X, ALU.max).then_inc(s_mc, 1)
                        return
                    if what == "mT":
                        v.wait_ge(s_mT, done(1, n, 0))
                        v.tensor_scalar(mrow[:, p, :], psM[0:1, :], -1.0, None, ALU.mult).then_inc(s_mrow, 1)
                        return
                    a = int(what[1:])
                    ps = psA[a % 2]
                    if a <= len(KCH):
                        v.wait_ge(s_aH, done(1 + len(KCH), n, a))
                        if a == 0:
                            v.scalar_tensor_tensor(ql[:, p, :], ps[:, :], bq[:, bass.ds(h, 1)], qh[:, p, :],
                                                   ALU.add, ALU.subtract).then_inc(s_aF, 1)
                        else:
                            c0, cn = KCH[a - 1]
                            v.scalar_tensor_tensor(kl[:, p, c0:c0 + cn], ps[:, 0:cn], bkv[:, bass.ds(h, 1)],
                                                   kh[:, p, c0:c0 + cn], ALU.add, ALU.subtract).then_inc(s_aF, 1)
                    else:
                        it, c = divmod(a - 1 - len(KCH), len(KCH))
                        c0, cn = KCH[c]
                        v.wait_ge(s_aP, done(NA, n, a))
                        v.tensor_reduce(mx[:, p, it, c:c + 1], ps[:, 0:cn], AX.X, ALU.max).then_inc(s_aF, 1)

                def out_lo(n):
                    v.wait_ge(s_oH, done(1, n, 0))
                    v.wait_ge(s_yP, done(2, n, 1) - 2)
                    v.scalar_tensor_tensor(ol[:, :], psO[:, :], 1.0 / 64, oh[:, :], ALU.mult,
                                           ALU.subtract).then_inc(s_oL, 1)

                def tail(n, h, p, step_):
                    if step_ == 0:
                        v.wait_ge(s_lP, done(1, n, 0) + 1)
                        v.reciprocal(rl[:, p, :], psM[:, 0:ST]).then_inc(s_rl, 1)
                        return
                    v.wait_ge(s_yP, done(2, n, step_ - 1))
                    v.wait_ge(s_rl, done(1, n, 0) + 1)
                    if step_ == 1:
                        v.wait_ge(s_yF, done(2, n, -1))
                    for u in range(2):
                        it = 2 * (step_ - 1) + u
                        xs = X[:, bass.ds(b * ST + it, 1), :].rearrange("p a c -> p (a c)")
                        ins = v.scalar_tensor_tensor(xs, psW[:, u, :], rl[:, p, it:it + 1], xs, ALU.mult, ALU.add)
                    ins.then_inc(s_yF, 1)

                def main(h, p, with_pre, with_tail):
                    n = b * H0 + h
                    if with_tail:
                        out_lo(n - 1)
                    for j in range(JT0):
                        r = rows(j, JT0, JR0)
                        dn, pj = ring_prev(j)
                        v.wait_ge(s_pH, done(JT0, n, j))
                        v.wait_ge(s_pv, done(JT0, n + dn, pj))
                        v.tensor_tensor(pl[0:r, j % R, :], pf[0:r, j % R, :], ph[0:r, j % R, :],
                                        ALU.subtract).then_inc(s_pL, 1)
                        if with_tail and j in (1, 2, 4):
                            tail(n - 1, h - 1, 1 - p, (1, 2, 4).index(j))
                        if with_pre:
                            for what in SLOTS[j]:
                                pre(n + 1, h + 1, 1 - p, what)

                for what in sum(SLOTS, []):
                    pre(b * H0, b * 0, 0, what)
                main(b * 0, 0, True, False)
                with v.Fori(0, 3) as t:
                    main(t * 2 + 1, 1, True, True)
                    main(t * 2 + 2, 0, True, True)
                main(b * 0 + (H0 - 1), 1, False, True)
                out_lo(b * H0 + (H0 - 1))
                for step_ in range(3):
                    tail(b * H0 + (H0 - 1), b * 0 + (H0 - 1), 1, step_)
            v.wait_ge(s_yF, 2 * (B * H0 + 1))
            for t in range(NT):
                ins = v.tensor_tensor(X[:, t, :], X[:, t, :], bb[:, :], ALU.add)
            ins.then_inc(s_fin, 1)
            v.wait_ge(s_fin, 1)


def experts(nc, X, identf, io, layer):
    E, F = 8, 1024
    FT = F // P
    CH = 512
    NCH = B * S // CH
    IT = CH // P
    CAP = 2 * B * S // E
    names = {0: ("L0_ffn_w_router", "L0_ffn_w1", "L0_ffn_w2"),
             1: ("L1_ffn_Wr", "L1_ffn_W1", "L1_ffn_W2")}[layer]
    GELU = ACT.Gelu_apprx_tanh if layer == 0 else ACT.Gelu
    GI = KC * NT // 4

    with ExitStack() as ctx:
        tag = f"f{layer}_"

        def sb(name, shape, dt=F32):
            return ctx.enter_context(nc.sbuf_tensor(tag + name, shape, dt))

        def sem(name):
            return ctx.enter_context(nc.semaphore(tag + name))

        xn = sb("xn", [P, NT, D])
        st, mv = sb("st", [P, NT, 6]), sb("mv", [P, NT, 2])
        ve, mhalf, rstd = sb("ve", [P, NT]), sb("mhalf", [P, NT]), sb("rstd", [P, NT])
        xth, xtl = sb("xth", [P, KC, B * S], F16), sb("xtl", [P, KC, B * S], F16)
        wr, wrh, wrl = sb("wr", [P, KC, E]), sb("wrh", [P, KC, E], F16), sb("wrl", [P, KC, E], F16)
        brb = sb("brb", [P, E])
        b2 = sb("b2", [E, D])
        bias = sb("bias", [1, D])
        b1r = sb("b1r", [E * FT, P])
        b1 = sb("b1", [P, E, FT])
        b1e = sb("b1e", [P, 2, FT])
        ones = sb("ones", [P, P])
        upper = sb("upper", [P, P])
        revi = sb("revi", [P, E])
        lg = sb("lg", [P, NT, E])
        sh, ex, sc, sc2, eq, cand, oh1, oh2, wgt, wgs, off, tot, rank, valid = (
            sb(n, [P, NT, E]) for n in ("sh", "ex", "sc", "sc2", "eq", "cand", "oh1", "oh2", "wgt", "wgs", "off",
                                        "tot", "rank", "valid"))
        m1, m2, f1, sm, rs = (sb(n, [P, NT]) for n in ("m1", "m2", "f1", "sm", "rs"))
        wt = sb("wt", [E, NT, P])
        w1f, w2f = sb("w1f", [P, KC, F]), sb("w2f", [P, FT, D])
        w1h, w1l = sb("w1h", [P, 2, KC, F], F16), sb("w1l", [P, 2, KC, F], F16)
        w2h, w2l = sb("w2h", [P, 2, FT, D], F16), sb("w2l", [P, 2, FT, D], F16)
        R = 4
        hf = sb("hf", [P, R, CH])
        hh, hl = sb("hh", [P, R, CH], F16), sb("hl", [P, R, CH], F16)
        psH = [ctx.enter_context(nc.psum_tensor(tag + f"psH{i}", [P, 512], F32)) for i in range(4)]
        psY = [ctx.enter_context(nc.psum_tensor(tag + f"psY{i}", [P, 512], F32)) for i in range(IT)]

        s_const = sem("const")
        s_small = sem("small")
        s_w = sem("w")
        s_st = sem("st")
        s_mv = sem("mv")
        s_pool = sem("pool")
        s_rstd = sem("rstd")
        s_nt = sem("nt")
        s_tP = sem("tP")
        s_tH = sem("tH")
        s_tL = sem("tL")
        s_wr = sem("wr")
        s_lg = sem("lg")
        s_b1 = sem("b1")
        s_sh = sem("sh")
        s_ex = sem("ex")
        s_sel = sem("sel")
        s_rk = sem("rk")
        s_wg = sem("wg")
        s_wtP = sem("wtP")
        s_wtF = sem("wtF")
        s_wh = sem("wh")
        s_wl = sem("wl")
        s_hP = sem("hP")
        s_hH = sem("hH")
        s_hF = sem("hF")
        s_hL = sem("hL")
        s_y = sem("y")
        s_yF = sem("yF")

        block = ctx.enter_context(nc.Block(no_gpsimd_drain=True))
        NSMALL = 5 if layer else 2

        @block.sync
        def _(sp):
            sp.dma_start(wr[:, :, :], io[names[0]].rearrange("(k p) e -> p k e", p=P)).then_inc(s_small, 16)
            if layer:
                sp.dma_start(brb[:, :], io["L1_ffn_br"].rearrange("(a e) -> a e", a=1).to_broadcast([P, E])
                             ).then_inc(s_small, 16)
                sp.dma_start(b2[:, :], io["L1_ffn_b2"]).then_inc(s_small, 16)
                sp.dma_start(b1r[:, :], io["L1_ffn_b1"].rearrange("e (f p) -> (e f) p", p=P)).then_inc(s_small, 16)
                sp.dma_start(bias[:, :], io["L1_ffn_b2"][0:1, :]).then_inc(s_small, 16)
            else:
                sp.dma_start(bias[:, :], io["L0_ffn_bias"].rearrange("a b d -> (a b) d")).then_inc(s_small, 16)
            with sp.Fori(0, E) as e:
                sp.wait_ge(s_wl, e + 1)
                sp.dma_start(w1f[:, :, :], io[names[1]][bass.ds(e, 1)].rearrange("a (k p) f -> p (a k) f", p=P)
                             ).then_inc(s_w, 16)
                sp.dma_start(w2f[:, :, :], io[names[2]][bass.ds(e, 1)].rearrange("a (f p) d -> p (a f) d", p=P)
                             ).then_inc(s_w, 16)

        @block.gpsimd
        def _(g):
            for t, val in ((mhalf, -0.5), (ones, 1.0), (upper, 0.0)):
                g.memset(t[:], val).then_inc(s_const, 1)
            for e in range(E):
                g.memset(revi[:, e:e + 1], float(E - e)).then_inc(s_const, 1)
            g.sem_inc(s_wh, 1)
            g.wait_ge(s_const, 3 + E)
            g.affine_select(out=upper[:, :], in_=upper[:, :], compare_op=ALU.is_ge, fill=1.0, base=0,
                            pattern=[[-1, P]], channel_multiplier=1).then_inc(s_const, 1)
            g.wait_ge(s_mv, 1)
            g.tensor_scalar(ve[:, :], mv[:, :, 1], EPS, None, ALU.add).then_inc(s_pool, 1)
            g.wait_ge(s_pool, 1)
            g.tensor_tensor(rstd[:, :], ve[:, :], mhalf[:, :], ALU.pow).then_inc(s_rstd, 1)
            with g.Fori(0, E // 2) as gg:
                for p in range(2):
                    e = gg * 2 + p
                    g.wait_ge(s_w, e * 32 + 32)
                    g.wait_ge(s_yF, e * NCH + 1)
                    g.nop(nofuse=True)
                    g.tensor_scalar(w1h[:, p, :, :], w1f[:, :, :], WS, None, ALU.mult)
                    g.tensor_scalar(w2h[:, p, :, :], w2f[:, :, :], WS, None, ALU.mult).then_inc(s_wh, 1)

        @block.scalar
        def _(act):
            act.sem_inc(s_hH, FT)
            act.sem_inc(s_hF, FT)
            act.wait_ge(s_small, 16 * NSMALL)
            act.activation(wrh[:, :, :], wr[:, :, :], ACT.Copy, scale=WS).then_inc(s_wr, 1)
            for i in range(GI):
                k, q = i % KC, i // KC
                act.wait_ge(s_tP, i + 1)
                act.activation(xth[:, k, q * 512:q * 512 + 512], psH[i % 4][:, :], ACT.Copy).then_inc(s_tH, 1)
            act.wait_ge(s_sh, 1)
            act.activation(ex[:, :, :], sh[:, :, :], ACT.Exp).then_inc(s_ex, 1)
            with act.Fori(0, E // 2) as gg:
                for p in range(2):
                    e = gg * 2 + p
                    with act.Fori(0, NCH) as c:
                        n = e * NCH + c
                        for f in range(FT):
                            act.wait_ge(s_hP, n * FT + f + 1)
                            act.wait_ge(s_y, done(FT, n, f - R))
                            bs = b1e[:, p, f:f + 1] if layer else 0.0
                            act.activation(hh[:, f % R, :], psH[f % 4][:, :], GELU, bias=bs,
                                           scale=1.0 / WS).then_inc(s_hH, 1)
                            act.wait_ge(s_hL, done(FT, n, f - R))
                            act.activation(hf[:, f % R, :], psH[f % 4][:, :], GELU, bias=bs,
                                           scale=1.0 / WS).then_inc(s_hF, 1)

        @block.tensor
        def _(pe):
            pe.sem_inc(s_y, FT)
            pe.wait_ge(s_const, 4 + E)
            pe.wait_ge(s_small, 16 * NSMALL)
            for i in range(GI):
                k, q = i % KC, i // KC
                pe.wait_ge(s_nt, 4 * q + 4)
                if i >= 4:
                    pe.wait_ge(s_tL, i - 3)
                for u in range(4):
                    ins = pe.transpose(psH[i % 4][:, u * P:(u + 1) * P], xn[:, 4 * q + u, k * P:(k + 1) * P],
                                       identf[:, :])
                ins.then_inc(s_tP, 1)
            if layer:
                pe.transpose(psY[1][:, 0:E * FT], b1r[:, :], identf[0:E * FT, 0:E * FT]).then_inc(s_b1, 1)
            pe.wait_ge(s_tL, GI)
            pe.wait_ge(s_wr, 2)
            for t in range(NT):
                ts = slice(t * P, (t + 1) * P)
                for k in range(KC):
                    for m, (a, w) in enumerate(((xth, wrh), (xth, wrl), (xtl, wrh))):
                        ins = pe.matmul(psY[0][:, t * E:(t + 1) * E], a[:, k, ts], w[:, k, :],
                                        start=(k == 0 and m == 0), stop=(k == KC - 1 and m == 2))
            ins.then_inc(s_lg, 1)
            if not layer:
                pe.wait_ge(s_sel, 1)
                sel = cand[:, :, :].rearrange("p t e -> p (t e)")
                pe.matmul(psY[2][:, 0:NT * E], upper[:, :], sel, start=True, stop=True)
                pe.matmul(psY[3][:, 0:NT * E], ones[:, :], sel, start=True, stop=True).then_inc(s_rk, 1)
            pe.wait_ge(s_wg, 1)
            if layer:
                for q in range(NT // 4):
                    for u in range(4):
                        ins = pe.transpose(psH[q][0:E, u * P:(u + 1) * P], wgt[:, 4 * q + u, :], identf[:, :])
                    ins.then_inc(s_wtP, 1)
            for t in range(NT):
                if layer:
                    pe.wait_ge(s_wtF, t // 4 + 1 if t < 4 else NT // 4 + t - 3)
                    if t < 4:
                        pe.wait_ge(s_wtF, NT // 4)
                    ins = pe.matmul(psY[t % 4][:, 0:D], wt[:, t, :], b2[:, :], start=True, stop=True)
                else:
                    if t >= 4:
                        pe.wait_ge(s_wtF, t - 3)
                    ins = pe.matmul(psY[t % 4][:, 0:D], ones[0:1, :], bias[:, :], start=True, stop=True)
                ins.then_inc(s_wtP, 1)
            pe.wait_ge(s_wtF, NT + (NT // 4 if layer else 0))

            with pe.Fori(0, E // 2) as gg:
                for p in range(2):
                    e = gg * 2 + p
                    pe.wait_ge(s_wl, e + 2)
                    pe.nop(nofuse=True)
                    with pe.Fori(0, NCH) as c:
                        n = e * NCH + c

                        def hidden(f):
                            pe.wait_ge(s_hF, done(FT, n, f - 4))
                            fs = slice(f * P, (f + 1) * P)
                            for k in range(KC):
                                xh_, xl_ = (x[:, k, bass.ds(c * CH, CH)] for x in (xth, xtl))
                                ps = psH[f % 4][:, :]
                                pe.matmul(ps, w1h[:, p, k, fs], xh_, start=(k == 0), stop=False)
                                pe.matmul(ps, w1h[:, p, k, fs], xl_, start=False, stop=False)
                                ins = pe.matmul(ps, w1l[:, p, k, fs], xh_, start=False, stop=(k == KC - 1))
                            ins.then_inc(s_hP, 1)

                        def output(f):
                            if f == 0:
                                pe.wait_ge(s_yF, n + 1)
                            pe.wait_ge(s_hH, done(FT, n, f))
                            for it in range(IT):
                                cs = slice(it * P, (it + 1) * P)
                                pe.matmul(psY[it][:, 0:D], hh[:, f % R, cs], w2h[:, p, f, :], start=(f == 0),
                                          stop=False)
                                pe.matmul(psY[it][:, 0:D], hh[:, f % R, cs], w2l[:, p, f, :], start=False,
                                          stop=False)
                            pe.wait_ge(s_hL, done(FT, n, f))
                            for it in range(IT):
                                cs = slice(it * P, (it + 1) * P)
                                ins = pe.matmul(psY[it][:, 0:D], hl[:, f % R, cs], w2h[:, p, f, :], start=False,
                                                stop=(f == FT - 1))
                            ins.then_inc(s_y, 1)

                        for f in range(FT):
                            hidden(f)
                            if f >= 1:
                                output(f - 1)
                        output(FT - 1)

        @block.vector
        def _(v):
            v.sem_inc(s_wl, 1)
            v.sem_inc(s_hL, FT)
            v.sem_inc(s_yF, 1)
            ch = Chain(v, s_st)
            v.wait_ge(s_const, 4 + E)
            v.wait_ge(s_small, 16 * NSMALL)
            for t in range(NT):
                ch.step(v.bn_stats(st[:, t, :], X[:, t, :]))
            ch.wait()
            for t in range(NT):
                ch.step(v.bn_aggr(mv[:, t, :], st[:, t, :]))
            ch.wait()
            v.sem_inc(s_mv, 1)
            v.wait_ge(s_wr, 1)
            v.scalar_tensor_tensor(wrl[:, :, :], wr[:, :, :], WS, wrh[:, :, :], ALU.mult,
                                   ALU.subtract).then_inc(s_wr, 1)
            v.wait_ge(s_rstd, 1)
            for t in range(NT):
                v.tensor_scalar(xn[:, t, :], X[:, t, :], mv[:, t, 0:1], rstd[:, t:t + 1], ALU.subtract,
                                ALU.mult).then_inc(s_nt, 1)
            for i in range(GI):
                k, q = i % KC, i // KC
                cs = slice(q * 512, q * 512 + 512)
                v.wait_ge(s_tH, i + 1)
                v.tensor_tensor(xtl[:, k, cs], psH[i % 4][:, :], xth[:, k, cs], ALU.subtract).then_inc(s_tL, 1)
            if layer:
                v.wait_ge(s_b1, 1)
                ch.step(v.tensor_copy(b1[:, :, :].rearrange("p e f -> p (e f)"), psY[1][:, 0:E * FT]))

            def wide(t):
                return t[:, :].unsqueeze(2).broadcast_to([P, NT, E])

            def along(t):
                return t[:, :].unsqueeze(1).broadcast_to([P, NT, E])

            def op(ins):
                ch.step(ins)
                ch.wait()

            def first_max(src, mval, onehot):
                op(v.tensor_reduce(mval[:, :], src, AX.X, ALU.max))
                op(v.tensor_tensor(eq[:, :, :], src, wide(mval), ALU.is_ge))
                op(v.tensor_tensor(cand[:, :, :], eq[:, :, :], along(revi), ALU.mult))
                op(v.tensor_reduce(f1[:, :], cand[:, :, :], AX.X, ALU.max))
                op(v.tensor_tensor(onehot[:, :, :], along(revi), wide(f1), ALU.is_equal))

            v.wait_ge(s_lg, 1)
            plog = psY[0][:, 0:NT * E].rearrange("p (t e) -> p t e", e=E)
            op(v.tensor_scalar(lg[:, :, :], plog, 1.0 / WS, None, ALU.mult))
            if layer:
                op(v.tensor_tensor(lg[:, :, :], lg[:, :, :], along(brb), ALU.add))
            op(v.tensor_reduce(m1[:, :], lg[:, :, :], AX.X, ALU.max))
            v.tensor_tensor(sh[:, :, :], lg[:, :, :], wide(m1), ALU.subtract).then_inc(s_sh, 1)
            v.wait_ge(s_ex, 1)
            if not layer:
                op(v.tensor_reduce(sm[:, :], ex[:, :, :], AX.X, ALU.add))
                op(v.reciprocal(rs[:, :], sm[:, :]))
                op(v.tensor_tensor(sc[:, :, :], ex[:, :, :], wide(rs), ALU.mult))
                first_max(sc[:, :, :], m1, oh1)
                op(v.scalar_tensor_tensor(sc2[:, :, :], oh1[:, :, :], -2.0, sc[:, :, :], ALU.mult, ALU.add))
                first_max(sc2[:, :, :], m2, oh2)
                ch.step(v.tensor_tensor(cand[:, :, :], oh1[:, :, :], oh2[:, :, :], ALU.add))
                ch.wait()
                v.sem_inc(s_sel, 1)
                v.wait_ge(s_rk, 1)
                op(v.tensor_copy(tot[:, :, :], psY[3][:, 0:NT * E].rearrange("p (t e) -> p t e", e=E)))
                op(v.memset(off[:, 0, :], 0.0))
                for t in range(1, NT):
                    op(v.tensor_tensor(off[:, t, :], off[:, t - 1, :], tot[:, t - 1, :], ALU.add))
                op(v.tensor_tensor(rank[:, :, :], psY[2][:, 0:NT * E].rearrange("p (t e) -> p t e", e=E),
                                   off[:, :, :], ALU.add))
                op(v.tensor_scalar(valid[:, :, :], rank[:, :, :], float(CAP), None, ALU.is_lt))
                op(v.tensor_tensor(eq[:, :, :], cand[:, :, :], valid[:, :, :], ALU.mult))
                op(v.tensor_tensor(wgt[:, :, :], eq[:, :, :], sc[:, :, :], ALU.mult))
            else:
                first_max(lg[:, :, :], m2, oh1)
                op(v.scalar_tensor_tensor(sc2[:, :, :], oh1[:, :, :], -3.0e38, lg[:, :, :], ALU.mult, ALU.add))
                op(v.tensor_reduce(m2[:, :], sc2[:, :, :], AX.X, ALU.max))
                op(v.tensor_tensor(eq[:, :, :], lg[:, :, :], wide(m2), ALU.is_ge))
                op(v.tensor_tensor(sc[:, :, :], eq[:, :, :], ex[:, :, :], ALU.mult))
                op(v.tensor_reduce(sm[:, :], sc[:, :, :], AX.X, ALU.add))
                op(v.reciprocal(rs[:, :], sm[:, :]))
                op(v.tensor_tensor(wgt[:, :, :], sc[:, :, :], wide(rs), ALU.mult))
            op(v.tensor_scalar(wgs[:, :, :], wgt[:, :, :], 1.0 / WS, None, ALU.mult))
            v.sem_inc(s_wg, 1)
            nq = NT // 4 if layer else 0
            for q in range(nq):
                v.wait_ge(s_wtP, q + 1)
                v.tensor_copy(wt[:, 4 * q:4 * q + 4, :].rearrange("e t p -> e (t p)"),
                              psH[q][0:E, :]).then_inc(s_wtF, 1)
            for t in range(NT):
                v.wait_ge(s_wtP, nq + t + 1)
                v.tensor_tensor(X[:, t, :], X[:, t, :], psY[t % 4][:, 0:D], ALU.add).then_inc(s_wtF, 1)
            v.wait_ge(s_wtF, nq + NT)

            with v.Fori(0, E // 2) as gg:
                for p in range(2):
                    e = gg * 2 + p
                    v.wait_ge(s_wh, e + 2)
                    if layer:
                        v.tensor_copy(b1e[:, p, :], b1[:, bass.ds(e, 1), :].rearrange("p a f -> p (a f)"))
                    v.scalar_tensor_tensor(w1l[:, p, :, :], w1f[:, :, :], WS, w1h[:, p, :, :], ALU.mult, ALU.subtract)
                    v.scalar_tensor_tensor(w2l[:, p, :, :], w2f[:, :, :], WS, w2h[:, p, :, :], ALU.mult,
                                           ALU.subtract).then_inc(s_wl, 1)
                    with v.Fori(0, NCH) as c:
                        n = e * NCH + c
                        for f in range(FT):
                            v.wait_ge(s_hF, done(FT, n, f))
                            v.wait_ge(s_y, done(FT, n, f - R))
                            v.tensor_tensor(hl[:, f % R, :], hf[:, f % R, :], hh[:, f % R, :],
                                            ALU.subtract).then_inc(s_hL, 1)
                        v.wait_ge(s_y, done(FT, n, FT - 1))
                        v.wait_ge(s_yF, n + 1)
                        for it in range(IT):
                            t = c * IT + it
                            xs = X[:, bass.ds(t, 1), :].rearrange("p a c -> p (a c)")
                            ws_ = wgs[:, bass.ds(t, 1), :].rearrange("p a e -> p (a e)")[:, bass.ds(e, 1)]
                            ins = v.scalar_tensor_tensor(xs, psY[it][:, 0:D], ws_, xs, ALU.mult, ALU.add)
                        ins.then_inc(s_yF, 1)
            v.wait_ge(s_yF, E * NCH + 1)


def attention1(nc, X, identf, io):
    H, DH = 8, 32
    G = H * DH // P
    HG = H // G
    JT, JR = MT, MR
    KCH = chunks(M)
    NCK = len(KCH)
    NQ = KC * NT // 4 + G * B
    NGC = KC * -(-JT // 4)
    NW = NGC + G * NCK + JT
    NA = ST * NCK
    SCALE = DH ** -0.5
    KR = 3 * DH + 1
    VC = 2 * DH + 1
    R = 3
    NS = 3

    with ExitStack() as ctx:
        def sb(name, shape, dt=F32):
            return ctx.enter_context(nc.sbuf_tensor("c_" + name, shape, dt))

        def sem(name):
            return ctx.enter_context(nc.semaphore("c_" + name))

        wf = sb("wf", [P, 3, G, D])
        wth, wtl = sb("wth", [P, 3, KC, D], F16), sb("wtl", [P, 3, KC, D], F16)
        ltn = sb("ltn", [P, NT, D])
        st, mv = sb("st", [P, NT, 6]), sb("mv", [P, NT, 2])
        ve, mhalf, rstd = sb("ve", [P, NT]), sb("mhalf", [P, NT]), sb("rstd", [P, NT])
        lth, ltl = sb("lth", [P, KC, B * S], F16), sb("ltl", [P, KC, B * S], F16)
        qhs, qls = sb("qhs", [P, G, B * S], F16), sb("qls", [P, G, B * S], F16)
        qst = sb("qst", [P, H, B * S], F16)
        kst = sb("kst", [P, H, M], F16)
        khs, kls = sb("khs", [P, G, M], F16), sb("kls", [P, G, M], F16)
        vst = sb("vst", [P, JT, H, VC], F16)
        cx = sb("cx", [P, JT, D])
        cth, ctl = sb("cth", [P, KC, M], F16), sb("ctl", [P, KC, M], F16)
        mx, mc = sb("mx", [P, ST, NCK]), sb("mc", [P, ST])
        pf = sb("pf", [P, R, S])
        ph, pl = sb("ph", [P, R, S], F16), sb("pl", [P, R, S], F16)
        of = sb("of", [VC, S])
        fold = sb("fold", [VC, DH + 1])
        rl = sb("rl", [P, ST])

        psA = [ctx.enter_context(nc.psum_tensor(f"c_psA{i}", [P, 512], F32)) for i in range(2)]
        psS = [ctx.enter_context(nc.psum_tensor(f"c_psS{i}", [P, 512], F32)) for i in range(NS)]
        psO = ctx.enter_context(nc.psum_tensor("c_psO", [P, 512], F32))
        psM = ctx.enter_context(nc.psum_tensor("c_psM", [P, 512], F32))
        psT = ctx.enter_context(nc.psum_tensor("c_psT", [P, 512], F32))
        ring4 = psA + psS[0:2]

        s_const = sem("const")
        s_w = sem("w")
        s_cx = sem("cx")
        s_st = sem("st")
        s_mv = sem("mv")
        s_pool = sem("pool")
        s_rstd = sem("rstd")
        s_nt = sem("nt")
        s_uP = sem("uP")
        s_uH = sem("uH")
        s_uL = sem("uL")
        s_q = sem("q")
        s_wP = sem("wP")
        s_wH = sem("wH")
        s_wL = sem("wL")
        s_k = sem("k")
        s_aP = sem("aP")
        s_aF = sem("aF")
        s_mc = sem("mc")
        s_mT = sem("mT")
        s_mr = sem("mr")
        s_sP = sem("sP")
        s_pF = sem("pF")
        s_pH = sem("pH")
        s_pL = sem("pL")
        s_pv = sem("pv")
        s_oF = sem("oF")
        s_tP = sem("tP")
        s_rl = sem("rl")
        s_tF = sem("tF")

        block = ctx.enter_context(nc.Block(no_gpsimd_drain=True))
        NCONST = 6
        names = ("L1_xattn_Wq", "L1_xattn_Wk", "L1_xattn_Wv")

        def ring_prev(j):
            if j >= R:
                return 0, j - R
            return -1, max(q for q in range(JT) if q % R == j)

        SLOTS = [[] for _ in range(JT)]
        for a in range(NA):
            SLOTS[a // 2].append(a)
        SLOTS[8].append("mc")
        SLOTS[9].append("mT")

        @block.sync
        def _(sp):
            for i, name in enumerate(names):
                sp.dma_start(wf[:, i, :, :], io[name].rearrange("(g p) c -> p g c", p=P)).then_inc(s_w, 16)
            sp.wait_ge(s_uL, 3 + NQ)
            for h in range(H):
                r0 = (h % HG) * DH
                for piece, src in enumerate((qhs, qhs, qls)):
                    sp.dma_start(qst[piece * DH:(piece + 1) * DH, h, :], src[r0:r0 + DH, h // HG, :]).then_inc(s_q, 16)
            with sp.Fori(0, B) as b:
                sp.wait_ge(s_wP, b * NW + NGC)
                src = io["ctx_1024"][bass.ds(b, 1), :, :].rearrange("a m c -> (a m) c")
                sp.dma_start(cx[:, 0:MT - 1, :],
                             src[0:(MT - 1) * P, :].rearrange("(t p) c -> p t c", p=P)).then_inc(s_cx, 16)
                sp.dma_start(cx[0:MR, MT - 1, :], src[(MT - 1) * P:M, :]).then_inc(s_cx, 16)
                for g in range(G):
                    sp.wait_ge(s_wL, done(NW, b, NGC + (g + 1) * NCK - 1))
                    for u in range(HG):
                        for piece, src_ in enumerate((khs, kls, khs)):
                            sp.dma_start(kst[piece * DH:(piece + 1) * DH, g * HG + u, :],
                                         src_[u * DH:(u + 1) * DH, g, :]).then_inc(s_k, 16)

        @block.gpsimd
        def _(g):
            for i, (t, val) in enumerate(((mhalf[:, :], -0.5), (kst[3 * DH:KR, :, :], 1.0),
                                          (vst[:, :, :, 2 * DH:VC], WS), (fold[:, :], 0.0),
                                          (fold[2 * DH:VC, DH:DH + 1], 1.0))):
                g.memset(t, val).then_inc(s_const, 1)
                g.wait_ge(s_const, i + 1)
            g.affine_select(out=fold[0:2 * DH, 0:DH], in_=fold[0:2 * DH, 0:DH], compare_op=ALU.not_equal, fill=1.0,
                            base=0, pattern=[[-1, DH]], channel_multiplier=1).then_inc(s_pool, 1)
            g.wait_ge(s_pool, 1)
            g.affine_select(out=fold[0:2 * DH, 0:DH], in_=fold[0:2 * DH, 0:DH], compare_op=ALU.not_equal, fill=1.0,
                            base=-DH, pattern=[[-1, DH]], channel_multiplier=1).then_inc(s_pool, 1)
            g.wait_ge(s_pool, 2)
            g.sem_inc(s_const, 1)
            g.wait_ge(s_mv, 1)
            g.tensor_scalar(ve[:, :], mv[:, :, 1], EPS, None, ALU.add).then_inc(s_pool, 1)
            g.wait_ge(s_pool, 3)
            g.tensor_tensor(rstd[:, :], ve[:, :], mhalf[:, :], ALU.pow).then_inc(s_rstd, 1)

        @block.scalar
        def _(act):
            act.sem_inc(s_wH, NW)
            act.sem_inc(s_pF, JT)
            act.sem_inc(s_pH, JT)
            act.sem_inc(s_oF, 1)
            for i in range(3 + NQ):
                act.wait_ge(s_uP, i + 1)
                ps = ring4[i % 4]
                if i < 3:
                    act.activation(wth[:, i, :, :].rearrange("p k n -> p (k n)"), ps[:, :], ACT.Copy,
                                   scale=WS).then_inc(s_uH, 1)
                elif i < 3 + KC * NT // 4:
                    k, q = (i - 3) % KC, (i - 3) // KC
                    act.activation(lth[:, k, q * 512:q * 512 + 512], ps[:, :], ACT.Copy).then_inc(s_uH, 1)
                else:
                    u = i - 3 - KC * NT // 4
                    g, b = u % G, u // G
                    act.activation(qhs[:, g, b * S:(b + 1) * S], ps[:, :], ACT.Copy, scale=1.0 / WS).then_inc(s_uH, 1)
            with act.Fori(0, B) as b:
                for i in range(NW):
                    act.wait_ge(s_wP, done(NW, b, i))
                    ps = ring4[i % 4]
                    if i < NGC:
                        k, q = i % KC, i // KC
                        n = min(512, M - q * 512)
                        act.activation(cth[:, k, q * 512:q * 512 + n], ps[:, 0:n], ACT.Copy).then_inc(s_wH, 1)
                    elif i < NGC + G * NCK:
                        g, c = divmod(i - NGC, NCK)
                        c0, cn = KCH[c]
                        act.activation(khs[:, g, c0:c0 + cn], ps[:, 0:cn], ACT.Copy, scale=1.0 / WS).then_inc(s_wH, 1)
                    else:
                        j = i - NGC - G * NCK
                        r = rows(j, JT, JR)
                        act.activation(vst[0:r, j, :, 0:DH], ps[0:r, 0:D].rearrange("p (h d) -> p h d", d=DH),
                                       ACT.Copy).then_inc(s_wH, 1)

                def out_copy(n):
                    act.wait_ge(s_pv, done(JT, n, JT - 1))
                    act.wait_ge(s_tP, done(1, n, 0) - 1)
                    act.activation(of[:, :], psO[0:VC, :], ACT.Copy).then_inc(s_oF, 1)

                def main(h, with_tail):
                    n = b * H + h
                    if with_tail:
                        out_copy(n - 1)
                    for j in range(JT):
                        r = rows(j, JT, JR)
                        dn, pj = ring_prev(j)
                        act.wait_ge(s_sP, done(JT, n, j))
                        act.wait_ge(s_pL, done(JT, n + dn, pj))
                        act.activation(pf[0:r, j % R, :], psS[j % NS][0:r, :], ACT.Exp, scale=SCALE).then_inc(s_pF, 1)
                        act.wait_ge(s_pv, done(JT, n + dn, pj))
                        act.activation(ph[0:r, j % R, :], psS[j % NS][0:r, :], ACT.Exp, scale=SCALE).then_inc(s_pH, 1)

                main(b * 0, False)
                with act.Fori(1, H) as h:
                    main(h, True)
                out_copy(b * H + (H - 1))

        @block.tensor
        def _(pe):
            pe.sem_inc(s_wP, NW)
            pe.sem_inc(s_aP, NA)
            pe.sem_inc(s_mT, 1)
            pe.sem_inc(s_sP, JT)
            pe.sem_inc(s_pv, JT)
            pe.sem_inc(s_tP, 1)

            def triple(out, hi, lo, xh_, xl_, first=True, last=True):
                pe.matmul(out, hi, xh_, start=first, stop=False)
                pe.matmul(out, hi, xl_, start=False, stop=False)
                return pe.matmul(out, lo, xh_, start=False, stop=last)

            pe.wait_ge(s_w, 48)
            pe.wait_ge(s_const, NCONST)
            for i in range(3 + NQ):
                ps = ring4[i % 4]
                if i >= 4:
                    pe.wait_ge(s_uL, i - 3)
                if i < 3:
                    for k in range(KC):
                        for g in range(G):
                            o = (k * G + g) * P
                            ins = pe.transpose(ps[:, o:o + P], wf[:, i, g, k * P:(k + 1) * P], identf[:, :])
                elif i < 3 + KC * NT // 4:
                    k, q = (i - 3) % KC, (i - 3) // KC
                    pe.wait_ge(s_nt, 4 * q + 4)
                    for u in range(4):
                        ins = pe.transpose(ps[:, u * P:(u + 1) * P], ltn[:, 4 * q + u, k * P:(k + 1) * P],
                                           identf[:, :])
                else:
                    u = i - 3 - KC * NT // 4
                    g, b = u % G, u // G
                    if u == 0:
                        pe.wait_ge(s_uL, 3 + KC * NT // 4)
                    ts = slice(b * S, (b + 1) * S)
                    for k in range(KC):
                        ws = slice(g * P, (g + 1) * P)
                        ins = triple(ps[:, :], wth[:, 0, k, ws], wtl[:, 0, k, ws], lth[:, k, ts], ltl[:, k, ts],
                                     k == 0, k == KC - 1)
                ins.then_inc(s_uP, 1)
            pe.wait_ge(s_uL, 3 + NQ)
            pe.wait_ge(s_q, 3 * H * 16)

            with pe.Fori(0, B) as b:
                for i in range(NW):
                    ps = ring4[i % 4]
                    if i < 4:
                        if i == 0:
                            pe.wait_ge(s_aF, (b * H) * NA + NA)
                            pe.wait_ge(s_pH, (b * H) * JT + JT)
                            pe.wait_ge(s_cx, b * 32 + 32)
                    else:
                        pe.wait_ge(s_wL, done(NW, b, NGC - 1 if i == NGC else i - 4))
                    if i < NGC:
                        k, q = i % KC, i // KC
                        for u in range(4):
                            tl = q * 4 + u
                            if tl >= JT:
                                break
                            r = rows(tl, JT, JR)
                            ins = pe.transpose(ps[:, u * P:u * P + r], cx[0:r, tl, k * P:(k + 1) * P],
                                               identf[0:r, 0:r])
                    elif i < NGC + G * NCK:
                        g, c = divmod(i - NGC, NCK)
                        c0, cn = KCH[c]
                        for k in range(KC):
                            ws = slice(g * P, (g + 1) * P)
                            ins = triple(ps[:, 0:cn], wth[:, 1, k, ws], wtl[:, 1, k, ws], cth[:, k, c0:c0 + cn],
                                         ctl[:, k, c0:c0 + cn], k == 0, k == KC - 1)
                    else:
                        j = i - NGC - G * NCK
                        r = rows(j, JT, JR)
                        js = slice(j * P, j * P + r)
                        for k in range(KC):
                            ins = triple(ps[0:r, 0:D], cth[:, k, js], ctl[:, k, js], wth[:, 2, k, :], wtl[:, 2, k, :],
                                         k == 0, k == KC - 1)
                    ins.then_inc(s_wP, 1)

                def head(t, h, cs, r=P):
                    return t[0:r, bass.ds(h, 1), cs].rearrange("p a n -> p (a n)")

                def pre(n, h, what):
                    if what == "mc":
                        return
                    if what == "mT":
                        pe.wait_ge(s_mc, done(1, n, 0))
                        pe.wait_ge(s_mr, done(1, n, 0) - 1)
                        for it in range(ST):
                            ins = pe.transpose(psM[0:1, it * P:(it + 1) * P], mc[:, it:it + 1], identf[:, :])
                        ins.then_inc(s_mT, 1)
                        return
                    a = what
                    it, c = divmod(a, NCK)
                    c0, cn = KCH[c]
                    pe.wait_ge(s_aF, done(NA, n, a - 2))
                    pe.matmul(psA[a % 2][:, 0:cn], head(qst, h, bass.ds(b * S + it * P, P), KR - 1),
                              head(kst, h, slice(c0, c0 + cn), KR - 1), start=True, stop=True).then_inc(s_aP, 1)

                def pv(n, h, j):
                    r = rows(j, JT, JR)
                    w = vst[0:r, j, bass.ds(h, 1), :].rearrange("p a n -> p (a n)")
                    pe.wait_ge(s_pH, done(JT, n, j))
                    if j == 0:
                        pe.wait_ge(s_oF, done(1, n, 0) - 1)
                    pe.matmul(psO[0:VC, :], w, ph[0:r, j % R, :], start=(j == 0), stop=False)
                    pe.wait_ge(s_pL, done(JT, n, j))
                    pe.matmul(psO[0:VC, :], w, pl[0:r, j % R, :], start=False, stop=(j == JT - 1)).then_inc(s_pv, 1)

                def tail(n):
                    pe.wait_ge(s_oF, done(1, n, 0))
                    pe.wait_ge(s_tF, done(1, n, 0) - 1)
                    for it in range(ST):
                        ins = pe.matmul(psT[:, it * (DH + 1):(it + 1) * (DH + 1)], of[:, it * P:(it + 1) * P],
                                        fold[:, :], start=True, stop=True)
                    ins.then_inc(s_tP, 1)

                def main(h, with_pre, with_tail):
                    n = b * H + h
                    for j in range(JT):
                        r = rows(j, JT, JR)
                        pj = j - NS if j >= NS else max(q for q in range(JT) if q % NS == j) - JT
                        pe.wait_ge(s_pH, done(JT, n, pj))
                        if j == 0:
                            pe.wait_ge(s_mr, done(1, n, 0))
                        pe.matmul(psS[j % NS][0:r, :], head(kst, h, slice(j * P, j * P + r), KR),
                                  head(qst, h, bass.ds(b * S, S), KR), start=True, stop=True).then_inc(s_sP, 1)
                        if with_pre:
                            for what in SLOTS[j]:
                                pre(n + 1, h + 1, what)
                        if j >= 1:
                            pv(n, h, j - 1)
                        if with_tail and j == 1:
                            tail(n - 1)
                    pv(n, h, JT - 1)

                pe.wait_ge(s_wL, done(NW, b, NW - 1))
                pe.wait_ge(s_k, (b + 1) * (3 * H * 16))
                for what in sum(SLOTS, []):
                    pre(b * H, b * 0, what)
                main(b * 0, True, False)
                with pe.Fori(1, H - 1) as h:
                    main(h, True, True)
                main(b * 0 + (H - 1), False, True)
                tail(b * H + (H - 1))

        @block.vector
        def _(v):
            v.sem_inc(s_wL, NW)
            v.sem_inc(s_aF, NA)
            v.sem_inc(s_mc, 1)
            v.sem_inc(s_mr, 1)
            v.sem_inc(s_pL, JT)
            v.sem_inc(s_rl, 1)
            v.sem_inc(s_tF, 1)
            ch = Chain(v, s_st)
            v.wait_ge(s_const, NCONST)
            for t in range(NT):
                ch.step(v.bn_stats(st[:, t, :], X[:, t, :]))
            ch.wait()
            for t in range(NT):
                ch.step(v.bn_aggr(mv[:, t, :], st[:, t, :]))
            ch.wait()
            v.sem_inc(s_mv, 1)
            v.wait_ge(s_rstd, 1)
            for t in range(NT):
                v.tensor_scalar(ltn[:, t, :], X[:, t, :], mv[:, t, 0:1], rstd[:, t:t + 1], ALU.subtract,
                                ALU.mult).then_inc(s_nt, 1)
            for i in range(3 + NQ):
                ps = ring4[i % 4]
                v.wait_ge(s_uH, i + 1)
                if i < 3:
                    v.scalar_tensor_tensor(wtl[:, i, :, :].rearrange("p k n -> p (k n)"), ps[:, :], WS,
                                           wth[:, i, :, :].rearrange("p k n -> p (k n)"), ALU.mult,
                                           ALU.subtract).then_inc(s_uL, 1)
                elif i < 3 + KC * NT // 4:
                    k, q = (i - 3) % KC, (i - 3) // KC
                    cs = slice(q * 512, q * 512 + 512)
                    v.tensor_tensor(ltl[:, k, cs], ps[:, :], lth[:, k, cs], ALU.subtract).then_inc(s_uL, 1)
                else:
                    u = i - 3 - KC * NT // 4
                    g, b = u % G, u // G
                    cs = slice(b * S, (b + 1) * S)
                    v.scalar_tensor_tensor(qls[:, g, cs], ps[:, :], 1.0 / WS, qhs[:, g, cs], ALU.mult,
                                           ALU.subtract).then_inc(s_uL, 1)
            with v.Fori(0, B) as b:
                for i in range(NW):
                    v.wait_ge(s_wH, done(NW, b, i))
                    ps = ring4[i % 4]
                    if i < NGC:
                        k, q = i % KC, i // KC
                        n = min(512, M - q * 512)
                        cs = slice(q * 512, q * 512 + n)
                        v.tensor_tensor(ctl[:, k, cs], ps[:, 0:n], cth[:, k, cs], ALU.subtract).then_inc(s_wL, 1)
                    elif i < NGC + G * NCK:
                        g, c = divmod(i - NGC, NCK)
                        c0, cn = KCH[c]
                        v.scalar_tensor_tensor(kls[:, g, c0:c0 + cn], ps[:, 0:cn], 1.0 / WS, khs[:, g, c0:c0 + cn],
                                               ALU.mult, ALU.subtract).then_inc(s_wL, 1)
                    else:
                        j = i - NGC - G * NCK
                        r = rows(j, JT, JR)
                        v.tensor_tensor(vst[0:r, j, :, DH:2 * DH], ps[0:r, 0:D].rearrange("p (h d) -> p h d", d=DH),
                                        vst[0:r, j, :, 0:DH], ALU.subtract).then_inc(s_wL, 1)

                def pre(n, h, what):
                    if what == "mc":
                        v.wait_ge(s_aF, done(NA, n, NA - 1))
                        v.tensor_reduce(mc[:, :], mx[:, :, :], AX.X, ALU.max).then_inc(s_mc, 1)
                        return
                    if what == "mT":
                        v.wait_ge(s_mT, done(1, n, 0))
                        v.tensor_scalar(qst[KR - 1:KR, bass.ds(h, 1), bass.ds(b * S, S)].rearrange("p a n -> p (a n)"),
                                        psM[0:1, :], -1.0, None, ALU.mult).then_inc(s_mr, 1)
                        return
                    it, c = divmod(what, NCK)
                    c0, cn = KCH[c]
                    v.wait_ge(s_aP, done(NA, n, what))
                    v.tensor_reduce(mx[:, it, c:c + 1], psA[what % 2][:, 0:cn], AX.X, ALU.max).then_inc(s_aF, 1)

                def tail(n, h):
                    v.wait_ge(s_tP, done(1, n, 0))
                    pt = psT[:, 0:ST * (DH + 1)].rearrange("p (t n) -> p t n", n=DH + 1)
                    v.reciprocal(rl[:, :], pt[:, :, DH]).then_inc(s_rl, 1)
                    v.wait_ge(s_rl, done(1, n, 0))
                    for it in range(ST):
                        xs = X[:, bass.ds(b * ST + it, 1), bass.ds(h * DH, DH)].rearrange("p a c -> p (a c)")
                        ins = v.scalar_tensor_tensor(xs, pt[:, it, 0:DH], rl[:, it:it + 1], xs, ALU.mult, ALU.add)
                    ins.then_inc(s_tF, 1)

                def main(h, with_pre, with_tail):
                    n = b * H + h
                    for j in range(JT):
                        r = rows(j, JT, JR)
                        dn, pj = ring_prev(j)
                        v.wait_ge(s_pH, done(JT, n, j))
                        v.wait_ge(s_pv, done(JT, n + dn, pj))
                        v.tensor_tensor(pl[0:r, j % R, :], pf[0:r, j % R, :], ph[0:r, j % R, :],
                                        ALU.subtract).then_inc(s_pL, 1)
                        if with_pre:
                            for what in SLOTS[j]:
                                pre(n + 1, h + 1, what)
                        if with_tail and j == 2:
                            tail(n - 1, h - 1)

                for what in sum(SLOTS, []):
                    pre(b * H, b * 0, what)
                main(b * 0, True, False)
                with v.Fori(1, H - 1) as h:
                    main(h, True, True)
                main(b * 0 + (H - 1), False, True)
                tail(b * H + (H - 1), b * 0 + (H - 1))
            v.wait_ge(s_tF, B * H + 1)


def build(nc, io, out, phases):
    with ExitStack() as ctx:
        X = ctx.enter_context(nc.sbuf_tensor("X", [P, NT, D], F32))
        identf = ctx.enter_context(nc.sbuf_tensor("identf", [P, P], F32))
        s_id = ctx.enter_context(nc.semaphore("s_id"))
        s_out = ctx.enter_context(nc.semaphore("s_out"))
        with nc.Block(no_gpsimd_drain=True) as block:
            @block.gpsimd
            def _(g):
                g.memset(identf[:, :], 0.0).then_inc(s_id, 1)
                g.wait_ge(s_id, 1)
                g.affine_select(out=identf[:, :], in_=identf[:, :], compare_op=ALU.not_equal, fill=1.0, base=0,
                                pattern=[[-1, P]], channel_multiplier=1).then_inc(s_id, 1)
                g.wait_ge(s_id, 2)
        if "A" in phases:
            attention0(nc, X, identf, io)
        if "B" in phases:
            experts(nc, X, identf, io, 0)
        if "C" in phases:
            attention1(nc, X, identf, io)
        if "D" in phases:
            experts(nc, X, identf, io, 1)
        with nc.Block(no_gpsimd_drain=True) as block:
            @block.sync
            def _(sp):
                sp.dma_start(out.rearrange("b (t p) c -> p (b t) c", p=P), X[:, :, :]).then_inc(s_out, 16)
                sp.wait_ge(s_out, 16)


PHASES = "ABCD"
_INS = ['x', 'ctx_1024', 'L0_xattn_gamma_media', 'L0_xattn_beta_media', 'L0_xattn_gamma_lat', 'L0_xattn_beta_lat',
        'L0_xattn_Wq', 'L0_xattn_bq', 'L0_xattn_Wkv', 'L0_xattn_bkv', 'L0_xattn_Wo', 'L0_xattn_bo',
        'L0_ffn_w_router', 'L0_ffn_w1', 'L0_ffn_w2', 'L0_ffn_bias', 'L1_xattn_Wq', 'L1_xattn_Wk', 'L1_xattn_Wv',
        'L1_ffn_W1', 'L1_ffn_b1', 'L1_ffn_W2', 'L1_ffn_b2', 'L1_ffn_Wr', 'L1_ffn_br']


def kernel(**inputs):
    import numpy as np
    import concourse.bacc as bacc
    from concourse.bass_utils import run_bass_kernel_spmd

    nc = bacc.Bacc("TRN2", target_bir_lowering=False, num_devices=1)
    arrays, io = {}, {}
    for name in _INS:
        a = np.ascontiguousarray(inputs[name])
        arrays[f"in_{name}"] = a
        io[name] = nc.dram_tensor(f"in_{name}", a.shape, F32, kind="ExternalInput").ap()
    out = nc.dram_tensor("out_0", (B, S, D), F32, kind="ExternalOutput").ap()
    build(nc, io, out, PHASES)
    r = run_bass_kernel_spmd(nc, [arrays], core_ids=[0])
    return r.results[0]["out_0"]
```

```python
from contextlib import ExitStack

import concourse.bass as bass
from concourse import mybir

F32 = mybir.dt.float32
F16 = mybir.dt.float16
BF16 = mybir.dt.bfloat16
ALU = mybir.AluOpType
ACT = mybir.ActivationFunctionType
AX = mybir.AxisListType

P = 128
B, S, D = 4, 512, 256
M = 1601
KC = D // P
NT = B * S // P
ST = S // P
MT = -(-M // P)
MR = M - (MT - 1) * P
WS = 16.0
EPS = 1e-5

H0, DH0 = 8, 128
J0 = S + M
JT0 = -(-J0 // P)
JR0 = J0 - (JT0 - 1) * P
INNER = H0 * DH0


def done(per, n, k):
    return (n + 1) * per + k + 1


def rows(j, tiles, last):
    return last if j == tiles - 1 else P


class Chain:

    def __init__(self, eng, sem, base=0, ):
        self.eng, self.sem, self.count, self.base = eng, sem, 0, base

    def step(self, ins):
        ins.then_inc(self.sem, 1)
        self.count += 1

    def wait(self):
        self.eng.wait_ge(self.sem, self.base + self.count)


def chunks(total, size=512):
    return [(o, min(size, total - o)) for o in range(0, total, size)]


def ring(tiles, size):
    out = [j % size for j in range(tiles)]
    if tiles % size == 1:
        out[-1] = size - 2
    return out


def before(slots, j):
    same = [q for q in range(j) if slots[q] == slots[j]]
    return (0, same[-1]) if same else (-1, max(q for q in range(len(slots)) if slots[q] == slots[j]))


def attention0(nc, X, identf, io):
    KCH = chunks(J0)
    NA = 1 + len(KCH) + ST * len(KCH)
    NG = KC * -(-JT0 // 4)
    NV = JT0 * INNER // 512
    NW = NG + NV
    SCALE = DH0 ** -0.5 / (WS * WS)
    LAG = 2
    PR = ring(JT0, 5)
    SR = ring(JT0, 3)
    R, NS = max(PR) + 1, max(SR) + 1
    TAIL = [LAG + 1, LAG + 2, LAG + 4]

    with ExitStack() as ctx:
        def sb(name, shape, dt):
            return ctx.enter_context(nc.sbuf_tensor("a_" + name, shape, dt))

        def pb(name, shape, dt=F32):
            return ctx.enter_context(nc.psum_tensor("a_" + name, shape, dt))

        used = []

        def sem(name):
            used.append(ctx.enter_context(nc.semaphore("a_" + name)))
            return used[-1]

        wqh, wql = sb("wqh", [P, KC, INNER], F16), sb("wql", [P, KC, INNER], F16)
        wkvh, wkvl = sb("wkvh", [P, KC, 2 * INNER], F16), sb("wkvl", [P, KC, 2 * INNER], F16)
        woh, wol = sb("woh", [P, H0, D], F16), sb("wol", [P, H0, D], F16)
        vh, vl = sb("vh", [P, JT0, INNER], F16), sb("vl", [P, JT0, INNER], F16)
        stage_a = vh[:, 0:16, :].rearrange("p a b -> p (a b)").bitcast(F32)
        stage_b = vl[:, 0:16, :].rearrange("p a b -> p (a b)").bitcast(F32)
        wq_f = stage_a[:, 0:2048].rearrange("p (k n) -> p k n", k=KC)
        wkv_f = stage_a[:, 2048:6144].rearrange("p (k n) -> p k n", k=KC)
        wo_f = stage_b[:, 0:2048].rearrange("p (h n) -> p h n", h=H0)
        xth, xtl = sb("xth", [P, KC, J0], F16), sb("xtl", [P, KC, J0], F16)
        cx = sb("cx", [P, MT, D], F32)
        lat = sb("lat", [P, ST, D], F32)
        st = sb("st", [P, MT + ST, 6], F32)
        mv = sb("mv", [P, MT + ST, 2], F32)
        mhalf = sb("mhalf", [P, MT + ST], F32)
        rstd = sb("rstd", [P, MT + ST], F32)
        ve = sb("ve", [P, MT + ST], F32)
        tmp = sb("tmp", [P, 512], F32)
        gm, bm, gl, bl = (sb(n, [P, KC], F32) for n in ("gm", "bm", "gl", "bl"))
        bq, bkv = sb("bq", [P, H0], F32), sb("bkv", [P, 2 * H0], F32)
        bo = sb("bo", [1, D], F32)
        qh, ql = sb("qh", [P, 2, S], F16), sb("ql", [P, 2, S], F16)
        kh, kl = sb("kh", [P, 2, J0], F16), sb("kl", [P, 2, J0], F16)
        mx = sb("mx", [P, 2, ST, len(KCH)], F32)
        mc = sb("mc", [P, 2, ST], F32)
        mrow = sb("mrow", [1, 2, S], BF16)
        oneb = sb("oneb", [1, P], BF16)
        onef = sb("onef", [P, P], F32)
        four = sb("four", [P, 1], F32)
        pf = sb("pf", [P, R, S], F32)
        ph, pl = sb("ph", [P, R, S], F16), sb("pl", [P, R, S], F16)
        acc = sb("acc", [P, 2, S], F32)
        oh, ol = sb("oh", [P, S], F16), sb("ol", [P, S], F16)
        rl = sb("rl", [P, 2, ST], F32)
        brow = sb("brow", [1, D], F32)
        bb = sb("bb", [P, D], F32)

        psA = [pb(f"psA{i}", [P, 512]) for i in range(2)]
        psS = [pb(f"psS{i}", [P, 512]) for i in range(NS)]
        psO = pb("psO", [P, 512])
        psW = pb("psW", [P, 2, D])
        psM = pb("psM", [P, 512])
        ring4 = psA + psS[0:2]

        s_const = sem("const")
        s_small = sem("small")
        s_w = sem("w")
        s_wh = sem("wh")
        s_wl = sem("wl")
        s_b16 = sem("b16")
        s_br = sem("br")
        s_brow = sem("brow")
        s_cx = sem("cx")
        s_st = sem("st")
        s_mv = sem("mv")
        s_pool = sem("pool")
        s_rstd = sem("rstd")
        s_nt = sem("nt")
        s_wP = sem("wP")
        s_wH = sem("wH")
        s_wt = sem("wt")
        s_wL = sem("wL")
        s_aP = sem("aP")
        s_aH = sem("aH")
        s_aF = sem("aF")
        s_mc = sem("mc")
        s_mT = sem("mT")
        s_mrow = sem("mrow")
        s_sP = sem("sP")
        s_pF = sem("pF")
        s_pH = sem("pH")
        s_pL = sem("pL")
        s_pv = sem("pv")
        s_acc = sem("acc")
        s_oH = sem("oH")
        s_oL = sem("oL")
        s_lP = sem("lP")
        s_rl = sem("rl")
        s_yP = sem("yP")
        s_yF = sem("yF")
        s_fin = sem("fin")

        def clear():
            with nc.Block(no_gpsimd_drain=True) as last:
                @last.gpsimd
                def _(g):
                    for one in used:
                        g.sem_clear(one)

        ctx.callback(clear)
        block = ctx.enter_context(nc.Block(no_gpsimd_drain=True))

        @block.sync
        def _(sp):
            for name, t, k in (("L0_xattn_gamma_media", gm, KC), ("L0_xattn_beta_media", bm, KC),
                               ("L0_xattn_gamma_lat", gl, KC), ("L0_xattn_beta_lat", bl, KC),
                               ("L0_xattn_bq", bq, H0), ("L0_xattn_bkv", bkv, 2 * H0)):
                sp.dma_start(t[:, :], io[name].rearrange("(k p) -> p k", p=P),
                             allow_slow_non_contiguous=True).then_inc(s_small, 16)
            sp.dma_start(bo[:, :], io["L0_xattn_bo"].rearrange("(a n) -> a n", a=1)).then_inc(s_small, 16)
            with sp.Fori(0, B) as b:
                sp.wait_ge(s_wP, done(NW, b, -1) - NV)
                src = io["ctx_1024"][bass.ds(b, 1), :, :].rearrange("a m c -> (a m) c")
                sp.dma_start(cx[:, 0:MT - 1, :],
                             src[0:(MT - 1) * P, :].rearrange("(t p) c -> p t c", p=P)).then_inc(s_cx, 16)
                sp.dma_start(cx[0:MR, MT - 1, :], src[(MT - 1) * P:M, :]).then_inc(s_cx, 16)

        @block.gpsimd
        def _(g):
            for t, v in ((mhalf, -0.5), (onef, 1.0), (four, 4.0), (mv, 0.0), (oneb, 1.0)):
                g.memset(t[:], v).then_inc(s_const, 1)
            g.sem_inc(s_rstd, 3)
            g.sem_inc(s_acc, JT0)
            g.wait_ge(s_const, 5)
            sel = [(0, ST), (ST, ST + MT), (0, ST)]
            with g.Fori(0, B) as b:
                for r, (lo, hi) in enumerate(sel):
                    g.wait_ge(s_mv, b * 3 + r + 1)
                    g.nop(nofuse=True)
                    g.tensor_scalar(ve[:, lo:hi], mv[:, lo:hi, 1], EPS, None, ALU.add).then_inc(s_pool, 1)
                    g.wait_ge(s_pool, b * 3 + r + 1)
                    g.tensor_tensor(rstd[:, lo:hi], ve[:, lo:hi], mhalf[:, lo:hi], ALU.pow).then_inc(s_rstd, 1)

                def sums(h, p):
                    n = b * H0 + h
                    for j in range(JT0):
                        k = rows(j, JT0, JR0)
                        g.wait_ge(s_pF, done(JT0, n, j))
                        if j == 0:
                            g.wait_ge(s_lP, done(1, n, 0) - 2)
                            g.nop(nofuse=True)
                            g.tensor_copy(acc[:, p, :], pf[:, PR[0], :]).then_inc(s_acc, 1)
                        else:
                            g.wait_ge(s_acc, done(JT0, n, j - 1))
                            g.tensor_tensor(acc[0:k, p, :], acc[0:k, p, :], pf[0:k, PR[j], :],
                                            ALU.add).then_inc(s_acc, 1)

                sums(0, 0)
                with g.Fori(0, 3) as t:
                    sums(t * 2 + 1, 1)
                    sums(t * 2 + 2, 0)
                sums(H0 - 1, 1)

        def pre_slots():
            out = [[] for _ in range(JT0)]
            out[0] = ["A0", "A1"]
            out[1] = ["A2", "A3"]
            out[2] = ["A4", "A5"]
            for i in range(ST * len(KCH)):
                out[3 + i // 2].append(f"A{1 + len(KCH) + i}")
            out[13].append("mc")
            out[14].append("mT")
            return out

        SLOTS = pre_slots()

        @block.scalar
        def _(act):
            act.dma_start(wkv_f, io["L0_xattn_Wkv"].rearrange("(k p) n -> p k n", p=P)).then_inc(s_w, 16)
            act.dma_start(wq_f, io["L0_xattn_Wq"].rearrange("(k p) n -> p k n", p=P)).then_inc(s_w, 16)
            act.dma_start(wo_f, io["L0_xattn_Wo"].rearrange("(h p) n -> p h n", p=P)).then_inc(s_w, 16)
            act.sem_inc(s_wH, NW)
            act.sem_inc(s_aH, 1 + len(KCH))
            act.sem_inc(s_pF, JT0)
            act.sem_inc(s_pH, JT0)
            act.sem_inc(s_oH, 1)
            act.wait_ge(s_w, 48)
            act.wait_ge(s_small, 16 * 7)
            for hi, f in ((wkvh, wkv_f), (wqh, wq_f), (woh, wo_f)):
                act.activation(hi[:, :, :], f, ACT.Copy, scale=WS).then_inc(s_wh, 1)
            with act.Fori(0, B) as b:
                for i in range(NW):
                    act.wait_ge(s_wP, done(NW, b, i))
                    ps = ring4[i % 4]
                    if i < NG:
                        k, gidx = i % KC, i // KC
                        c0 = gidx * 512
                        n = min(512, J0 - c0)
                        gg, be = (gl, bl) if gidx == 0 else (gm, bm)
                        act.activation(xth[:, k, c0:c0 + n], ps[:, 0:n], ACT.Identity,
                                       bias=be[:, k:k + 1], scale=gg[:, k:k + 1]).then_inc(s_wH, 1)
                    else:
                        j, half = (i - NG) // 2, (i - NG) % 2
                        r = rows(j, JT0, JR0)
                        act.activation(vh[0:r, j, half * 512:half * 512 + 512], ps[0:r, :],
                                       ACT.Copy).then_inc(s_wH, 1)

                def pre(n, h, p, what):
                    if what[0] != "A":
                        return
                    a = int(what[1:])
                    if a > len(KCH):
                        return
                    act.wait_ge(s_aP, done(NA, n, a))
                    act.nop(nofuse=True)
                    if a == 0:
                        act.activation(qh[:, p, :], psA[0][:, :], ACT.Identity,
                                       bias=bq[:, bass.ds(h, 1)]).then_inc(s_aH, 1)
                    else:
                        c0, cn = KCH[a - 1]
                        act.activation(kh[:, p, c0:c0 + cn], psA[a % 2][:, 0:cn], ACT.Identity,
                                       bias=bkv[:, bass.ds(h, 1)]).then_inc(s_aH, 1)

                def out_hi(n):
                    act.wait_ge(s_pv, done(JT0, n, JT0 - 1))
                    act.wait_ge(s_yP, done(2, n, 1) - 2)
                    act.activation(oh[:, :], psO[:, :], ACT.Copy, scale=1.0 / 64).then_inc(s_oH, 1)

                def main(h, p, with_pre, with_tail):
                    n = b * H0 + h
                    for j in range(JT0):
                        r = rows(j, JT0, JR0)
                        dn, pj = before(PR, j)
                        if with_tail and j == LAG:
                            out_hi(n - 1)
                        act.wait_ge(s_sP, done(JT0, n, j))
                        act.wait_ge(s_pL, done(JT0, n + dn, pj))
                        act.wait_ge(s_acc, done(JT0, n + dn, pj))
                        act.activation(pf[0:r, PR[j], :], psS[SR[j]][0:r, :], ACT.Exp,
                                       scale=SCALE).then_inc(s_pF, 1)
                        act.wait_ge(s_pv, done(JT0, n + dn, pj))
                        act.activation(ph[0:r, PR[j], :], psS[SR[j]][0:r, :], ACT.Exp,
                                       scale=SCALE).then_inc(s_pH, 1)
                        if with_pre:
                            for what in SLOTS[j]:
                                pre(n + 1, h + 1, 1 - p, what)

                for what in sum(SLOTS, []):
                    pre(b * H0, b * 0, 0, what)
                main(b * 0, 0, True, False)
                with act.Fori(0, 3) as t:
                    main(t * 2 + 1, 1, True, True)
                    main(t * 2 + 2, 0, True, True)
                main(b * 0 + (H0 - 1), 1, False, True)
                out_hi(b * H0 + (H0 - 1))

        @block.tensor
        def _(pe):
            pe.sem_inc(s_wP, NW)
            pe.sem_inc(s_aP, NA)
            pe.sem_inc(s_mT, 1)
            pe.sem_inc(s_sP, JT0)
            pe.sem_inc(s_pv, JT0)
            pe.sem_inc(s_lP, 2)
            pe.sem_inc(s_yP, 2)
            pe.wait_ge(s_const, 5)
            pe.wait_ge(s_small, 16 * 7)
            pe.wait_ge(s_w, 48)
            for h in range(H0):
                pe.matmul(psM[0:1, 0:D], bkv[:, H0 + h:H0 + h + 1], wo_f[:, h, :], start=(h == 0), stop=False)
            pe.matmul(psM[0:1, 0:D], onef[0:1, 0:1], bo[:, :], start=False, stop=True).then_inc(s_br, 1)
            pe.wait_ge(s_brow, 1)
            pe.matmul(psM[:, 0:D], onef[0:1, :], brow[:, :], start=True, stop=True).then_inc(s_br, 1)
            pe.wait_ge(s_brow, 2)

            def triple(out, hi, lo, xh_, xl_, first=True, last=True):
                pe.matmul(out, hi, xh_, start=first, stop=False)
                pe.matmul(out, hi, xl_, start=False, stop=False)
                return pe.matmul(out, lo, xh_, start=False, stop=last)

            with pe.Fori(0, B) as b:
                for i in range(NW):
                    if i < 4:
                        if i == 0:
                            pe.wait_ge(s_aF, (b * H0) * NA + NA)
                            pe.wait_ge(s_pH, (b * H0) * JT0 + JT0)
                    else:
                        pe.wait_ge(s_wL, done(NW, b, NG - 1 if i == NG else i - 4))
                    ps = ring4[i % 4]
                    if i < NG:
                        k, gidx = i % KC, i // KC
                        pe.wait_ge(s_nt, b * 2 + (1 if gidx == 0 else 2))
                        for u in range(4):
                            tl = gidx * 4 + u
                            if tl >= JT0:
                                break
                            r = rows(tl, JT0, JR0)
                            src = lat[:, tl, :] if tl < ST else cx[0:r, tl - ST, :]
                            ins = pe.transpose(ps[:, u * P:u * P + r], src[:, k * P:(k + 1) * P], identf[0:r, 0:r])
                        ins.then_inc(s_wP, 1)
                    else:
                        j, half = (i - NG) // 2, (i - NG) % 2
                        r = rows(j, JT0, JR0)
                        if i == NG:
                            pe.wait_ge(s_wl, 3)
                        for k in range(KC):
                            cs = slice(j * P, j * P + r)
                            ws = slice(INNER + half * 512, INNER + half * 512 + 512)
                            ins = triple(ps[0:r, :], xth[:, k, cs], xtl[:, k, cs], wkvh[:, k, ws], wkvl[:, k, ws],
                                         k == 0, k == KC - 1)
                        ins.then_inc(s_wP, 1)

                def pre(n, h, p, what):
                    if what == "mc":
                        return
                    if what == "mT":
                        pe.wait_ge(s_mc, done(1, n, 0))
                        pe.wait_ge(s_rl, done(1, n, 0) - 2)
                        for it in range(ST):
                            ins = pe.transpose(psM[0:1, it * P:(it + 1) * P], mc[:, p, it:it + 1], identf[:, :])
                        ins.then_inc(s_mT, 1)
                        return
                    a = int(what[1:])
                    ps = psA[a % 2]
                    pe.wait_ge(s_aF, done(NA, n, a - 2))
                    if a == 0:
                        for k in range(KC):
                            ws = bass.ds(h * DH0, DH0)
                            ins = triple(ps[:, 0:S], wqh[:, k, ws], wql[:, k, ws], xth[:, k, 0:S], xtl[:, k, 0:S],
                                         k == 0, k == KC - 1)
                    elif a <= len(KCH):
                        c0, cn = KCH[a - 1]
                        for k in range(KC):
                            ws = bass.ds(h * DH0, DH0)
                            ins = triple(ps[:, 0:cn], wkvh[:, k, ws], wkvl[:, k, ws], xth[:, k, c0:c0 + cn],
                                         xtl[:, k, c0:c0 + cn], k == 0, k == KC - 1)
                    else:
                        it, c = divmod(a - 1 - len(KCH), len(KCH))
                        c0, cn = KCH[c]
                        ins = pe.matmul(ps[:, 0:cn], qh[:, p, it * P:(it + 1) * P], kh[:, p, c0:c0 + cn],
                                        start=True, stop=True)
                    ins.then_inc(s_aP, 1)

                def pv(n, h, p, j):
                    r = rows(j, JT0, JR0)
                    vs = bass.ds(h * DH0, DH0)
                    pe.wait_ge(s_pH, done(JT0, n, j))
                    if j == 0:
                        pe.wait_ge(s_oL, done(1, n, 0) - 1)
                    pe.matmul(psO[:, :], vh[0:r, j, vs], ph[0:r, PR[j], :], start=(j == 0), stop=False)
                    pe.matmul(psO[:, :], vl[0:r, j, vs], ph[0:r, PR[j], :], start=False, stop=False)
                    pe.wait_ge(s_pL, done(JT0, n, j))
                    pe.matmul(psO[:, :], vh[0:r, j, vs], pl[0:r, PR[j], :], start=False,
                              stop=(j == JT0 - 1)).then_inc(s_pv, 1)

                def tail(n, h, p, step):
                    if step == 0:
                        pe.wait_ge(s_acc, done(JT0, n, JT0 - 1))
                        pe.wait_ge(s_mrow, done(1, n, 0))
                        for it in range(ST):
                            ins = pe.matmul(psM[:, it:it + 1], acc[:, p, it * P:(it + 1) * P], four[:, :],
                                            start=True, stop=True)
                        ins.then_inc(s_lP, 1)
                        return
                    pe.wait_ge(s_oL, done(1, n, 0))
                    pe.wait_ge(s_yF, done(2, n, step - 1) - 1)
                    for u in range(2):
                        it = 2 * (step - 1) + u
                        cs = slice(it * P, (it + 1) * P)
                        ins = triple(psW[:, u, :], oh[:, cs], ol[:, cs], woh[:, bass.ds(h, 1), :].rearrange("p a n -> p (a n)"),
                                     wol[:, bass.ds(h, 1), :].rearrange("p a n -> p (a n)"))
                    ins.then_inc(s_yP, 1)

                def main(h, p, with_pre, with_tail):
                    n = b * H0 + h
                    for j in range(JT0):
                        r = rows(j, JT0, JR0)
                        js = slice(j * P, j * P + r)
                        dn, pj = before(SR, j)
                        pe.wait_ge(s_pH, done(JT0, n + dn, pj))
                        if j == 0:
                            pe.wait_ge(s_mrow, done(1, n, 0))
                        ps = psS[SR[j]][0:r, :]
                        triple(ps, kh[:, p, js], kl[:, p, js], qh[:, p, :], ql[:, p, :], True, False)
                        pe.matmul(ps, oneb[:, 0:r], mrow[:, p, :], start=False, stop=True).then_inc(s_sP, 1)
                        if j >= LAG:
                            pv(n, h, p, j - LAG)
                        elif with_tail:
                            pv(n - 1, h - 1, 1 - p, JT0 - LAG + j)
                        if with_tail and j in TAIL:
                            tail(n - 1, h - 1, 1 - p, TAIL.index(j))
                        if with_pre:
                            for what in SLOTS[j]:
                                pre(n + 1, h + 1, 1 - p, what)

                pe.wait_ge(s_wL, done(NW, b, NW - 1))
                for what in sum(SLOTS, []):
                    pre(b * H0, b * 0, 0, what)
                main(b * 0, 0, True, False)
                with pe.Fori(0, 3) as t:
                    main(t * 2 + 1, 1, True, True)
                    main(t * 2 + 2, 0, True, True)
                main(b * 0 + (H0 - 1), 1, False, True)
                for j in range(JT0 - LAG, JT0):
                    pv(b * H0 + (H0 - 1), b * 0 + (H0 - 1), 1, j)
                for step in range(3):
                    tail(b * H0 + (H0 - 1), b * 0 + (H0 - 1), 1, step)

        @block.vector
        def _(v):
            v.sem_inc(s_wL, NW)
            v.sem_inc(s_aF, NA)
            v.sem_inc(s_mc, 1)
            v.sem_inc(s_mrow, 1)
            v.sem_inc(s_pL, JT0)
            v.sem_inc(s_oL, 1)
            v.sem_inc(s_rl, 2)
            v.sem_inc(s_yF, 2)
            v.wait_ge(s_small, 16 * 7)
            v.tensor_scalar(bq[:, :], bq[:, :], WS, None, ALU.mult).then_inc(s_b16, 1)
            v.tensor_scalar(bkv[:, 0:H0], bkv[:, 0:H0], WS, None, ALU.mult).then_inc(s_b16, 1)
            v.wait_ge(s_br, 1)
            v.tensor_copy(brow[:, :], psM[0:1, 0:D]).then_inc(s_brow, 1)
            v.wait_ge(s_br, 2)
            v.tensor_copy(bb[:, :], psM[:, 0:D]).then_inc(s_brow, 1)
            for i, (lo, f, hi) in enumerate(((wkvl, wkv_f, wkvh), (wql, wq_f, wqh), (wol, wo_f, woh))):
                v.wait_ge(s_wh, i + 1)
                v.scalar_tensor_tensor(lo[:, :, :], f, WS, hi[:, :, :], ALU.mult, ALU.subtract).then_inc(s_wl, 1)
            v.wait_ge(s_const, 5)
            v.wait_ge(s_b16, 2)
            steps = [0]
            NST = 4 * ST + 2 * MT + 2 * ST + MT

            with v.Fori(0, B) as b:
                steps[0] = 0

                def step(ins):
                    ins.then_inc(s_st, 1)
                    steps[0] += 1

                def own():
                    v.wait_ge(s_st, b * NST + steps[0])

                def stats(src, slot, r=P):
                    step(v.bn_stats(st[0:r, slot, :], src))

                def aggr(slots, last_rows=P):
                    own()
                    v.nop(nofuse=True)
                    for q, s in enumerate(slots):
                        r = last_rows if q == len(slots) - 1 else P
                        step(v.bn_aggr(mv[0:r, s, :], st[0:r, s, :]))

                for u in range(ST):
                    stats(X[:, bass.ds(b * ST + u, 1), :].rearrange("p a c -> p (a c)"), u)
                aggr(range(ST))
                own()
                v.sem_inc(s_mv, 1)
                v.wait_ge(s_cx, b * 32 + 32)
                for u in range(MT):
                    r = rows(u, MT, MR)
                    stats(cx[0:r, u, :], ST + u, r)
                aggr(range(ST, ST + MT), MR)
                own()
                v.sem_inc(s_mv, 1)
                v.wait_ge(s_rstd, b * 3 + 3 + 1)
                for u in range(ST):
                    step(v.tensor_scalar(lat[:, u, :], X[:, bass.ds(b * ST + u, 1), :].rearrange("p a c -> p (a c)"),
                                         mv[:, u, 0:1], rstd[:, u:u + 1], ALU.subtract, ALU.mult))
                own()
                for u in range(ST):
                    stats(lat[:, u, :], u)
                aggr(range(ST))
                own()
                v.sem_inc(s_mv, 1)
                v.wait_ge(s_rstd, b * 3 + 3 + 2)
                for u in range(MT):
                    r = rows(u, MT, MR)
                    step(v.tensor_scalar(cx[0:r, u, :], cx[0:r, u, :], mv[0:r, ST + u, 0:1],
                                         rstd[0:r, ST + u:ST + u + 1], ALU.subtract, ALU.mult))
                v.wait_ge(s_rstd, b * 3 + 3 + 3)
                for u in range(ST):
                    step(v.tensor_scalar(lat[:, u, :], lat[:, u, :], mv[:, u, 0:1], rstd[:, u:u + 1],
                                         ALU.subtract, ALU.mult))
                own()
                v.sem_inc(s_nt, 2)

                for i in range(NW):
                    v.wait_ge(s_wH, done(NW, b, i))
                    ps = ring4[i % 4]
                    if i < NG:
                        k, gidx = i % KC, i // KC
                        c0 = gidx * 512
                        n = min(512, J0 - c0)
                        gg, be = (gl, bl) if gidx == 0 else (gm, bm)
                        if i >= 1:
                            v.wait_ge(s_wL, done(NW, b, i - 1))
                        v.tensor_scalar(tmp[:, 0:n], ps[:, 0:n], gg[:, k:k + 1], be[:, k:k + 1],
                                        ALU.mult, ALU.add).then_inc(s_wt, 1)
                        v.wait_ge(s_wt, b * NG + i + 1)
                        v.tensor_tensor(xtl[:, k, c0:c0 + n], tmp[:, 0:n], xth[:, k, c0:c0 + n],
                                        ALU.subtract).then_inc(s_wL, 1)
                    else:
                        j, half = (i - NG) // 2, (i - NG) % 2
                        r = rows(j, JT0, JR0)
                        cs = slice(half * 512, half * 512 + 512)
                        v.tensor_tensor(vl[0:r, j, cs], ps[0:r, :], vh[0:r, j, cs], ALU.subtract).then_inc(s_wL, 1)

                def pre(n, h, p, what):
                    if what == "mc":
                        v.wait_ge(s_aF, done(NA, n, NA - 1))
                        v.tensor_reduce(mc[:, p, :], mx[:, p, :, :], AX.X, ALU.max).then_inc(s_mc, 1)
                        return
                    if what == "mT":
                        v.wait_ge(s_mT, done(1, n, 0))
                        v.tensor_scalar(mrow[:, p, :], psM[0:1, :], -1.0, None, ALU.mult).then_inc(s_mrow, 1)
                        return
                    a = int(what[1:])
                    ps = psA[a % 2]
                    if a <= len(KCH):
                        v.wait_ge(s_aH, done(1 + len(KCH), n, a))
                        if a == 0:
                            v.scalar_tensor_tensor(ql[:, p, :], ps[:, :], bq[:, bass.ds(h, 1)], qh[:, p, :],
                                                   ALU.add, ALU.subtract).then_inc(s_aF, 1)
                        else:
                            c0, cn = KCH[a - 1]
                            v.scalar_tensor_tensor(kl[:, p, c0:c0 + cn], ps[:, 0:cn], bkv[:, bass.ds(h, 1)],
                                                   kh[:, p, c0:c0 + cn], ALU.add, ALU.subtract).then_inc(s_aF, 1)
                    else:
                        it, c = divmod(a - 1 - len(KCH), len(KCH))
                        c0, cn = KCH[c]
                        v.wait_ge(s_aP, done(NA, n, a))
                        v.tensor_reduce(mx[:, p, it, c:c + 1], ps[:, 0:cn], AX.X, ALU.max).then_inc(s_aF, 1)

                def out_lo(n):
                    v.wait_ge(s_oH, done(1, n, 0))
                    v.wait_ge(s_yP, done(2, n, 1) - 2)
                    v.scalar_tensor_tensor(ol[:, :], psO[:, :], 1.0 / 64, oh[:, :], ALU.mult,
                                           ALU.subtract).then_inc(s_oL, 1)

                def tail(n, h, p, step_):
                    if step_ == 0:
                        v.wait_ge(s_lP, done(1, n, 0) + 1)
                        v.reciprocal(rl[:, p, :], psM[:, 0:ST]).then_inc(s_rl, 1)
                        return
                    v.wait_ge(s_yP, done(2, n, step_ - 1))
                    v.wait_ge(s_rl, done(1, n, 0) + 1)
                    if step_ == 1:
                        v.wait_ge(s_yF, done(2, n, -1))
                    for u in range(2):
                        it = 2 * (step_ - 1) + u
                        xs = X[:, bass.ds(b * ST + it, 1), :].rearrange("p a c -> p (a c)")
                        ins = v.scalar_tensor_tensor(xs, psW[:, u, :], rl[:, p, it:it + 1], xs, ALU.mult, ALU.add)
                    ins.then_inc(s_yF, 1)

                def main(h, p, with_pre, with_tail):
                    n = b * H0 + h
                    def low(j):
                        r = rows(j, JT0, JR0)
                        dn, pj = before(PR, j)
                        v.wait_ge(s_pH, done(JT0, n, j))
                        v.wait_ge(s_pv, done(JT0, n + dn, pj))
                        v.tensor_tensor(pl[0:r, PR[j], :], pf[0:r, PR[j], :], ph[0:r, PR[j], :],
                                        ALU.subtract).then_inc(s_pL, 1)

                    for j in range(JT0):
                        if j >= 1:
                            low(j - 1)
                        if with_tail and j == LAG:
                            out_lo(n - 1)
                        if with_tail and j in TAIL:
                            tail(n - 1, h - 1, 1 - p, TAIL.index(j))
                        if with_pre:
                            for what in SLOTS[j]:
                                pre(n + 1, h + 1, 1 - p, what)
                    low(JT0 - 1)

                for what in sum(SLOTS, []):
                    pre(b * H0, b * 0, 0, what)
                main(b * 0, 0, True, False)
                with v.Fori(0, 3) as t:
                    main(t * 2 + 1, 1, True, True)
                    main(t * 2 + 2, 0, True, True)
                main(b * 0 + (H0 - 1), 1, False, True)
                out_lo(b * H0 + (H0 - 1))
                for step_ in range(3):
                    tail(b * H0 + (H0 - 1), b * 0 + (H0 - 1), 1, step_)
            v.wait_ge(s_yF, 2 * (B * H0 + 1))
            for t in range(NT):
                ins = v.tensor_tensor(X[:, t, :], X[:, t, :], bb[:, :], ALU.add)
            ins.then_inc(s_fin, 1)
            v.wait_ge(s_fin, 1)


def experts(nc, X, identf, io, layer):
    E, F = 8, 1024
    FT = F // P
    T = B * S
    CH = 256
    IT = CH // P
    CAP = 2 * T // E
    NC = E * CAP // CH if layer == 0 else 2 * T // CH + E
    ROWS = (NC + 1) * CH
    MAXC = T // CH
    U32, I32 = mybir.dt.uint32, mybir.dt.int32
    names = {0: ("L0_ffn_w_router", "L0_ffn_w1", "L0_ffn_w2"),
             1: ("L1_ffn_Wr", "L1_ffn_W1", "L1_ffn_W2")}[layer]
    GELU = ACT.Gelu_apprx_tanh if layer == 0 else ACT.Gelu
    GI = KC * NT // 4
    PR = ring(FT, 4)
    HR = ring(FT, 3)
    GR = 4

    with ExitStack() as ctx:
        tag = f"f{layer}_"

        def sb(name, shape, dt=F32):
            return ctx.enter_context(nc.sbuf_tensor(tag + name, shape, dt))

        def sem(name):
            return ctx.enter_context(nc.semaphore(tag + name))

        w16 = sb("w16", [P, E, 4, KC * F], F16)
        stage = sb("stage", [P, 2, KC * F])
        wt = sb("wt", [E, NT, P]) if layer else None
        xth, xtl = w16[:, E - 1, 0:2, :], w16[:, E - 1, 2:4, :]
        xn = sb("xn", [P, NT, D])
        room = xn[:, :, :].rearrange("p t c -> p (t c)")
        hf = room[:, 0:1024].rearrange("p (r t) -> p r t", t=CH)
        xb = room[:, 1024:2048].rearrange("p (b u c) -> p b u c", b=2, c=D)
        yb = room[:, 2048:3072].rearrange("p (b u c) -> p b u c", b=2, c=D)
        hh = room[:, 3072:3584].bitcast(F16).rearrange("p (r t) -> p r t", t=CH)
        hl = room[:, 3584:4096].bitcast(F16).rearrange("p (r t) -> p r t", t=CH)
        gy = xn[:, 0:GR, :]
        xh, xl = sb("xh", [P, 2, KC, CH], F16), sb("xl", [P, 2, KC, CH], F16)
        st, mv = sb("st", [P, NT, 6]), sb("mv", [P, NT, 2])
        ve, mhalf, rstd = sb("ve", [P, NT]), sb("mhalf", [P, NT]), sb("rstd", [P, NT])
        wr, wrh, wrl = sb("wr", [P, KC, E]), sb("wrh", [P, KC, E], F16), sb("wrl", [P, KC, E], F16)
        brb = sb("brb", [P, E])
        b2 = sb("b2", [E, D])
        bias = sb("bias", [1, D])
        b1r = sb("b1r", [E * FT, P])
        b1 = sb("b1", [P, E, FT])
        b1e = sb("b1e", [P, 2, FT])
        ones, upper = sb("ones", [P, P]), sb("upper", [P, P])
        zero = sb("zero", [P, D])
        revi, iexp, thr = sb("revi", [P, E]), sb("iexp", [P, E]), sb("thr", [P, MAXC])
        lg, ex, sc, sc2, eq, cand, oh1, oh2, wgt, off, tot = (
            sb(n, [P, NT, E]) for n in ("lg", "ex", "sc", "sc2", "eq", "cand", "oh1", "oh2", "wgt", "off", "tot"))
        m1, m2, f1, sm, rs = (sb(n, [P, NT]) for n in ("m1", "m2", "f1", "sm", "rs"))
        pos, wk = sb("pos", [P, 2, NT]), sb("wk", [P, 2, NT])
        vd, dump = sb("vd", [P, 2, NT]), sb("dump", [P, 2, NT])
        dumpi = sb("dumpi", [P, 2, NT], I32)
        sidx, gidx = sb("sidx", [P, 2, NT], U32), sb("gidx", [P, 2, NT], U32)
        nch, cb, base = sb("nch", [P, E]), sb("cb", [P, E]), sb("base", [P, E])
        cmpc = sb("cmpc", [P, E, MAXC])
        ci, ciE = sb("ci", [1, NC], I32), sb("ciE", [1, NC, E])
        cf, tf = sb("cf", [1, NC]), sb("tf", [1, NC + 1])
        table = sb("table", [1, NC + 1], I32)
        tie_e = sb("tie_e", [1, T // CH * E + 1], I32)
        rest, restf, flag = sb("rest", [P, 1]), sb("restf", [1, 1]), sb("flag", [1, 1], I32)

        xrows = nc.dram_tensor(tag + "xrows", (ROWS + 2 * T, D), F32, kind="Internal").ap()
        yrows = nc.dram_tensor(tag + "yrows", (NC * CH, D), F32, kind="Internal").ap()
        xall = nc.dram_tensor(tag + "xall", (T + CH, D), F32, kind="Internal").ap()

        psH = [ctx.enter_context(nc.psum_tensor(tag + f"psH{i}", [P, 512], F32)) for i in range(3)]
        psX = ctx.enter_context(nc.psum_tensor(tag + "psX", [P, 512], F32))
        psY = [ctx.enter_context(nc.psum_tensor(tag + f"psY{i}", [P, 512], F32)) for i in range(2 * IT)]
        ring4 = psH + [psX]

        s_const = sem("const")
        s_z = sem("z")
        s_small = sem("small")
        s_w = [sem("w0"), sem("w1")]
        s_wh = sem("wh")
        s_wl = sem("wl")
        s_st = sem("st")
        s_mv = sem("mv")
        s_pool = sem("pool")
        s_rstd = sem("rstd")
        s_nt = sem("nt")
        s_tP = sem("tP")
        s_tH = sem("tH")
        s_tL = sem("tL")
        s_wr = sem("wr")
        s_lg = sem("lg")
        s_b1 = sem("b1")
        s_sh = sem("sh")
        s_ex = sem("ex")
        s_sel = sem("sel")
        s_rk = sem("rk")
        s_idx = sem("idx")
        s_rest = sem("rest")
        s_tab = sem("tab")
        s_sc = sem("sc")
        s_wtP = sem("wtP")
        s_wtF = sem("wtF")
        s_gy = [sem(f"gy{i}") for i in range(GR)]
        s_gu = sem("gu")

        class Loop:

            def __init__(self, name):
                self.xb = [sem(name + "xb0"), sem(name + "xb1")]
                self.ys = [sem(name + "ys0"), sem(name + "ys1")]
                self.xP = sem(name + "xP")
                self.xH = sem(name + "xH")
                self.xL = sem(name + "xL")
                self.b1 = sem(name + "b1")
                self.hP = sem(name + "hP")
                self.hH = sem(name + "hH")
                self.hF = sem(name + "hF")
                self.hL = sem(name + "hL")
                self.hU = sem(name + "hU")
                self.yF = sem(name + "yF")

        main = Loop("m")
        TC = T // CH
        NTIE = E * TC

        block = ctx.enter_context(nc.Block(no_gpsimd_drain=True))
        NSMALL = 4 if layer else 2
        NCONST = 5 + 2 * E + MAXC + 5
        PIECES, EARLY = FT, 2
        PH = PIECES // 2
        PS = KC * F // PH


        def load_rows(sp, L, m, p, src):
            sp.wait_ge(L.xP, m * 2 + p + 1)
            sp.dma_start(xb[:, p, :, :], src.rearrange("(u p) c -> p u c", p=P)).then_inc(L.xb[p], 16)

        def pe_turn(pe, L, m, p):
            n = m * 2 + p
            pe.wait_ge(L.xb[p], m * 16 + 16)
            pe.wait_ge(L.xL, n + 1)
            for k in range(KC):
                for u in range(IT):
                    ins = pe.transpose(psX[:, k * CH + u * P:k * CH + (u + 1) * P],
                                       xb[:, p, u, k * P:(k + 1) * P], identf[:, :])
            ins.then_inc(L.xP, 1)

        def pe_hidden(pe, L, n, p, e, f):
            dn, pf = before(HR, f)
            pe.wait_ge(L.hF, done(FT, n + dn, pf))
            ps = psH[HR[f]][:, 0:CH]
            for k in range(KC):
                ks = slice(k * F + f * P, k * F + (f + 1) * P)
                a, b_ = (w16[:, bass.ds(e, 1), part, ks].rearrange("p a f -> p (a f)") for part in (0, 1))
                pe.matmul(ps, a, xh[:, p, k, :], start=(k == 0), stop=False)
                pe.matmul(ps, a, xl[:, p, k, :], start=False, stop=False)
                ins = pe.matmul(ps, b_, xh[:, p, k, :], start=False, stop=(k == KC - 1))
            ins.then_inc(L.hP, 1)

        def pe_output(pe, L, n, p, e, f):
            ds = slice(f * D, (f + 1) * D)
            a, b_ = (w16[:, bass.ds(e, 1), part, ds].rearrange("p a d -> p (a d)") for part in (2, 3))
            if f == 0:
                pe.wait_ge(L.yF, n + 1)
            pe.wait_ge(L.hH, done(FT, n, f))
            for it in range(IT):
                y, h = psY[p * IT + it][:, 0:D], hh[:, PR[f], it * P:(it + 1) * P]
                pe.matmul(y, h, a, start=(f == 0), stop=False)
                pe.matmul(y, h, b_, start=False, stop=False)
            pe.wait_ge(L.hL, done(FT, n, f))
            for it in range(IT):
                y, h = psY[p * IT + it][:, 0:D], hl[:, PR[f], it * P:(it + 1) * P]
                ins = pe.matmul(y, h, a, start=False, stop=(f == FT - 1))
            ins.then_inc(L.hU, 1)

        def pe_chunk(pe, L, m, p, experts_of, c, splits):
            n = m * 2 + p
            e, e_next = (pe.value_load(experts_of[0:1, bass.ds(c + i, 1)], min_val=0, max_val=E - 1)
                         for i in range(2))
            for f in range(2, FT):
                pe_hidden(pe, L, n, p, e, f)
                pe_output(pe, L, n, p, e, f - 2)
                if f == 3:
                    pe_turn(pe, L, m + p, 1 - p)
            pe.wait_ge(L.xL, n + 3)
            if splits:
                pe.wait_ge(s_wl, (n + 3) * PIECES)
            for f in range(2):
                pe_hidden(pe, L, n + 1, 1 - p, e_next, f)
                pe_output(pe, L, n, p, e, FT - 2 + f)

        def split_high(act, e, q):
            half, cs = q // PH, slice(q % PH * PS, (q % PH + 1) * PS)
            act.wait_ge(s_w[half], e * 16 + 16)
            act.nop(nofuse=True)
            w = w16[:, bass.ds(e, 1), 2 * half, cs].rearrange("p a f -> p (a f)")
            act.activation(w, stage[:, half, cs], ACT.Copy, scale=WS).then_inc(s_wh, 1)

        def split_low(v, e, q):
            half, cs = q // PH, slice(q % PH * PS, (q % PH + 1) * PS)
            v.wait_ge(s_wh, e * PIECES + q + 1)
            w = [w16[:, bass.ds(e, 1), 2 * half + part, cs].rearrange("p a f -> p (a f)") for part in (0, 1)]
            v.scalar_tensor_tensor(w[1], stage[:, half, cs], WS, w[0], ALU.mult, ALU.subtract).then_inc(s_wl, 1)

        def act_turn(act, L, m, p):
            act.wait_ge(L.xP, m * 2 + p + 3)
            act.activation(xh[:, p, :, :].rearrange("p k t -> p (k t)"), psX[:, :], ACT.Copy).then_inc(L.xH, 1)

        def act_chunk(act, L, m, p, splits):
            n = m * 2 + p
            if layer:
                act.wait_ge(L.b1, n + 1)
                act.nop(nofuse=True)
            for f in range(FT):
                dn, pf = before(PR, f)
                bs = b1e[:, p, f:f + 1] if layer else 0.0
                ps = psH[HR[f]][:, 0:CH]
                act.wait_ge(L.hP, n * FT + f + 1)
                act.wait_ge(L.hU, done(FT, n + dn, pf))
                act.activation(hh[:, PR[f], :], ps, GELU, bias=bs, scale=1.0 / WS).then_inc(L.hH, 1)
                act.wait_ge(L.hL, done(FT, n + dn, pf))
                act.activation(hf[:, PR[f], :], ps, GELU, bias=bs, scale=1.0 / WS).then_inc(L.hF, 1)
                if f == 4:
                    act_turn(act, L, m + p, 1 - p)
                if splits:
                    split_high(act, n + EARLY, f)

        def dve_turn(v, L, m, p):
            v.wait_ge(L.xH, m * 2 + p + 1)
            v.tensor_tensor(xl[:, p, :, :].rearrange("p k t -> p (k t)"), psX[:, :],
                            xh[:, p, :, :].rearrange("p k t -> p (k t)"), ALU.subtract).then_inc(L.xL, 1)

        def dve_bias(v, L, m, p, e, wait=True):
            if wait:
                v.wait_ge(L.hF, done(FT, m * 2 + p - 1, -1))
                v.nop(nofuse=True)
            v.tensor_copy(b1e[:, p, :], b1[:, bass.ds(e, 1), :].rearrange("p a f -> p (a f)")).then_inc(L.b1, 1)

        def dve_chunk(v, L, m, p, take, splits, bias_next):
            n = m * 2 + p
            for f in range(FT):
                dn, pf = before(PR, f)
                v.wait_ge(L.hF, done(FT, n, f))
                v.wait_ge(L.hU, done(FT, n + dn, pf))
                v.tensor_tensor(hl[:, PR[f], :], hf[:, PR[f], :], hh[:, PR[f], :], ALU.subtract).then_inc(L.hL, 1)
                if f == 4:
                    dve_turn(v, L, m + p, 1 - p)
                if f == 5 and layer:
                    bias_next()
                if splits:
                    split_low(v, n + EARLY, f)
            v.wait_ge(L.hU, done(FT, n, FT - 1))
            take(n)

        @block.sync
        def _(sp):
            sp.dma_start(wr[:, :, :], io[names[0]].rearrange("(k p) e -> p k e", p=P)).then_inc(s_small, 16)
            if layer:
                sp.dma_start(brb[:, :], io["L1_ffn_br"].rearrange("(a e) -> a e", a=1).to_broadcast([P, E])
                             ).then_inc(s_small, 16)
                sp.dma_start(b2[:, :], io["L1_ffn_b2"]).then_inc(s_small, 16)
                sp.dma_start(b1r[:, :], io["L1_ffn_b1"].rearrange("e (f p) -> (e f) p", p=P)).then_inc(s_small, 16)
            else:
                sp.dma_start(bias[:, :], io["L0_ffn_bias"].rearrange("a b d -> (a b) d")).then_inc(s_small, 16)
            def load_weights(e, half):
                sp.wait_ge(s_wl, (e + 1) * PIECES - PIECES + (half + 1) * PH)
                if half == 0:
                    src = io[names[1]][bass.ds(e, 1)].rearrange("a (k p) f -> p (a k) f", p=P)
                    dst = stage[:, 0, :].rearrange("p (k f) -> p k f", k=KC)
                else:
                    src = io[names[2]][bass.ds(e, 1)].rearrange("a (f p) d -> p (a f) d", p=P)
                    dst = stage[:, 1, :].rearrange("p (f d) -> p f d", f=FT)
                sp.dma_start(dst, src).then_inc(s_w[half], 16)

            def load_chunk(m, p):
                load_rows(sp, main, m, p, xrows[bass.ds((m * 2 + p) * CH, CH), :])

            with sp.Fori(0, EARLY + 1) as e:
                for half in range(2):
                    load_weights(e, half)
            sp.wait_ge(s_z, 16)
            sp.wait_ge(s_sc, 16 * (2 * NT + 2 * layer))
            for c in range(EARLY + 1):
                load_chunk(c // 2, c % 2)
            def store(m, p):
                n = m * 2 + p
                sp.wait_ge(main.yF, n + 3)
                sp.dma_start(yrows[bass.ds(n * CH, CH), :].rearrange("(u p) c -> p u c", p=P),
                             yb[:, p, :, :]).then_inc(main.ys[p], 16)

            load_weights(3, 0)
            load_chunk(1, 1)
            load_weights(3, 1)
            store(0, 0)
            with sp.Fori(2, E // 2) as m:
                for p in range(2):
                    load_weights(m * 2 + p, 0)
                    load_chunk(m, p)
                    load_weights(m * 2 + p, 1)
                    store(m - 2 + p, 1 - p)
            with sp.Fori(E // 2, NC // 2) as m:
                for p in range(2):
                    load_chunk(m, p)
                    store(m - 2 + p, 1 - p)
            load_rows(sp, main, NC // 2, 0, xall[0:CH, :] if layer else xrows[NC * CH:(NC + 1) * CH, :])
            for n in range(NC - 3, NC):
                store(n // 2, n % 2)
            if layer:
                sp.wait_ge(s_tab, 1)
                found = sp.value_load(flag[0:1, 0:1], min_val=0, max_val=T * E)
                with sp.If(found > 0):
                    sp.wait_ge(s_gu, 2 * NT)
                    with sp.Fori(0, E) as e:
                        with sp.Fori(0, TC // 2) as c:
                            m = e * (TC // 2) + c + NC // 2
                            load_rows(sp, main, m, 1, xall[bass.ds((c * 2 + 1) * CH, CH), :])
                            load_rows(sp, main, m + 1, 0, xall[bass.ds((c * 2 + 2) * CH, CH), :])
                    sp.wait_ge(main.xb[0], 16 * ((NC + NTIE) // 2 + 1))
            sp.wait_ge(main.xb[0], 16 * (NC // 2 + 1))

        @block.gpsimd
        def _(g):
            k = [0]

            def const(ap, val):
                g.memset(ap, val).then_inc(s_const, 1)
                k[0] += 1

            for ap, val in ((mhalf[:, :], -0.5), (ones[:, :], 1.0), (upper[:, :], 0.0), (zero[:, :], 0.0)):
                const(ap, val)
            for e in range(E):
                const(revi[:, e:e + 1], float(E - e))
                const(iexp[:, e:e + 1], float(e))
            for c in range(MAXC):
                const(thr[:, c:c + 1], float(c * CH) if c else -1.0)
            g.wait_ge(s_const, k[0])
            g.affine_select(out=upper[:, :], in_=upper[:, :], compare_op=ALU.is_ge, fill=1.0, base=0,
                            pattern=[[-1, P]], channel_multiplier=1).then_inc(s_const, 1)
            g.iota(dumpi[:, :, :], pattern=[[T, 2], [P, NT]], base=ROWS, channel_multiplier=1).then_inc(s_const, 1)
            if layer:
                g.iota(ci[:, :], pattern=[[1, NC]], base=0, channel_multiplier=0).then_inc(s_const, 1)
                g.iota(tie_e[:, 0:NTIE], pattern=[[1, E], [0, TC]], base=0, channel_multiplier=0).then_inc(s_const, 1)
                g.iota(tie_e[:, NTIE:NTIE + 1], pattern=[[1, 1]], base=0, channel_multiplier=0).then_inc(s_const, 1)
            else:
                g.iota(table[:, 0:NC], pattern=[[1, E], [0, NC // E]], base=0, channel_multiplier=0
                       ).then_inc(s_const, 1)
                g.iota(table[:, NC:NC + 1], pattern=[[1, 1]], base=0, channel_multiplier=0).then_inc(s_const, 1)
                g.sem_inc(s_const, 1)
            g.sem_inc(s_const, 1)
            g.wait_ge(s_const, NCONST)
            g.dma_start(xrows[0:ROWS, :].rearrange("(t p) c -> p t c", p=P),
                        zero[:, :].unsqueeze(1).broadcast_to([P, ROWS // P, D])).then_inc(s_z, 16)
            g.wait_ge(s_mv, 1)
            g.tensor_scalar(ve[:, :], mv[:, :, 1], EPS, None, ALU.add).then_inc(s_pool, 1)
            g.wait_ge(s_pool, 1)
            g.tensor_tensor(rstd[:, :], ve[:, :], mhalf[:, :], ALU.pow).then_inc(s_rstd, 1)
            if layer:
                g.wait_ge(s_nt, NT)
                g.dma_start(xall[0:T, :].rearrange("(t p) c -> p t c", p=P), xn[:, :, :]).then_inc(s_sc, 16)
                g.dma_start(xall[T:T + CH, :].rearrange("(t p) c -> p t c", p=P), xn[:, 0:IT, :]).then_inc(s_sc, 16)
            g.wait_ge(s_z, 16)
            g.wait_ge(s_idx, 1)
            for t in range(NT):
                for q in range(2):
                    g.indirect_dma_start(xrows, bass.IndirectOffsetOnAxis(ap=sidx[:, q, t:t + 1], axis=0),
                                         xn[:, t, :], None).then_inc(s_sc, 16)
            g.wait_ge(main.yF, NC + 2)
            g.wait_ge(main.xb[0], 16 * (NC // 2 + 1))
            for p in range(2):
                g.wait_ge(main.ys[p], 16 * (NC // 2 + 1))
            for i in range(2 * NT):
                t, q = i // 2, i % 2
                if i >= GR:
                    g.wait_ge(s_gu, i - GR + 1)
                g.indirect_dma_start(gy[:, i % GR, :], None, yrows,
                                     bass.IndirectOffsetOnAxis(ap=gidx[:, q, t:t + 1], axis=0)
                                     ).then_inc(s_gy[i % GR], 16)

        @block.scalar
        def _(act):
            act.sem_inc(main.hF, FT)
            act.sem_inc(main.hH, FT)
            act.wait_ge(s_small, 16 * NSMALL)
            act.activation(wrh[:, :, :], wr[:, :, :], ACT.Copy, scale=WS).then_inc(s_wr, 1)
            for i in range(GI):
                kk, q = i % KC, i // KC
                act.wait_ge(s_tP, i + 1)
                act.activation(xth[:, kk, q * 512:q * 512 + 512], ring4[i % 4][:, :], ACT.Copy).then_inc(s_tH, 1)
            act.wait_ge(s_sh, 1)
            act.activation(ex[:, :, :], sc2[:, :, :], ACT.Exp).then_inc(s_ex, 1)
            act.wait_ge(s_lg, 1)
            with act.Fori(0, EARLY) as e:
                for q in range(PIECES):
                    split_high(act, e, q)
            act_turn(act, main, 0, 0)
            for first, last, splits in ((0, (E - EARLY) // 2, True), ((E - EARLY) // 2, NC // 2, False)):
                with act.Fori(first, last) as m:
                    for p in range(2):
                        act_chunk(act, main, m, p, splits)
            for p in range(2):
                act.wait_ge(main.ys[p], 16 * (NC // 2 + 1))
            if layer:
                act.wait_ge(s_tab, 1)
                found = act.value_load(flag[0:1, 0:1], min_val=0, max_val=T * E)
                with act.If(found > 0):
                    act.wait_ge(s_gu, 2 * NT)
                    with act.Fori(NC // 2, (NC + NTIE) // 2) as m:
                        for p in range(2):
                            act_chunk(act, main, m, p, False)

        @block.tensor
        def _(pe):
            pe.sem_inc(main.xP, 2)
            pe.sem_inc(main.hU, FT)
            pe.wait_ge(s_const, NCONST)
            pe.wait_ge(s_small, 16 * NSMALL)
            for i in range(GI):
                kk, q = i % KC, i // KC
                pe.wait_ge(s_nt, 4 * q + 4)
                if i >= 4:
                    pe.wait_ge(s_tL, i - 3)
                for u in range(4):
                    ins = pe.transpose(ring4[i % 4][:, u * P:(u + 1) * P], xn[:, 4 * q + u, kk * P:(kk + 1) * P],
                                       identf[:, :])
                ins.then_inc(s_tP, 1)
            if layer:
                pe.transpose(psY[1][:, 0:E * FT], b1r[:, :], identf[0:E * FT, 0:E * FT]).then_inc(s_b1, 1)
            pe.wait_ge(s_tL, GI)
            pe.wait_ge(s_wr, 2)
            for t in range(NT):
                ts = slice(t * P, (t + 1) * P)
                for kk in range(KC):
                    for j, (a, w) in enumerate(((xth, wrh), (xth, wrl), (xtl, wrh))):
                        ins = pe.matmul(psY[0][:, t * E:(t + 1) * E], a[:, kk, ts], w[:, kk, :],
                                        start=(kk == 0 and j == 0), stop=(kk == KC - 1 and j == 2))
            ins.then_inc(s_lg, 1)
            pe.wait_ge(s_sel, 1)
            sel = cand[:, :, :].rearrange("p t e -> p (t e)")
            pe.matmul(psY[2][:, 0:NT * E], upper[:, :], sel, start=True, stop=True)
            pe.matmul(psY[3][:, 0:NT * E], ones[:, :], sel, start=True, stop=True).then_inc(s_rk, 1)
            if layer:
                pe.wait_ge(s_rest, 1)
                pe.matmul(psY[1][0:1, 0:1], ones[:, 0:1], rest[:, :], start=True, stop=True).then_inc(s_rk, 1)
                pe.wait_ge(s_tab, 1)

            pe.wait_ge(s_idx, 1)
            nq = NT // 4 if layer else 0
            for q in range(nq):
                if q >= 2:
                    pe.wait_ge(s_wtF, q - 1)
                for u in range(4):
                    ins = pe.transpose(psH[q % 2][0:E, u * P:(u + 1) * P], wgt[:, 4 * q + u, :], identf[:, :])
                ins.then_inc(s_wtP, 1)
            for t in range(NT):
                if layer:
                    pe.wait_ge(s_wtF, nq + max(0, t - 3))
                    ins = pe.matmul(psY[t % 4][:, 0:D], wt[:, t, :], b2[:, :], start=True, stop=True)
                else:
                    if t >= 4:
                        pe.wait_ge(s_wtF, t - 3)
                    ins = pe.matmul(psY[t % 4][:, 0:D], ones[0:1, :], bias[:, :], start=True, stop=True)
                ins.then_inc(s_wtP, 1)
            pe.wait_ge(s_wtF, nq + NT)

            pe_turn(pe, main, 0, 0)
            pe.wait_ge(main.xL, 2)
            pe.wait_ge(s_wl, 2 * PIECES)
            for f in range(2):
                pe_hidden(pe, main, 0, 0, 0, f)
            for first, last, splits in ((0, (E - EARLY) // 2, True), ((E - EARLY) // 2, NC // 2, False)):
                with pe.Fori(first, last) as m:
                    for p in range(2):
                        pe_chunk(pe, main, m, p, table, m * 2 + p, splits)
                if splits:
                    pe.wait_ge(s_wl, (E + 1) * PIECES)
            if layer:
                found = pe.value_load(flag[0:1, 0:1], min_val=0, max_val=T * E)
                with pe.If(found > 0):
                    pe.wait_ge(s_gu, 2 * NT)
                    with pe.Fori(0, NTIE // 2) as m:
                        for p in range(2):
                            pe_chunk(pe, main, m + NC // 2, p, tie_e, m * 2 + p, False)

        @block.vector
        def _(v):
            v.sem_inc(s_wl, PIECES)
            v.sem_inc(main.xL, 1)
            v.sem_inc(main.hL, FT)
            v.sem_inc(main.yF, 2)
            v.sem_inc(main.ys[0], 16)
            v.sem_inc(main.ys[1], 16)
            ch = Chain(v, s_st)
            v.wait_ge(s_const, NCONST)
            v.wait_ge(s_small, 16 * NSMALL)
            for t in range(NT):
                ch.step(v.bn_stats(st[:, t, :], X[:, t, :]))
            ch.wait()
            for t in range(NT):
                ch.step(v.bn_aggr(mv[:, t, :], st[:, t, :]))
            ch.wait()
            v.sem_inc(s_mv, 1)
            v.wait_ge(s_wr, 1)
            v.scalar_tensor_tensor(wrl[:, :, :], wr[:, :, :], WS, wrh[:, :, :], ALU.mult,
                                   ALU.subtract).then_inc(s_wr, 1)
            ch.step(v.tensor_copy(dump[:, :, :], dumpi[:, :, :]))
            if layer:
                ch.step(v.tensor_copy(cf[:, :], ci[:, :]))
            v.wait_ge(s_rstd, 1)
            for t in range(NT):
                v.tensor_scalar(xn[:, t, :], X[:, t, :], mv[:, t, 0:1], rstd[:, t:t + 1], ALU.subtract,
                                ALU.mult).then_inc(s_nt, 1)
            for i in range(GI):
                kk, q = i % KC, i // KC
                cs = slice(q * 512, q * 512 + 512)
                v.wait_ge(s_tH, i + 1)
                v.tensor_tensor(xtl[:, kk, cs], ring4[i % 4][:, :], xth[:, kk, cs], ALU.subtract).then_inc(s_tL, 1)
            if layer:
                v.wait_ge(s_b1, 1)
                ch.step(v.tensor_copy(b1[:, :, :].rearrange("p e f -> p (e f)"), psY[1][:, 0:E * FT]))

            def wide(t):
                return t[:, :].unsqueeze(2).broadcast_to([P, NT, E])

            def along(t):
                return t[:, :].unsqueeze(1).broadcast_to([P, NT, E])

            def op(ins):
                ch.step(ins)
                ch.wait()

            def first_max(src, mval, onehot):
                op(v.tensor_reduce(mval[:, :], src, AX.X, ALU.max))
                op(v.tensor_tensor(eq[:, :, :], src, wide(mval), ALU.is_ge))
                op(v.tensor_tensor(cand[:, :, :], eq[:, :, :], along(revi), ALU.mult))
                op(v.tensor_reduce(f1[:, :], cand[:, :, :], AX.X, ALU.max))
                op(v.tensor_tensor(onehot[:, :, :], along(revi), wide(f1), ALU.is_equal))

            def tiles(ps):
                return ps[:, 0:NT * E].rearrange("p (t e) -> p t e", e=E)

            v.wait_ge(s_lg, 1)
            op(v.tensor_scalar(lg[:, :, :], tiles(psY[0]), 1.0 / WS, None, ALU.mult))
            if layer:
                op(v.tensor_tensor(lg[:, :, :], lg[:, :, :], along(brb), ALU.add))
            op(v.tensor_reduce(m1[:, :], lg[:, :, :], AX.X, ALU.max))
            v.tensor_tensor(sc2[:, :, :], lg[:, :, :], wide(m1), ALU.subtract).then_inc(s_sh, 1)
            v.wait_ge(s_ex, 1)
            if not layer:
                op(v.tensor_reduce(sm[:, :], ex[:, :, :], AX.X, ALU.add))
                op(v.reciprocal(rs[:, :], sm[:, :]))
                op(v.tensor_tensor(sc[:, :, :], ex[:, :, :], wide(rs), ALU.mult))
                first_max(sc[:, :, :], m1, oh1)
                op(v.scalar_tensor_tensor(sc2[:, :, :], oh1[:, :, :], -2.0, sc[:, :, :], ALU.mult, ALU.add))
                first_max(sc2[:, :, :], m2, oh2)
                op(v.tensor_copy(wgt[:, :, :], sc[:, :, :]))
            else:
                first_max(lg[:, :, :], m2, oh1)
                op(v.scalar_tensor_tensor(sc2[:, :, :], oh1[:, :, :], -3.0e38, lg[:, :, :], ALU.mult, ALU.add))
                first_max(sc2[:, :, :], m2, oh2)
                op(v.tensor_tensor(eq[:, :, :], lg[:, :, :], wide(m2), ALU.is_ge))
                op(v.tensor_tensor(sc[:, :, :], eq[:, :, :], ex[:, :, :], ALU.mult))
                op(v.tensor_reduce(sm[:, :], sc[:, :, :], AX.X, ALU.add))
                op(v.reciprocal(rs[:, :], sm[:, :]))
                op(v.tensor_tensor(wgt[:, :, :], sc[:, :, :], wide(rs), ALU.mult))
            op(v.tensor_tensor(cand[:, :, :], oh1[:, :, :], oh2[:, :, :], ALU.add))
            v.sem_inc(s_sel, 1)
            if layer:
                op(v.tensor_tensor(sc2[:, :, :], eq[:, :, :], cand[:, :, :], ALU.subtract))
                op(v.tensor_reduce(rest[:, :], sc2[:, :, :].rearrange("p t e -> p (t e)"), AX.X, ALU.add))
                v.sem_inc(s_rest, 1)
                op(v.tensor_tensor(sc[:, :, :], sc2[:, :, :], wgt[:, :, :], ALU.mult))
                op(v.tensor_scalar(sc[:, :, :], sc[:, :, :], 1.0 / WS, None, ALU.mult))
            v.wait_ge(s_rk, 1)
            op(v.tensor_copy(tot[:, :, :], tiles(psY[3])))
            op(v.memset(off[:, 0, :], 0.0))
            for t in range(1, NT):
                op(v.tensor_tensor(off[:, t, :], off[:, t - 1, :], tot[:, t - 1, :], ALU.add))
            if layer:
                op(v.tensor_tensor(nch[:, :], off[:, NT - 1, :], tot[:, NT - 1, :], ALU.add))
            op(v.tensor_tensor(off[:, :, :], tiles(psY[2]), off[:, :, :], ALU.add))
            if layer:
                op(v.tensor_tensor(cmpc[:, :, :], nch[:, :].unsqueeze(2).broadcast_to([P, E, MAXC]),
                                   thr[:, :].unsqueeze(1).broadcast_to([P, E, MAXC]), ALU.is_gt))
                op(v.tensor_reduce(nch[:, :], cmpc[:, :, :], AX.X, ALU.add))
                op(v.memset(cb[:, 0:1], 0.0))
                for e in range(1, E):
                    op(v.tensor_tensor(cb[:, e:e + 1], cb[:, e - 1:e], nch[:, e - 1:e], ALU.add))
                op(v.tensor_scalar(base[:, :], cb[:, :], float(CH), None, ALU.mult))
                op(v.tensor_tensor(ciE[:, :, :], cf[:, :].unsqueeze(2).broadcast_to([1, NC, E]),
                                   cb[0:1, :].unsqueeze(1).broadcast_to([1, NC, E]), ALU.is_ge))
                op(v.tensor_reduce(tf[:, 0:NC], ciE[:, :, 1:E], AX.X, ALU.add))
                op(v.memset(tf[:, NC:NC + 1], 0.0))
                op(v.tensor_copy(table[:, :], tf[:, :]))
                v.wait_ge(s_rk, 2)
                op(v.tensor_copy(flag[:, :], psY[1][0:1, 0:1]))
                v.sem_inc(s_tab, 1)
            else:
                op(v.tensor_scalar(base[:, :], iexp[:, :], float(CAP), None, ALU.mult))
            op(v.tensor_tensor(tot[:, :, :], off[:, :, :], along(base), ALU.add))
            for q, oh in enumerate((oh1, oh2)):
                op(v.tensor_tensor(eq[:, :, :], oh[:, :, :], tot[:, :, :], ALU.mult))
                op(v.tensor_reduce(pos[:, q, :], eq[:, :, :], AX.X, ALU.add))
                op(v.tensor_tensor(eq[:, :, :], oh[:, :, :], wgt[:, :, :], ALU.mult))
                op(v.tensor_reduce(wk[:, q, :], eq[:, :, :], AX.X, ALU.add))
                if not layer:
                    op(v.tensor_tensor(eq[:, :, :], oh[:, :, :], off[:, :, :], ALU.mult))
                    op(v.tensor_reduce(f1[:, :], eq[:, :, :], AX.X, ALU.add))
                    op(v.tensor_scalar(vd[:, q, :], f1[:, :], float(CAP), None, ALU.is_lt))
            if not layer:
                op(v.tensor_tensor(wk[:, :, :], wk[:, :, :], vd[:, :, :], ALU.mult))
                op(v.tensor_tensor(pos[:, :, :], pos[:, :, :], vd[:, :, :], ALU.mult))
                op(v.tensor_copy(gidx[:, :, :], pos[:, :, :]))
                op(v.tensor_scalar(vd[:, :, :], vd[:, :, :], -1.0, 1.0, ALU.mult, ALU.add))
                op(v.tensor_tensor(dump[:, :, :], dump[:, :, :], vd[:, :, :], ALU.mult))
                op(v.tensor_tensor(pos[:, :, :], pos[:, :, :], dump[:, :, :], ALU.add))
                op(v.tensor_copy(sidx[:, :, :], pos[:, :, :]))
            else:
                op(v.tensor_copy(gidx[:, :, :], pos[:, :, :]))
                op(v.tensor_copy(sidx[:, :, :], pos[:, :, :]))
            v.sem_inc(s_idx, 1)
            with v.Fori(0, EARLY) as e:
                for q in range(PIECES):
                    split_low(v, e, q)
            nq = NT // 4 if layer else 0
            for q in range(nq):
                v.wait_ge(s_wtP, q + 1)
                v.tensor_copy(wt[:, 4 * q:4 * q + 4, :].rearrange("e t p -> e (t p)"),
                              psH[q % 2][0:E, :]).then_inc(s_wtF, 1)
            for t in range(NT):
                v.wait_ge(s_wtP, nq + t + 1)
                v.tensor_tensor(X[:, t, :], X[:, t, :], psY[t % 4][:, 0:D], ALU.add).then_inc(s_wtF, 1)

            def take_rows(m, p):
                def take(n):
                    v.wait_ge(main.ys[p], m * 16 + 16)
                    for it in range(IT):
                        ins = v.tensor_scalar(yb[:, p, it, :], psY[p * IT + it][:, 0:D], 1.0 / WS, None, ALU.mult)
                    ins.then_inc(main.yF, 1)
                return take

            def bias_of(experts_of, c, m, p):
                def load():
                    e = v.value_load(experts_of[0:1, bass.ds(c, 1)], min_val=0, max_val=E - 1)
                    dve_bias(v, main, m, p, e)
                return load

            dve_turn(v, main, 0, 0)
            if layer:
                dve_bias(v, main, 0, 0, 0, wait=False)
            for first, last, splits in ((0, (E - EARLY) // 2, True), ((E - EARLY) // 2, NC // 2, False)):
                with v.Fori(first, last) as m:
                    for p in range(2):
                        dve_chunk(v, main, m, p, take_rows(m, p), splits, bias_of(table, m * 2 + p + 1, m + p, 1 - p))
            for i in range(2 * NT):
                t, q = i // 2, i % 2
                v.wait_ge(s_gy[i % GR], 16 * (i // GR + 1))
                v.wait_ge(s_wtF, nq + NT) if i == 0 else v.wait_ge(s_gu, i)
                v.scalar_tensor_tensor(X[:, t, :], gy[:, i % GR, :], wk[:, q, t:t + 1], X[:, t, :], ALU.mult,
                                       ALU.add).then_inc(s_gu, 1)
            v.wait_ge(s_gu, 2 * NT)
            if layer:
                def take_ties(e, c, p):
                    def take(n):
                        v.wait_ge(main.yF, n + 2)
                        for it in range(IT):
                            t = (c * 2 + p) * IT + it
                            xs = X[:, bass.ds(t, 1), :].rearrange("p a c -> p (a c)")
                            w = sc[:, bass.ds(t, 1), :].rearrange("p a e -> p (a e)")[:, bass.ds(e, 1)]
                            ins = v.scalar_tensor_tensor(xs, psY[p * IT + it][:, 0:D], w, xs, ALU.mult, ALU.add)
                        ins.then_inc(main.yF, 1)
                    return take

                found = v.value_load(flag[0:1, 0:1], min_val=0, max_val=T * E)
                with v.If(found > 0):
                    with v.Fori(0, E) as e:
                        with v.Fori(0, TC // 2) as c:
                            for p in range(2):
                                m = e * (TC // 2) + c
                                dve_chunk(v, main, m + NC // 2, p, take_ties(e, c, p), False,
                                          bias_of(tie_e, m * 2 + p + 1, m + p + NC // 2, 1 - p))
                    v.wait_ge(main.yF, NC + NTIE + 2)


def attention1(nc, X, identf, io):
    H, DH = 8, 32
    G = H * DH // P
    HG = H // G
    JT, JR = MT, MR
    KCH = chunks(M)
    NCK = len(KCH)
    NQ = KC * NT // 4 + G * B
    NGC = KC * -(-JT // 4)
    NW = NGC + G * NCK + JT
    NA = 1 + ST * (NCK - 1)
    SCALE = DH ** -0.5
    KR = 3 * DH + 1
    VC = 2 * DH + 1
    LAG = 5
    PR = ring(JT, 7)
    SR = ring(JT, 4)
    R, NS = max(PR) + 1, max(SR) + 1
    VT = [2, 6, 10]
    GT = [j for j in range(JT) if j not in VT]

    with ExitStack() as ctx:
        def sb(name, shape, dt=F32):
            return ctx.enter_context(nc.sbuf_tensor("c_" + name, shape, dt))

        def sem(name):
            return ctx.enter_context(nc.semaphore("c_" + name))

        wf = sb("wf", [P, 3, G, D])
        wth, wtl = sb("wth", [P, 3, KC, D], F16), sb("wtl", [P, 3, KC, D], F16)
        st, mv = sb("st", [P, NT, 6]), sb("mv", [P, NT, 2])
        ve, mhalf, rstd = sb("ve", [P, NT]), sb("mhalf", [P, NT]), sb("rstd", [P, NT])
        qhs, qls = sb("qhs", [P, G, B * S], F16), sb("qls", [P, G, B * S], F16)
        qst = sb("qst", [P, H, B * S], F16)
        ltn = qst[:, 0:H // 2, :].rearrange("p h n -> p (h n)").bitcast(F32).rearrange("p (t c) -> p t c", c=D)
        lth = qst[:, H // 2:H // 2 + KC, :]
        ltl = qst[:, H // 2 + KC:H, :]
        kst = sb("kst", [P, H, M], F16)
        khs, kls = sb("khs", [P, G, M], F16), sb("kls", [P, G, M], F16)
        vst = sb("vst", [P, JT, H, VC], F16)
        cx = sb("cx", [P, JT, D])
        cth, ctl = sb("cth", [P, KC, M], F16), sb("ctl", [P, KC, M], F16)
        mx, mc = sb("mx", [P, ST, NCK]), sb("mc", [P, ST])
        pf = sb("pf", [P, R, S])
        ph, pl = sb("ph", [P, R, S], F16), sb("pl", [P, R, S], F16)
        of = sb("of", [VC, S])
        fold = sb("fold", [VC, DH + 1])
        rl = sb("rl", [P, ST])

        psA = [ctx.enter_context(nc.psum_tensor(f"c_psA{i}", [P, 512], F32)) for i in range(2)]
        psS = [ctx.enter_context(nc.psum_tensor(f"c_psS{i}", [P, 512], F32)) for i in range(NS)]
        psO = ctx.enter_context(nc.psum_tensor("c_psO", [P, 512], F32))
        psM = ctx.enter_context(nc.psum_tensor("c_psM", [P, 512], F32))
        ring4 = psA + psS[0:2]

        s_const = sem("const")
        s_w = sem("w")
        s_cx = sem("cx")
        s_st = sem("st")
        s_mv = sem("mv")
        s_pool = sem("pool")
        s_rstd = sem("rstd")
        s_nt = sem("nt")
        s_uP = sem("uP")
        s_uH = sem("uH")
        s_uL = sem("uL")
        s_q = sem("q")
        s_wP = sem("wP")
        s_wH = sem("wH")
        s_wL = sem("wL")
        s_k = sem("k")
        s_aP = sem("aP")
        s_aF = sem("aF")
        s_mc = sem("mc")
        s_mT = sem("mT")
        s_mr = sem("mr")
        s_sP = sem("sP")
        s_pF = sem("pF")
        s_pH = sem("pH")
        s_pL = sem("pL")
        s_pG = sem("pG")
        s_pv = sem("pv")
        s_oF = sem("oF")
        s_tP = sem("tP")
        s_rl = sem("rl")
        s_tF = sem("tF")

        block = ctx.enter_context(nc.Block(no_gpsimd_drain=True))
        NCONST = 6
        names = ("L1_xattn_Wq", "L1_xattn_Wk", "L1_xattn_Wv")

        def wait_low(eng, n, j):
            if j in VT:
                eng.wait_ge(s_pL, done(len(VT), n, VT.index(j)))
            else:
                eng.wait_ge(s_pG, done(len(GT), n, GT.index(j)))

        SLOTS = [[] for _ in range(JT)]
        for a in range(NA):
            SLOTS[a * 10 // NA].append(a)
        SLOTS[10].append("mc")
        SLOTS[11].append("mT")

        @block.sync
        def _(sp):
            for i, name in enumerate(names):
                sp.dma_start(wf[:, i, :, :], io[name].rearrange("(g p) c -> p g c", p=P)).then_inc(s_w, 16)
            def load_context(b):
                src = io["ctx_1024"][bass.ds(b, 1), :, :].rearrange("a m c -> (a m) c")
                sp.dma_start(cx[:, 0:MT - 1, :],
                             src[0:(MT - 1) * P, :].rearrange("(t p) c -> p t c", p=P)).then_inc(s_cx, 16)
                sp.dma_start(cx[0:MR, MT - 1, :], src[(MT - 1) * P:M, :]).then_inc(s_cx, 16)

            load_context(0)
            sp.wait_ge(s_uL, 3 + NQ)
            for h in range(H):
                r0 = (h % HG) * DH
                for piece, src in enumerate((qhs, qhs, qls)):
                    sp.dma_start(qst[piece * DH:(piece + 1) * DH, h, :], src[r0:r0 + DH, h // HG, :]).then_inc(s_q, 16)
            def stack_keys(b):
                for g in range(G):
                    sp.wait_ge(s_wL, done(NW, b, NGC + (g + 1) * NCK - 1))
                    for u in range(HG):
                        for piece, src in enumerate((khs, kls, khs)):
                            sp.dma_start(kst[piece * DH:(piece + 1) * DH, g * HG + u, :],
                                         src[u * DH:(u + 1) * DH, g, :]).then_inc(s_k, 16)

            with sp.Fori(0, B - 1) as b:
                stack_keys(b)
                sp.wait_ge(s_wP, done(NW, b, NGC - 1))
                load_context(b + 1)
            stack_keys(B - 1)

        @block.gpsimd
        def _(g):
            g.memset(mhalf[:, :], -0.5).then_inc(s_const, 1)
            g.wait_ge(s_const, 1)
            g.wait_ge(s_mv, 1)
            g.tensor_scalar(ve[:, :], mv[:, :, 1], EPS, None, ALU.add).then_inc(s_pool, 1)
            g.wait_ge(s_pool, 1)
            g.tensor_tensor(rstd[:, :], ve[:, :], mhalf[:, :], ALU.pow).then_inc(s_rstd, 1)
            g.wait_ge(s_rstd, 1)
            for i, (t, val) in enumerate(((kst[3 * DH:KR, :, :], 1.0), (vst[:, :, :, 2 * DH:VC], WS),
                                          (fold[:, :], 0.0), (fold[2 * DH:VC, DH:DH + 1], 1.0))):
                g.memset(t, val).then_inc(s_const, 1)
                g.wait_ge(s_const, i + 2)
            g.affine_select(out=fold[0:2 * DH, 0:DH], in_=fold[0:2 * DH, 0:DH], compare_op=ALU.not_equal, fill=1.0,
                            base=0, pattern=[[-1, DH]], channel_multiplier=1).then_inc(s_pool, 1)
            g.wait_ge(s_pool, 2)
            g.affine_select(out=fold[0:2 * DH, 0:DH], in_=fold[0:2 * DH, 0:DH], compare_op=ALU.not_equal, fill=1.0,
                            base=-DH, pattern=[[-1, DH]], channel_multiplier=1).then_inc(s_pool, 1)
            g.wait_ge(s_pool, 3)
            g.sem_inc(s_const, 1)
            g.sem_inc(s_pG, len(GT))
            with g.Fori(0, B * H) as n:
                for j in GT:
                    r = rows(j, JT, JR)
                    dn, pj = before(PR, j)
                    g.wait_ge(s_pH, done(JT, n, j))
                    g.wait_ge(s_pv, done(JT, n + dn, pj))
                    g.tensor_tensor(pl[0:r, PR[j], :], pf[0:r, PR[j], :], ph[0:r, PR[j], :],
                                    ALU.subtract).then_inc(s_pG, 1)

        @block.scalar
        def _(act):
            act.sem_inc(s_wH, NW)
            act.sem_inc(s_pF, JT)
            act.sem_inc(s_pH, JT)
            act.sem_inc(s_oF, 1)
            for i in range(3 + NQ):
                act.wait_ge(s_uP, i + 1)
                ps = ring4[i % 4]
                if i < 3:
                    act.activation(wth[:, i, :, :].rearrange("p k n -> p (k n)"), ps[:, :], ACT.Copy,
                                   scale=WS).then_inc(s_uH, 1)
                elif i < 3 + KC * NT // 4:
                    k, q = (i - 3) % KC, (i - 3) // KC
                    act.activation(lth[:, k, q * 512:q * 512 + 512], ps[:, :], ACT.Copy).then_inc(s_uH, 1)
                else:
                    u = i - 3 - KC * NT // 4
                    g, b = u % G, u // G
                    act.activation(qhs[:, g, b * S:(b + 1) * S], ps[:, :], ACT.Copy, scale=1.0 / WS).then_inc(s_uH, 1)
            with act.Fori(0, B) as b:
                for i in range(NW):
                    act.wait_ge(s_wP, done(NW, b, i))
                    ps = ring4[i % 4]
                    if i < NGC:
                        k, q = i % KC, i // KC
                        n = min(512, M - q * 512)
                        act.activation(cth[:, k, q * 512:q * 512 + n], ps[:, 0:n], ACT.Copy).then_inc(s_wH, 1)
                    elif i < NGC + G * NCK:
                        g, c = divmod(i - NGC, NCK)
                        c0, cn = KCH[c]
                        act.activation(khs[:, g, c0:c0 + cn], ps[:, 0:cn], ACT.Copy, scale=1.0 / WS).then_inc(s_wH, 1)
                    else:
                        j = i - NGC - G * NCK
                        r = rows(j, JT, JR)
                        act.activation(vst[0:r, j, :, 0:DH], ps[0:r, 0:D].rearrange("p (h d) -> p h d", d=DH),
                                       ACT.Copy).then_inc(s_wH, 1)

                def out_copy(n):
                    act.wait_ge(s_pv, done(JT, n, JT - 1))
                    act.wait_ge(s_tP, done(1, n, 0) - 1)
                    act.activation(of[:, :], psO[0:VC, :], ACT.Copy).then_inc(s_oF, 1)

                def main(h, with_tail):
                    n = b * H + h
                    for j in range(JT):
                        r = rows(j, JT, JR)
                        dn, pj = before(PR, j)
                        if with_tail and j == LAG:
                            out_copy(n - 1)
                        act.wait_ge(s_sP, done(JT, n, j))
                        wait_low(act, n + dn, pj)
                        act.activation(pf[0:r, PR[j], :], psS[SR[j]][0:r, :], ACT.Exp, scale=SCALE).then_inc(s_pF, 1)
                        act.wait_ge(s_pv, done(JT, n + dn, pj))
                        act.activation(ph[0:r, PR[j], :], psS[SR[j]][0:r, :], ACT.Exp, scale=SCALE).then_inc(s_pH, 1)

                main(b * 0, False)
                with act.Fori(1, H) as h:
                    main(h, True)
                out_copy(b * H + (H - 1))

        @block.tensor
        def _(pe):
            pe.sem_inc(s_wP, NW)
            pe.sem_inc(s_aP, NA)
            pe.sem_inc(s_mT, 1)
            pe.sem_inc(s_sP, JT)
            pe.sem_inc(s_pv, JT)
            pe.sem_inc(s_tP, 1)

            def triple(out, hi, lo, xh_, xl_, first=True, last=True):
                pe.matmul(out, hi, xh_, start=first, stop=False)
                pe.matmul(out, hi, xl_, start=False, stop=False)
                return pe.matmul(out, lo, xh_, start=False, stop=last)

            pe.wait_ge(s_w, 48)
            for i in range(3 + NQ):
                ps = ring4[i % 4]
                if i >= 4:
                    pe.wait_ge(s_uL, i - 3)
                if i < 3:
                    for k in range(KC):
                        for g in range(G):
                            o = (k * G + g) * P
                            ins = pe.transpose(ps[:, o:o + P], wf[:, i, g, k * P:(k + 1) * P], identf[:, :])
                elif i < 3 + KC * NT // 4:
                    k, q = (i - 3) % KC, (i - 3) // KC
                    pe.wait_ge(s_nt, 4 * q + 4)
                    for u in range(4):
                        ins = pe.transpose(ps[:, u * P:(u + 1) * P], ltn[:, 4 * q + u, k * P:(k + 1) * P],
                                           identf[:, :])
                else:
                    u = i - 3 - KC * NT // 4
                    g, b = u % G, u // G
                    if u == 0:
                        pe.wait_ge(s_uL, 3 + KC * NT // 4)
                    ts = slice(b * S, (b + 1) * S)
                    for k in range(KC):
                        ws = slice(g * P, (g + 1) * P)
                        ins = triple(ps[:, :], wth[:, 0, k, ws], wtl[:, 0, k, ws], lth[:, k, ts], ltl[:, k, ts],
                                     k == 0, k == KC - 1)
                ins.then_inc(s_uP, 1)
            pe.wait_ge(s_uL, 3 + NQ)
            pe.wait_ge(s_const, NCONST)

            with pe.Fori(0, B) as b:
                for i in range(NW):
                    ps = ring4[i % 4]
                    if i < 4:
                        if i == 0:
                            pe.wait_ge(s_aF, (b * H) * NA + NA)
                            pe.wait_ge(s_pH, (b * H) * JT + JT)
                            pe.wait_ge(s_cx, b * 32 + 32)
                    else:
                        pe.wait_ge(s_wL, done(NW, b, NGC - 1 if i == NGC else i - 4))
                    if i < NGC:
                        k, q = i % KC, i // KC
                        for u in range(4):
                            tl = q * 4 + u
                            if tl >= JT:
                                break
                            r = rows(tl, JT, JR)
                            ins = pe.transpose(ps[:, u * P:u * P + r], cx[0:r, tl, k * P:(k + 1) * P],
                                               identf[0:r, 0:r])
                    elif i < NGC + G * NCK:
                        g, c = divmod(i - NGC, NCK)
                        c0, cn = KCH[c]
                        for k in range(KC):
                            ws = slice(g * P, (g + 1) * P)
                            ins = triple(ps[:, 0:cn], wth[:, 1, k, ws], wtl[:, 1, k, ws], cth[:, k, c0:c0 + cn],
                                         ctl[:, k, c0:c0 + cn], k == 0, k == KC - 1)
                    else:
                        j = i - NGC - G * NCK
                        r = rows(j, JT, JR)
                        js = slice(j * P, j * P + r)
                        for k in range(KC):
                            ins = triple(ps[0:r, 0:D], cth[:, k, js], ctl[:, k, js], wth[:, 2, k, :], wtl[:, 2, k, :],
                                         k == 0, k == KC - 1)
                    ins.then_inc(s_wP, 1)

                def head(t, h, cs, r=P):
                    return t[0:r, bass.ds(h, 1), cs].rearrange("p a n -> p (a n)")

                def pre(n, h, what, first=False):
                    if what == "mc":
                        return
                    if what == "mT":
                        pe.wait_ge(s_mc, done(1, n, 0))
                        pe.wait_ge(s_tF, done(1, n, 0) - (0 if first else 1))
                        for it in range(ST):
                            ins = pe.transpose(psM[0:1, it * P:(it + 1) * P], mc[:, it:it + 1], identf[:, :])
                        ins.then_inc(s_mT, 1)
                        return
                    a = what
                    pe.wait_ge(s_aF, done(NA, n, a - 2 if a != 0 else -1))
                    if a == 0:
                        for it in range(ST):
                            c0, cn = KCH[-1]
                            ins = pe.matmul(psA[0][:, it * cn:(it + 1) * cn],
                                            head(qst, h, bass.ds(b * S + it * P, P), KR - 1),
                                            head(kst, h, slice(c0, c0 + cn), KR - 1), start=True, stop=True)
                        ins.then_inc(s_aP, 1)
                        return
                    it, c = divmod(a - 1, NCK - 1)
                    c0, cn = KCH[c]
                    pe.matmul(psA[a % 2][:, 0:cn], head(qst, h, bass.ds(b * S + it * P, P), KR - 1),
                              head(kst, h, slice(c0, c0 + cn), KR - 1), start=True, stop=True).then_inc(s_aP, 1)

                def pv(n, h, j):
                    r = rows(j, JT, JR)
                    w = vst[0:r, j, bass.ds(h, 1), :].rearrange("p a n -> p (a n)")
                    pe.wait_ge(s_pH, done(JT, n, j))
                    if j == 0:
                        pe.wait_ge(s_oF, done(1, n, 0) - 1)
                    pe.matmul(psO[0:VC, :], w, ph[0:r, PR[j], :], start=(j == 0), stop=False)
                    wait_low(pe, n, j)
                    pe.matmul(psO[0:VC, :], w, pl[0:r, PR[j], :], start=False, stop=(j == JT - 1)).then_inc(s_pv, 1)

                def tail(n, last=False):
                    pe.wait_ge(s_oF, done(1, n, 0))
                    if last:
                        pe.wait_ge(s_tF, done(1, n, 0))
                    else:
                        pe.wait_ge(s_mr, done(1, n, 0) + 1)
                    for it in range(ST):
                        ins = pe.matmul(psM[:, it * (DH + 1):(it + 1) * (DH + 1)], of[:, it * P:(it + 1) * P],
                                        fold[:, :], start=True, stop=True)
                    ins.then_inc(s_tP, 1)

                def main(h, with_pre, with_tail):
                    n = b * H + h
                    for j in range(JT):
                        r = rows(j, JT, JR)
                        dn, pj = before(SR, j)
                        pe.wait_ge(s_pH, done(JT, n + dn, pj))
                        if j == 0:
                            pe.wait_ge(s_mr, done(1, n, 0))
                        pe.matmul(psS[SR[j]][0:r, :], head(kst, h, slice(j * P, j * P + r), KR),
                                  head(qst, h, bass.ds(b * S, S), KR), start=True, stop=True).then_inc(s_sP, 1)
                        if with_pre:
                            for what in SLOTS[j]:
                                pre(n + 1, h + 1, what)
                        if j >= LAG:
                            pv(n, h, j - LAG)
                        elif with_tail:
                            pv(n - 1, h - 1, JT - LAG + j)
                        if with_tail and j == LAG + 1:
                            tail(n - 1)

                pe.wait_ge(s_wL, done(NW, b, NW - 1))
                pe.wait_ge(s_k, (b + 1) * (3 * H * 16))
                pe.wait_ge(s_q, 3 * H * 16)
                for what in sum(SLOTS, []):
                    pre(b * H, b * 0, what, True)
                main(b * 0, True, False)
                with pe.Fori(1, H - 1) as h:
                    main(h, True, True)
                main(b * 0 + (H - 1), False, True)
                for j in range(JT - LAG, JT):
                    pv(b * H + (H - 1), b * 0 + (H - 1), j)
                tail(b * H + (H - 1), True)

        @block.vector
        def _(v):
            v.sem_inc(s_wL, NW)
            v.sem_inc(s_aF, NA)
            v.sem_inc(s_mc, 1)
            v.sem_inc(s_mr, 1)
            v.sem_inc(s_pL, len(VT))
            v.sem_inc(s_rl, 1)
            v.sem_inc(s_tF, 2)
            ch = Chain(v, s_st)
            for t in range(NT):
                ch.step(v.bn_stats(st[:, t, :], X[:, t, :]))
            ch.wait()
            for t in range(NT):
                ch.step(v.bn_aggr(mv[:, t, :], st[:, t, :]))
            ch.wait()
            v.sem_inc(s_mv, 1)
            v.wait_ge(s_rstd, 1)
            for t in range(NT):
                v.tensor_scalar(ltn[:, t, :], X[:, t, :], mv[:, t, 0:1], rstd[:, t:t + 1], ALU.subtract,
                                ALU.mult).then_inc(s_nt, 1)
            for i in range(3 + NQ):
                ps = ring4[i % 4]
                v.wait_ge(s_uH, i + 1)
                if i < 3:
                    v.scalar_tensor_tensor(wtl[:, i, :, :].rearrange("p k n -> p (k n)"), ps[:, :], WS,
                                           wth[:, i, :, :].rearrange("p k n -> p (k n)"), ALU.mult,
                                           ALU.subtract).then_inc(s_uL, 1)
                elif i < 3 + KC * NT // 4:
                    k, q = (i - 3) % KC, (i - 3) // KC
                    cs = slice(q * 512, q * 512 + 512)
                    v.tensor_tensor(ltl[:, k, cs], ps[:, :], lth[:, k, cs], ALU.subtract).then_inc(s_uL, 1)
                else:
                    u = i - 3 - KC * NT // 4
                    g, b = u % G, u // G
                    cs = slice(b * S, (b + 1) * S)
                    v.scalar_tensor_tensor(qls[:, g, cs], ps[:, :], 1.0 / WS, qhs[:, g, cs], ALU.mult,
                                           ALU.subtract).then_inc(s_uL, 1)
            with v.Fori(0, B) as b:
                for i in range(NW):
                    v.wait_ge(s_wH, done(NW, b, i))
                    ps = ring4[i % 4]
                    if i < NGC:
                        k, q = i % KC, i // KC
                        n = min(512, M - q * 512)
                        cs = slice(q * 512, q * 512 + n)
                        v.tensor_tensor(ctl[:, k, cs], ps[:, 0:n], cth[:, k, cs], ALU.subtract).then_inc(s_wL, 1)
                    elif i < NGC + G * NCK:
                        g, c = divmod(i - NGC, NCK)
                        c0, cn = KCH[c]
                        v.scalar_tensor_tensor(kls[:, g, c0:c0 + cn], ps[:, 0:cn], 1.0 / WS, khs[:, g, c0:c0 + cn],
                                               ALU.mult, ALU.subtract).then_inc(s_wL, 1)
                    else:
                        j = i - NGC - G * NCK
                        r = rows(j, JT, JR)
                        v.tensor_tensor(vst[0:r, j, :, DH:2 * DH], ps[0:r, 0:D].rearrange("p (h d) -> p h d", d=DH),
                                        vst[0:r, j, :, 0:DH], ALU.subtract).then_inc(s_wL, 1)

                def pre(n, h, what):
                    if what == "mc":
                        v.wait_ge(s_aF, done(NA, n, NA - 1))
                        v.tensor_reduce(mc[:, :], mx[:, :, :], AX.X, ALU.max).then_inc(s_mc, 1)
                        return
                    if what == "mT":
                        v.wait_ge(s_mT, done(1, n, 0))
                        v.tensor_scalar(qst[KR - 1:KR, bass.ds(h, 1), bass.ds(b * S, S)].rearrange("p a n -> p (a n)"),
                                        psM[0:1, :], -1.0, None, ALU.mult).then_inc(s_mr, 1)
                        return
                    v.wait_ge(s_aP, done(NA, n, what))
                    if what == 0:
                        cn = KCH[-1][1]
                        v.tensor_reduce(mx[:, :, NCK - 1], psA[0][:, 0:ST * cn].rearrange("p (t n) -> p t n", n=cn), AX.X,
                                        ALU.max).then_inc(s_aF, 1)
                        return
                    it, c = divmod(what - 1, NCK - 1)
                    c0, cn = KCH[c]
                    v.tensor_reduce(mx[:, it, c:c + 1], psA[what % 2][:, 0:cn], AX.X, ALU.max).then_inc(s_aF, 1)

                def tail(n, h):
                    v.wait_ge(s_tP, done(1, n, 0))
                    pt = psM[:, 0:ST * (DH + 1)].rearrange("p (t n) -> p t n", n=DH + 1)
                    v.reciprocal(rl[:, :], pt[:, :, DH]).then_inc(s_rl, 1)
                    v.wait_ge(s_rl, done(1, n, 0))
                    for it in range(ST):
                        xs = X[:, bass.ds(b * ST + it, 1), bass.ds(h * DH, DH)].rearrange("p a c -> p (a c)")
                        ins = v.scalar_tensor_tensor(xs, pt[:, it, 0:DH], rl[:, it:it + 1], xs, ALU.mult, ALU.add)
                    ins.then_inc(s_tF, 1)

                def main(h, with_pre, with_tail):
                    n = b * H + h
                    for slot in range(JT):
                        j = slot - 2
                        if j in VT:
                            r = rows(j, JT, JR)
                            dn, pj = before(PR, j)
                            v.wait_ge(s_pH, done(JT, n, j))
                            v.wait_ge(s_pv, done(JT, n + dn, pj))
                            v.tensor_tensor(pl[0:r, PR[j], :], pf[0:r, PR[j], :], ph[0:r, PR[j], :],
                                            ALU.subtract).then_inc(s_pL, 1)
                        if with_pre:
                            for what in SLOTS[slot]:
                                pre(n + 1, h + 1, what)
                        if with_tail and slot == LAG + 2:
                            tail(n - 1, h - 1)

                for what in sum(SLOTS, []):
                    pre(b * H, b * 0, what)
                main(b * 0, True, False)
                with v.Fori(1, H - 1) as h:
                    main(h, True, True)
                main(b * 0 + (H - 1), False, True)
                tail(b * H + (H - 1), b * 0 + (H - 1))
            v.wait_ge(s_tF, B * H + 2)


def build(nc, io, out, phases):
    with ExitStack() as ctx:
        X = ctx.enter_context(nc.sbuf_tensor("X", [P, NT, D], F32))
        identf = ctx.enter_context(nc.sbuf_tensor("identf", [P, P], F32))
        s_id = ctx.enter_context(nc.semaphore("s_id"))
        s_out = ctx.enter_context(nc.semaphore("s_out"))
        s_x = ctx.enter_context(nc.semaphore("s_x"))
        with nc.Block(no_gpsimd_drain=True) as block:
            @block.sync
            def _(sp):
                sp.dma_start(X[:, :, :], io["x"].rearrange("b (t p) c -> p (b t) c", p=P)).then_inc(s_x, 16)
                sp.wait_ge(s_x, 16)

            @block.gpsimd
            def _(g):
                g.memset(identf[:, :], 0.0).then_inc(s_id, 1)
                g.wait_ge(s_id, 1)
                g.affine_select(out=identf[:, :], in_=identf[:, :], compare_op=ALU.not_equal, fill=1.0, base=0,
                                pattern=[[-1, P]], channel_multiplier=1).then_inc(s_id, 1)
                g.wait_ge(s_id, 2)
        if "A" in phases:
            attention0(nc, X, identf, io)
        if "B" in phases:
            experts(nc, X, identf, io, 0)
        if "C" in phases:
            attention1(nc, X, identf, io)
        if "D" in phases:
            experts(nc, X, identf, io, 1)
        with nc.Block(no_gpsimd_drain=True) as block:
            @block.sync
            def _(sp):
                sp.dma_start(out.rearrange("b (t p) c -> p (b t) c", p=P), X[:, :, :]).then_inc(s_out, 16)
                sp.wait_ge(s_out, 16)


PHASES = "ABCD"
_INS = ['x', 'ctx_1024', 'L0_xattn_gamma_media', 'L0_xattn_beta_media', 'L0_xattn_gamma_lat', 'L0_xattn_beta_lat',
        'L0_xattn_Wq', 'L0_xattn_bq', 'L0_xattn_Wkv', 'L0_xattn_bkv', 'L0_xattn_Wo', 'L0_xattn_bo',
        'L0_ffn_w_router', 'L0_ffn_w1', 'L0_ffn_w2', 'L0_ffn_bias', 'L1_xattn_Wq', 'L1_xattn_Wk', 'L1_xattn_Wv',
        'L1_ffn_W1', 'L1_ffn_b1', 'L1_ffn_W2', 'L1_ffn_b2', 'L1_ffn_Wr', 'L1_ffn_br']


def kernel(**inputs):
    import numpy as np
    import concourse.bacc as bacc
    from concourse.bass_utils import run_bass_kernel_spmd

    nc = bacc.Bacc("TRN2", target_bir_lowering=False, num_devices=1)
    arrays, io = {}, {}
    for name in _INS:
        a = np.ascontiguousarray(inputs[name])
        arrays[f"in_{name}"] = a
        io[name] = nc.dram_tensor(f"in_{name}", a.shape, F32, kind="ExternalInput").ap()
    out = nc.dram_tensor("out_0", (B, S, D), F32, kind="ExternalOutput").ap()
    build(nc, io, out, PHASES)
    r = run_bass_kernel_spmd(nc, [arrays], core_ids=[0])
    return r.results[0]["out_0"]
```

```python
from contextlib import ExitStack

import concourse.bass as bass
from concourse import mybir

F32 = mybir.dt.float32
F16 = mybir.dt.float16
BF16 = mybir.dt.bfloat16
ALU = mybir.AluOpType
ACT = mybir.ActivationFunctionType
AX = mybir.AxisListType

P = 128
B, S, D = 4, 512, 256
M = 1601
KC = D // P
NT = B * S // P
ST = S // P
MT = -(-M // P)
MR = M - (MT - 1) * P
WS = 16.0
EPS = 1e-5

H0, DH0 = 8, 128
J0 = S + M
JT0 = -(-J0 // P)
JR0 = J0 - (JT0 - 1) * P
INNER = H0 * DH0


def done(per, n, k):
    return (n + 1) * per + k + 1


def rows(j, tiles, last):
    return last if j == tiles - 1 else P


class Chain:

    def __init__(self, eng, sem, base=0, ):
        self.eng, self.sem, self.count, self.base = eng, sem, 0, base

    def step(self, ins):
        ins.then_inc(self.sem, 1)
        self.count += 1

    def wait(self):
        self.eng.wait_ge(self.sem, self.base + self.count)


def chunks(total, size=512):
    return [(o, min(size, total - o)) for o in range(0, total, size)]


def ring(tiles, size):
    out = [j % size for j in range(tiles)]
    if tiles % size == 1:
        out[-1] = size - 2
    return out


def before(slots, j):
    same = [q for q in range(j) if slots[q] == slots[j]]
    return (0, same[-1]) if same else (-1, max(q for q in range(len(slots)) if slots[q] == slots[j]))


def attention0(nc, X, identf, io):
    KCH = chunks(J0)
    NA = 1 + len(KCH) + ST * len(KCH)
    NG = KC * -(-JT0 // 4)
    NV = JT0 * INNER // 512
    NW = NG + NV
    SCALE = DH0 ** -0.5 / (WS * WS)
    LAG = 2
    PR = ring(JT0, 5)
    SR = ring(JT0, 3)
    R, NS = max(PR) + 1, max(SR) + 1
    TAIL = [LAG + 1, LAG + 2, LAG + 4]

    with ExitStack() as ctx:
        def sb(name, shape, dt):
            return ctx.enter_context(nc.sbuf_tensor("a_" + name, shape, dt))

        def pb(name, shape, dt=F32):
            return ctx.enter_context(nc.psum_tensor("a_" + name, shape, dt))

        used = []

        def sem(name):
            used.append(ctx.enter_context(nc.semaphore("a_" + name)))
            return used[-1]

        wqh, wql = sb("wqh", [P, KC, INNER], F16), sb("wql", [P, KC, INNER], F16)
        wkvh, wkvl = sb("wkvh", [P, KC, 2 * INNER], F16), sb("wkvl", [P, KC, 2 * INNER], F16)
        woh, wol = sb("woh", [P, H0, D], F16), sb("wol", [P, H0, D], F16)
        vh, vl = sb("vh", [P, JT0, INNER], F16), sb("vl", [P, JT0, INNER], F16)
        stage_a = vh[:, 0:16, :].rearrange("p a b -> p (a b)").bitcast(F32)
        stage_b = vl[:, 0:16, :].rearrange("p a b -> p (a b)").bitcast(F32)
        wq_f = stage_a[:, 0:2048].rearrange("p (k n) -> p k n", k=KC)
        wkv_f = stage_a[:, 2048:6144].rearrange("p (k n) -> p k n", k=KC)
        wo_f = stage_b[:, 0:2048].rearrange("p (h n) -> p h n", h=H0)
        xth, xtl = sb("xth", [P, KC, J0], F16), sb("xtl", [P, KC, J0], F16)
        cx = sb("cx", [P, MT, D], F32)
        lat = sb("lat", [P, ST, D], F32)
        st = sb("st", [P, MT + ST, 6], F32)
        mv = sb("mv", [P, MT + ST, 2], F32)
        mhalf = sb("mhalf", [P, MT + ST], F32)
        rstd = sb("rstd", [P, MT + ST], F32)
        ve = sb("ve", [P, MT + ST], F32)
        tmp = sb("tmp", [P, 512], F32)
        gm, bm, gl, bl = (sb(n, [P, KC], F32) for n in ("gm", "bm", "gl", "bl"))
        bq, bkv = sb("bq", [P, H0], F32), sb("bkv", [P, 2 * H0], F32)
        bo = sb("bo", [1, D], F32)
        qh, ql = sb("qh", [P, 2, S], F16), sb("ql", [P, 2, S], F16)
        kh, kl = sb("kh", [P, 2, J0], F16), sb("kl", [P, 2, J0], F16)
        mx = sb("mx", [P, 2, ST, len(KCH)], F32)
        mc = sb("mc", [P, 2, ST], F32)
        mrow = sb("mrow", [1, 2, S], BF16)
        oneb = sb("oneb", [1, P], BF16)
        onef = sb("onef", [P, P], F32)
        four = sb("four", [P, 1], F32)
        pf = sb("pf", [P, R, S], F32)
        ph, pl = sb("ph", [P, R, S], F16), sb("pl", [P, R, S], F16)
        acc = sb("acc", [P, 2, S], F32)
        oh, ol = sb("oh", [P, S], F16), sb("ol", [P, S], F16)
        rl = sb("rl", [P, 2, ST], F32)
        brow = sb("brow", [1, D], F32)
        bb = sb("bb", [P, D], F32)

        psA = [pb(f"psA{i}", [P, 512]) for i in range(2)]
        psS = [pb(f"psS{i}", [P, 512]) for i in range(NS)]
        psO = pb("psO", [P, 512])
        psW = pb("psW", [P, 2, D])
        psM = pb("psM", [P, 512])
        ring4 = psA + psS[0:2]

        s_const = sem("const")
        s_small = sem("small")
        s_w = sem("w")
        s_wh = sem("wh")
        s_wl = sem("wl")
        s_b16 = sem("b16")
        s_br = sem("br")
        s_brow = sem("brow")
        s_cx = sem("cx")
        s_st = sem("st")
        s_mv = sem("mv")
        s_pool = sem("pool")
        s_rstd = sem("rstd")
        s_nt = sem("nt")
        s_wP = sem("wP")
        s_wH = sem("wH")
        s_wt = sem("wt")
        s_wL = sem("wL")
        s_aP = sem("aP")
        s_aH = sem("aH")
        s_aF = sem("aF")
        s_mc = sem("mc")
        s_mT = sem("mT")
        s_mrow = sem("mrow")
        s_sP = sem("sP")
        s_pF = sem("pF")
        s_pH = sem("pH")
        s_pL = sem("pL")
        s_pv = sem("pv")
        s_acc = sem("acc")
        s_oH = sem("oH")
        s_oL = sem("oL")
        s_lP = sem("lP")
        s_rl = sem("rl")
        s_yP = sem("yP")
        s_yF = sem("yF")
        s_fin = sem("fin")

        def clear():
            with nc.Block(no_gpsimd_drain=True) as last:
                @last.gpsimd
                def _(g):
                    for one in used:
                        g.sem_clear(one)

        ctx.callback(clear)
        block = ctx.enter_context(nc.Block(no_gpsimd_drain=True))

        @block.sync
        def _(sp):
            def load_context(b):
                src = io["ctx_1024"][bass.ds(b, 1), :, :].rearrange("a m c -> (a m) c")
                sp.dma_start(cx[:, 0:MT - 1, :],
                             src[0:(MT - 1) * P, :].rearrange("(t p) c -> p t c", p=P)).then_inc(s_cx, 16)
                sp.dma_start(cx[0:MR, MT - 1, :], src[(MT - 1) * P:M, :]).then_inc(s_cx, 16)

            load_context(0)
            for name, t, k in (("L0_xattn_gamma_media", gm, KC), ("L0_xattn_beta_media", bm, KC),
                               ("L0_xattn_gamma_lat", gl, KC), ("L0_xattn_beta_lat", bl, KC),
                               ("L0_xattn_bq", bq, H0), ("L0_xattn_bkv", bkv, 2 * H0)):
                sp.dma_start(t[:, :], io[name].rearrange("(k p) -> p k", p=P),
                             allow_slow_non_contiguous=True).then_inc(s_small, 16)
            sp.dma_start(bo[:, :], io["L0_xattn_bo"].rearrange("(a n) -> a n", a=1)).then_inc(s_small, 16)
            with sp.Fori(1, B) as b:
                sp.wait_ge(s_wP, done(NW, b, -1) - NV)
                load_context(b)

        @block.gpsimd
        def _(g):
            for t, v in ((mhalf, -0.5), (onef, 1.0), (four, 4.0), (mv, 0.0), (oneb, 1.0)):
                g.memset(t[:], v).then_inc(s_const, 1)
            g.sem_inc(s_rstd, 3)
            g.sem_inc(s_acc, JT0)
            g.wait_ge(s_const, 5)
            sel = [(0, ST), (ST, ST + MT), (0, ST)]
            def rstds(b, which):
                for r in which:
                    lo, hi = sel[r]
                    g.wait_ge(s_mv, b * 3 + r + 1)
                    g.nop(nofuse=True)
                    g.tensor_scalar(ve[:, lo:hi], mv[:, lo:hi, 1], EPS, None, ALU.add).then_inc(s_pool, 1)
                    g.wait_ge(s_pool, b * 3 + r + 1)
                    g.tensor_tensor(rstd[:, lo:hi], ve[:, lo:hi], mhalf[:, lo:hi], ALU.pow).then_inc(s_rstd, 1)

            def batch(b, last):
                if not last:
                    rstds(b + 1, (0, 1))

                def sums(h, p):
                    n = b * H0 + h
                    for j in range(JT0):
                        k = rows(j, JT0, JR0)
                        g.wait_ge(s_pF, done(JT0, n, j))
                        if j == 0:
                            g.wait_ge(s_lP, done(1, n, 0) - 2)
                            g.nop(nofuse=True)
                            g.tensor_copy(acc[:, p, :], pf[:, PR[0], :]).then_inc(s_acc, 1)
                        else:
                            g.wait_ge(s_acc, done(JT0, n, j - 1))
                            g.tensor_tensor(acc[0:k, p, :], acc[0:k, p, :], pf[0:k, PR[j], :],
                                            ALU.add).then_inc(s_acc, 1)

                sums(0, 0)
                if not last:
                    rstds(b + 1, (2,))
                with g.Fori(0, 3) as t:
                    sums(t * 2 + 1, 1)
                    sums(t * 2 + 2, 0)
                sums(H0 - 1, 1)

            rstds(0, (0, 1, 2))
            with g.Fori(0, B - 1) as b:
                batch(b, False)
            batch(B - 1, True)

        def pre_slots():
            out = [[] for _ in range(JT0)]
            out[0] = ["A0", "A1"]
            out[1] = ["A2", "A3"]
            out[2] = ["A4", "A5"]
            for i in range(ST * len(KCH)):
                out[3 + i // 2].append(f"A{1 + len(KCH) + i}")
            out[13].append("mc")
            out[14].append("mT")
            return out

        SLOTS = pre_slots()
        NEXT = [[] for _ in range(JT0)]
        for i in range(NG):
            NEXT[i // 2].append(f"T{i}")
        for i in range(NA):
            NEXT[NG // 2 + 1 + i * (JT0 - NG // 2 - 1) // NA].append(f"A{i}")
        NEXT[-1] += ["mc", "mT"]
        NONE = [[] for _ in range(JT0)]

        @block.scalar
        def _(act):
            act.wait_ge(s_cx, 32)
            act.dma_start(wkv_f, io["L0_xattn_Wkv"].rearrange("(k p) n -> p k n", p=P)).then_inc(s_w, 16)
            act.dma_start(wq_f, io["L0_xattn_Wq"].rearrange("(k p) n -> p k n", p=P)).then_inc(s_w, 16)
            act.dma_start(wo_f, io["L0_xattn_Wo"].rearrange("(h p) n -> p h n", p=P)).then_inc(s_w, 16)
            act.sem_inc(s_wH, NW)
            act.sem_inc(s_aH, 1 + len(KCH))
            act.sem_inc(s_pF, JT0)
            act.sem_inc(s_pH, JT0)
            act.sem_inc(s_oH, 1)
            act.wait_ge(s_w, 48)
            act.wait_ge(s_small, 16 * 7)
            for hi, f in ((wkvh, wkv_f), (wqh, wq_f), (woh, wo_f)):
                act.activation(hi[:, :, :], f, ACT.Copy, scale=WS).then_inc(s_wh, 1)
            def turn(b, i):
                act.wait_ge(s_wP, done(NW, b, i))
                k, gidx = i % KC, i // KC
                c0 = gidx * 512
                n = min(512, J0 - c0)
                gg, be = (gl, bl) if gidx == 0 else (gm, bm)
                act.activation(xth[:, k, c0:c0 + n], psA[i % 2][:, 0:n], ACT.Identity,
                               bias=be[:, k:k + 1], scale=gg[:, k:k + 1]).then_inc(s_wH, 1)

            def value(b, i):
                act.wait_ge(s_wP, done(NW, b, i))
                j, half = (i - NG) // 2, (i - NG) % 2
                r = rows(j, JT0, JR0)
                act.activation(vh[0:r, j, half * 512:half * 512 + 512], ring4[i % 4][0:r, :],
                               ACT.Copy).then_inc(s_wH, 1)

            def pre(n, h, p, what, b=None):
                if what[0] == "T":
                    turn(b, int(what[1:]))
                if what[0] != "A":
                    return
                a = int(what[1:])
                if a > len(KCH):
                    return
                act.wait_ge(s_aP, done(NA, n, a))
                act.nop(nofuse=True)
                if a == 0:
                    act.activation(qh[:, p, :], psA[0][:, :], ACT.Identity,
                                   bias=bq[:, bass.ds(h, 1)]).then_inc(s_aH, 1)
                else:
                    c0, cn = KCH[a - 1]
                    act.activation(kh[:, p, c0:c0 + cn], psA[a % 2][:, 0:cn], ACT.Identity,
                                   bias=bkv[:, bass.ds(h, 1)]).then_inc(s_aH, 1)

            def batch(b, last):
                for i in range(NG, NW):
                    value(b, i)

                def out_hi(n):
                    act.wait_ge(s_pv, done(JT0, n, JT0 - 1))
                    act.wait_ge(s_yP, done(2, n, 1) - 2)
                    act.activation(oh[:, :], psO[:, :], ACT.Copy, scale=1.0 / 64).then_inc(s_oH, 1)

                def main(h, p, slots, with_tail):
                    n = b * H0 + h
                    for j in range(JT0):
                        r = rows(j, JT0, JR0)
                        dn, pj = before(PR, j)
                        if with_tail and j == LAG:
                            out_hi(n - 1)
                        act.wait_ge(s_sP, done(JT0, n, j))
                        act.wait_ge(s_pL, done(JT0, n + dn, pj))
                        act.wait_ge(s_acc, done(JT0, n + dn, pj))
                        act.activation(pf[0:r, PR[j], :], psS[SR[j]][0:r, :], ACT.Exp,
                                       scale=SCALE).then_inc(s_pF, 1)
                        act.wait_ge(s_pv, done(JT0, n + dn, pj))
                        act.activation(ph[0:r, PR[j], :], psS[SR[j]][0:r, :], ACT.Exp,
                                       scale=SCALE).then_inc(s_pH, 1)
                        for what in slots[j]:
                            pre(n + 1, 0 if slots is NEXT else h + 1, 1 - p, what, b + 1)

                main(0, 0, SLOTS, False)
                with act.Fori(0, 3) as t:
                    main(t * 2 + 1, 1, SLOTS, True)
                    main(t * 2 + 2, 0, SLOTS, True)
                main(H0 - 1, 1, NONE if last else NEXT, True)
                out_hi(b * H0 + (H0 - 1))

            for what in sum(NEXT, []):
                pre(0, 0, 0, what, 0)
            with act.Fori(0, B - 1) as b:
                batch(b, False)
            batch(B - 1, True)

        @block.tensor
        def _(pe):
            pe.sem_inc(s_wP, NW)
            pe.sem_inc(s_aP, NA)
            pe.sem_inc(s_mT, 1)
            pe.sem_inc(s_sP, JT0)
            pe.sem_inc(s_pv, JT0)
            pe.sem_inc(s_lP, 2)
            pe.sem_inc(s_yP, 2)
            pe.wait_ge(s_const, 5)
            pe.wait_ge(s_small, 16 * 7)
            pe.wait_ge(s_w, 48)
            for h in range(H0):
                pe.matmul(psM[0:1, 0:D], bkv[:, H0 + h:H0 + h + 1], wo_f[:, h, :], start=(h == 0), stop=False)
            pe.matmul(psM[0:1, 0:D], onef[0:1, 0:1], bo[:, :], start=False, stop=True).then_inc(s_br, 1)
            pe.wait_ge(s_brow, 1)
            pe.matmul(psM[:, 0:D], onef[0:1, :], brow[:, :], start=True, stop=True).then_inc(s_br, 1)
            pe.wait_ge(s_brow, 2)

            def triple(out, hi, lo, xh_, xl_, first=True, last=True):
                pe.matmul(out, hi, xh_, start=first, stop=False)
                pe.matmul(out, hi, xl_, start=False, stop=False)
                return pe.matmul(out, lo, xh_, start=False, stop=last)

            def turn(b, i):
                if i == 0:
                    pe.wait_ge(s_aF, (b * H0) * NA + NA)
                elif i >= 2:
                    pe.wait_ge(s_wL, done(NW, b, i - 2))
                k, gidx = i % KC, i // KC
                pe.wait_ge(s_nt, b * 2 + (1 if gidx == 0 else 2))
                for u in range(4):
                    tl = gidx * 4 + u
                    if tl >= JT0:
                        break
                    r = rows(tl, JT0, JR0)
                    src = lat[:, tl, :] if tl < ST else cx[0:r, tl - ST, :]
                    ins = pe.transpose(psA[i % 2][:, u * P:u * P + r], src[:, k * P:(k + 1) * P], identf[0:r, 0:r])
                ins.then_inc(s_wP, 1)

            def value(b, i):
                if i == NG:
                    pe.wait_ge(s_wl, 3)
                    pe.wait_ge(s_aF, done(NA, b * H0, NA - 1))
                    pe.wait_ge(s_pH, (b * H0) * JT0 + JT0)
                elif i >= NG + 4:
                    pe.wait_ge(s_wL, done(NW, b, i - 4))
                j, half = (i - NG) // 2, (i - NG) % 2
                r = rows(j, JT0, JR0)
                for k in range(KC):
                    cs = slice(j * P, j * P + r)
                    ws = slice(INNER + half * 512, INNER + half * 512 + 512)
                    ins = triple(ring4[i % 4][0:r, :], xth[:, k, cs], xtl[:, k, cs], wkvh[:, k, ws], wkvl[:, k, ws],
                                 k == 0, k == KC - 1)
                ins.then_inc(s_wP, 1)

            def pre(n, h, p, what, b=None):
                if what[0] == "T":
                    turn(b, int(what[1:]))
                    return
                if what == "mc":
                    return
                if what == "mT":
                    pe.wait_ge(s_mc, done(1, n, 0))
                    pe.wait_ge(s_rl, done(1, n, 0) - 2)
                    for it in range(ST):
                        ins = pe.transpose(psM[0:1, it * P:(it + 1) * P], mc[:, p, it:it + 1], identf[:, :])
                    ins.then_inc(s_mT, 1)
                    return
                a = int(what[1:])
                ps = psA[a % 2]
                pe.wait_ge(s_aF, done(NA, n, a - 2))
                if a == 0:
                    if isinstance(h, int) and h == 0:
                        pe.wait_ge(s_wL, done(NW, b, NG - 1))
                        pe.wait_ge(s_wl, 3)
                    for k in range(KC):
                        ws = bass.ds(h * DH0, DH0)
                        ins = triple(ps[:, 0:S], wqh[:, k, ws], wql[:, k, ws], xth[:, k, 0:S], xtl[:, k, 0:S],
                                     k == 0, k == KC - 1)
                elif a <= len(KCH):
                    c0, cn = KCH[a - 1]
                    for k in range(KC):
                        ws = bass.ds(h * DH0, DH0)
                        ins = triple(ps[:, 0:cn], wkvh[:, k, ws], wkvl[:, k, ws], xth[:, k, c0:c0 + cn],
                                     xtl[:, k, c0:c0 + cn], k == 0, k == KC - 1)
                else:
                    it, c = divmod(a - 1 - len(KCH), len(KCH))
                    c0, cn = KCH[c]
                    ins = pe.matmul(ps[:, 0:cn], qh[:, p, it * P:(it + 1) * P], kh[:, p, c0:c0 + cn],
                                    start=True, stop=True)
                ins.then_inc(s_aP, 1)

            def batch(b, last):
                for i in range(NG, NW):
                    value(b, i)
                pe.wait_ge(s_wL, done(NW, b, NW - 1))

                def pv(n, h, p, j):
                    r = rows(j, JT0, JR0)
                    vs = bass.ds(h * DH0, DH0)
                    pe.wait_ge(s_pH, done(JT0, n, j))
                    if j == 0:
                        pe.wait_ge(s_oL, done(1, n, 0) - 1)
                    pe.matmul(psO[:, :], vh[0:r, j, vs], ph[0:r, PR[j], :], start=(j == 0), stop=False)
                    pe.matmul(psO[:, :], vl[0:r, j, vs], ph[0:r, PR[j], :], start=False, stop=False)
                    pe.wait_ge(s_pL, done(JT0, n, j))
                    pe.matmul(psO[:, :], vh[0:r, j, vs], pl[0:r, PR[j], :], start=False,
                              stop=(j == JT0 - 1)).then_inc(s_pv, 1)

                def tail(n, h, p, step):
                    if step == 0:
                        pe.wait_ge(s_acc, done(JT0, n, JT0 - 1))
                        pe.wait_ge(s_mrow, done(1, n, 0))
                        for it in range(ST):
                            ins = pe.matmul(psM[:, it:it + 1], acc[:, p, it * P:(it + 1) * P], four[:, :],
                                            start=True, stop=True)
                        ins.then_inc(s_lP, 1)
                        return
                    pe.wait_ge(s_oL, done(1, n, 0))
                    pe.wait_ge(s_yF, done(2, n, step - 1) - 1)
                    for u in range(2):
                        it = 2 * (step - 1) + u
                        cs = slice(it * P, (it + 1) * P)
                        wh, wl = (w[:, bass.ds(h, 1), :].rearrange("p a n -> p (a n)") for w in (woh, wol))
                        ins = triple(psW[:, u, :], oh[:, cs], ol[:, cs], wh, wl)
                    ins.then_inc(s_yP, 1)

                def main(h, p, slots, with_tail):
                    n = b * H0 + h
                    for j in range(JT0):
                        r = rows(j, JT0, JR0)
                        js = slice(j * P, j * P + r)
                        dn, pj = before(SR, j)
                        pe.wait_ge(s_pH, done(JT0, n + dn, pj))
                        if j == 0:
                            pe.wait_ge(s_mrow, done(1, n, 0))
                        ps = psS[SR[j]][0:r, :]
                        triple(ps, kh[:, p, js], kl[:, p, js], qh[:, p, :], ql[:, p, :], True, False)
                        pe.matmul(ps, oneb[:, 0:r], mrow[:, p, :], start=False, stop=True).then_inc(s_sP, 1)
                        if j >= LAG:
                            pv(n, h, p, j - LAG)
                        elif with_tail:
                            pv(n - 1, h - 1, 1 - p, JT0 - LAG + j)
                        if with_tail and j in TAIL:
                            tail(n - 1, h - 1, 1 - p, TAIL.index(j))
                        for what in slots[j]:
                            pre(n + 1, 0 if slots is NEXT else h + 1, 1 - p, what, b + 1)

                main(0, 0, SLOTS, False)
                with pe.Fori(0, 3) as t:
                    main(t * 2 + 1, 1, SLOTS, True)
                    main(t * 2 + 2, 0, SLOTS, True)
                main(H0 - 1, 1, NONE if last else NEXT, True)
                for j in range(JT0 - LAG, JT0):
                    pv(b * H0 + (H0 - 1), H0 - 1, 1, j)
                for step in range(3):
                    tail(b * H0 + (H0 - 1), H0 - 1, 1, step)

            for what in sum(NEXT, []):
                pre(0, 0, 0, what, 0)
            with pe.Fori(0, B - 1) as b:
                batch(b, False)
            batch(B - 1, True)

        @block.vector
        def _(v):
            def norms(b, NST):
                steps = [0]

                def step(ins):
                    ins.then_inc(s_st, 1)
                    steps[0] += 1

                def own():
                    v.wait_ge(s_st, b * NST + steps[0])

                def x_tile(u):
                    return X[:, bass.ds(b * ST + u, 1), :].rearrange("p a c -> p (a c)")

                def stats(src, slot, r=P):
                    step(v.bn_stats(st[0:r, slot, :], src))

                def aggr(s, first, last, r=P):
                    if first:
                        own()
                        v.nop(nofuse=True)
                    step(v.bn_aggr(mv[0:r, s, :], st[0:r, s, :]))
                    if last:
                        own()
                        v.sem_inc(s_mv, 1)

                def context_stats(u):
                    r = rows(u, MT, MR)
                    if u == 0:
                        v.wait_ge(s_cx, b * 32 + 32)
                    stats(cx[0:r, u, :], ST + u, r)

                def normal_latents(u):
                    if u == 0:
                        v.wait_ge(s_rstd, b * 3 + 3 + 2)
                    step(v.tensor_scalar(lat[:, u, :], x_tile(u), mv[:, u, 0:1], rstd[:, u:u + 1], ALU.subtract,
                                         ALU.mult))

                def latent_stats(u):
                    if u == 0:
                        own()
                    stats(lat[:, u, :], u)

                def normal_context(u):
                    r = rows(u, MT, MR)
                    step(v.tensor_scalar(cx[0:r, u, :], cx[0:r, u, :], mv[0:r, ST + u, 0:1],
                                         rstd[0:r, ST + u:ST + u + 1], ALU.subtract, ALU.mult))

                def second_norm(u):
                    if u == 0:
                        v.wait_ge(s_rstd, b * 3 + 3 + 3)
                    step(v.tensor_scalar(lat[:, u, :], lat[:, u, :], mv[:, u, 0:1], rstd[:, u:u + 1],
                                         ALU.subtract, ALU.mult))
                    if u == ST - 1:
                        own()
                        v.sem_inc(s_nt, 2)

                one = [(lambda u=u: stats(x_tile(u), u)) for u in range(ST)]
                one += [(lambda u=u: aggr(u, u == 0, u == ST - 1)) for u in range(ST)]
                two = [(lambda u=u: context_stats(u)) for u in range(MT)]
                two += [(lambda u=u: aggr(ST + u, u == 0, u == MT - 1, rows(u, MT, MR))) for u in range(MT)]
                three = [(lambda u=u: normal_latents(u)) for u in range(ST)]
                three += [(lambda u=u: latent_stats(u)) for u in range(ST)]
                three += [(lambda u=u: aggr(u, u == 0, u == ST - 1)) for u in range(ST)]
                three += [(lambda u=u: normal_context(u)) for u in range(MT)]
                four_ = [(lambda u=u: second_norm(u)) for u in range(ST)]
                return one, two, three, four_

            v.sem_inc(s_wL, NW)
            v.sem_inc(s_aF, NA)
            v.sem_inc(s_mc, 1)
            v.sem_inc(s_mrow, 1)
            v.sem_inc(s_pL, JT0)
            v.sem_inc(s_oL, 1)
            v.sem_inc(s_rl, 2)
            v.sem_inc(s_yF, 2)
            v.wait_ge(s_const, 5)
            NST = 4 * ST + 2 * MT + 2 * ST + MT
            for part in norms(0, NST):
                for run in part:
                    run()
            v.wait_ge(s_small, 16 * 7)
            v.tensor_scalar(bq[:, :], bq[:, :], WS, None, ALU.mult).then_inc(s_b16, 1)
            v.tensor_scalar(bkv[:, 0:H0], bkv[:, 0:H0], WS, None, ALU.mult).then_inc(s_b16, 1)
            v.wait_ge(s_br, 1)
            v.tensor_copy(brow[:, :], psM[0:1, 0:D]).then_inc(s_brow, 1)
            v.wait_ge(s_br, 2)
            v.tensor_copy(bb[:, :], psM[:, 0:D]).then_inc(s_brow, 1)
            v.wait_ge(s_b16, 2)

            def turn(b, i):
                v.wait_ge(s_wH, done(NW, b, i))
                k, gidx = i % KC, i // KC
                c0 = gidx * 512
                n = min(512, J0 - c0)
                gg, be = (gl, bl) if gidx == 0 else (gm, bm)
                if i >= 1:
                    v.wait_ge(s_wL, done(NW, b, i - 1))
                v.tensor_scalar(tmp[:, 0:n], psA[i % 2][:, 0:n], gg[:, k:k + 1], be[:, k:k + 1],
                                ALU.mult, ALU.add).then_inc(s_wt, 1)
                v.wait_ge(s_wt, b * NG + i + 1)
                v.tensor_tensor(xtl[:, k, c0:c0 + n], tmp[:, 0:n], xth[:, k, c0:c0 + n],
                                ALU.subtract).then_inc(s_wL, 1)

            def value(b, i):
                v.wait_ge(s_wH, done(NW, b, i))
                j, half = (i - NG) // 2, (i - NG) % 2
                r = rows(j, JT0, JR0)
                cs = slice(half * 512, half * 512 + 512)
                v.tensor_tensor(vl[0:r, j, cs], ring4[i % 4][0:r, :], vh[0:r, j, cs], ALU.subtract).then_inc(s_wL, 1)

            def pre(n, h, p, what, b=None):
                if what[0] == "T":
                    turn(b, int(what[1:]))
                    return
                if what == "mc":
                    v.wait_ge(s_aF, done(NA, n, NA - 1))
                    v.tensor_reduce(mc[:, p, :], mx[:, p, :, :], AX.X, ALU.max).then_inc(s_mc, 1)
                    return
                if what == "mT":
                    v.wait_ge(s_mT, done(1, n, 0))
                    v.tensor_scalar(mrow[:, p, :], psM[0:1, :], -1.0, None, ALU.mult).then_inc(s_mrow, 1)
                    return
                a = int(what[1:])
                ps = psA[a % 2]
                if a <= len(KCH):
                    v.wait_ge(s_aH, done(1 + len(KCH), n, a))
                    if a == 0:
                        v.scalar_tensor_tensor(ql[:, p, :], ps[:, :], bq[:, bass.ds(h, 1)], qh[:, p, :],
                                               ALU.add, ALU.subtract).then_inc(s_aF, 1)
                    else:
                        c0, cn = KCH[a - 1]
                        v.scalar_tensor_tensor(kl[:, p, c0:c0 + cn], ps[:, 0:cn], bkv[:, bass.ds(h, 1)],
                                               kh[:, p, c0:c0 + cn], ALU.add, ALU.subtract).then_inc(s_aF, 1)
                else:
                    it, c = divmod(a - 1 - len(KCH), len(KCH))
                    c0, cn = KCH[c]
                    v.wait_ge(s_aP, done(NA, n, a))
                    v.tensor_reduce(mx[:, p, it, c:c + 1], ps[:, 0:cn], AX.X, ALU.max).then_inc(s_aF, 1)

            def batch(b, last):
                one, two, three, four_ = ([], [], [], []) if last else norms(b + 1, NST)
                for i in range(NG, NW):
                    value(b, i)
                    q = i - NG
                    todo = one[q:q + 1]
                    if q >= NV // 3:
                        q -= NV // 3
                        per = NV - NV // 3
                        todo = todo + two[q * len(two) // per:(q + 1) * len(two) // per]
                    for run in todo:
                        run()

                def out_lo(n):
                    v.wait_ge(s_oH, done(1, n, 0))
                    v.wait_ge(s_yP, done(2, n, 1) - 2)
                    v.scalar_tensor_tensor(ol[:, :], psO[:, :], 1.0 / 64, oh[:, :], ALU.mult,
                                           ALU.subtract).then_inc(s_oL, 1)

                def tail(n, h, p, step_):
                    if step_ == 0:
                        v.wait_ge(s_lP, done(1, n, 0) + 1)
                        v.reciprocal(rl[:, p, :], psM[:, 0:ST]).then_inc(s_rl, 1)
                        return
                    v.wait_ge(s_yP, done(2, n, step_ - 1))
                    v.wait_ge(s_rl, done(1, n, 0) + 1)
                    if step_ == 1:
                        v.wait_ge(s_yF, done(2, n, -1))
                    for u in range(2):
                        it = 2 * (step_ - 1) + u
                        xs = X[:, bass.ds(b * ST + it, 1), :].rearrange("p a c -> p (a c)")
                        ins = v.scalar_tensor_tensor(xs, psW[:, u, :], rl[:, p, it:it + 1], xs, ALU.mult, ALU.add)
                    ins.then_inc(s_yF, 1)

                def main(h, p, slots, with_tail):
                    n = b * H0 + h
                    def low(j):
                        r = rows(j, JT0, JR0)
                        dn, pj = before(PR, j)
                        v.wait_ge(s_pH, done(JT0, n, j))
                        v.wait_ge(s_pv, done(JT0, n + dn, pj))
                        v.tensor_tensor(pl[0:r, PR[j], :], pf[0:r, PR[j], :], ph[0:r, PR[j], :],
                                        ALU.subtract).then_inc(s_pL, 1)

                    for j in range(JT0):
                        if j >= 1:
                            low(j - 1)
                        if with_tail and j == LAG:
                            out_lo(n - 1)
                        if with_tail and j in TAIL:
                            tail(n - 1, h - 1, 1 - p, TAIL.index(j))
                        if isinstance(h, int) and h == 0:
                            for run in three[j * len(three) // JT0:(j + 1) * len(three) // JT0]:
                                run()
                        if isinstance(h, int) and h == H0 - 1 and j == 0:
                            for run in four_:
                                run()
                        for what in slots[j]:
                            pre(n + 1, 0 if slots is NEXT else h + 1, 1 - p, what, b + 1)
                    low(JT0 - 1)

                main(0, 0, SLOTS, False)
                with v.Fori(0, 3) as t:
                    main(t * 2 + 1, 1, SLOTS, True)
                    main(t * 2 + 2, 0, SLOTS, True)
                main(H0 - 1, 1, NONE if last else NEXT, True)
                out_lo(b * H0 + (H0 - 1))
                for step_ in range(3):
                    tail(b * H0 + (H0 - 1), H0 - 1, 1, step_)

            for what in sum(NEXT, []):
                if what == "A0":
                    for i, (lo, f, hi) in enumerate(((wkvl, wkv_f, wkvh), (wql, wq_f, wqh), (wol, wo_f, woh))):
                        v.wait_ge(s_wh, i + 1)
                        v.scalar_tensor_tensor(lo[:, :, :], f, WS, hi[:, :, :], ALU.mult,
                                               ALU.subtract).then_inc(s_wl, 1)
                pre(0, 0, 0, what, 0)
            with v.Fori(0, B - 1) as b:
                batch(b, False)
            batch(B - 1, True)
            v.wait_ge(s_yF, 2 * (B * H0 + 1))
            for t in range(NT):
                ins = v.tensor_tensor(X[:, t, :], X[:, t, :], bb[:, :], ALU.add)
            ins.then_inc(s_fin, 1)
            v.wait_ge(s_fin, 1)


def experts(nc, X, identf, io, layer):
    E, F = 8, 1024
    FT = F // P
    T = B * S
    CH = 256
    IT = CH // P
    CAP = 2 * T // E
    NC = E * CAP // CH if layer == 0 else 2 * T // CH + E
    ROWS = (NC + 1) * CH
    MAXC = T // CH
    U32, I32 = mybir.dt.uint32, mybir.dt.int32
    names = {0: ("L0_ffn_w_router", "L0_ffn_w1", "L0_ffn_w2"),
             1: ("L1_ffn_Wr", "L1_ffn_W1", "L1_ffn_W2")}[layer]
    GELU = ACT.Gelu_apprx_tanh if layer == 0 else ACT.Gelu
    GI = KC * NT // 4
    PR = ring(FT, 4)
    HR = ring(FT, 3)
    GR = 4

    with ExitStack() as ctx:
        tag = f"f{layer}_"

        def sb(name, shape, dt=F32):
            return ctx.enter_context(nc.sbuf_tensor(tag + name, shape, dt))

        def sem(name):
            return ctx.enter_context(nc.semaphore(tag + name))

        w16 = sb("w16", [P, E, 4, KC * F], F16)
        stage = sb("stage", [P, 2, KC * F])
        wt = sb("wt", [E, NT, P]) if layer else None
        xth, xtl = w16[:, E - 1, 0:2, :], w16[:, E - 1, 2:4, :]
        xn = sb("xn", [P, NT, D])
        room = xn[:, :, :].rearrange("p t c -> p (t c)")
        hf = room[:, 0:1024].rearrange("p (r t) -> p r t", t=CH)
        xb = room[:, 1024:2048].rearrange("p (b u c) -> p b u c", b=2, c=D)
        yb = room[:, 2048:3072].rearrange("p (b u c) -> p b u c", b=2, c=D)
        hh = room[:, 3072:3584].bitcast(F16).rearrange("p (r t) -> p r t", t=CH)
        hl = room[:, 3584:4096].bitcast(F16).rearrange("p (r t) -> p r t", t=CH)
        gy = xn[:, 0:GR, :]
        xh, xl = sb("xh", [P, 2, KC, CH], F16), sb("xl", [P, 2, KC, CH], F16)
        st, mv = sb("st", [P, NT, 6]), sb("mv", [P, NT, 2])
        ve, mhalf, rstd = sb("ve", [P, NT]), sb("mhalf", [P, NT]), sb("rstd", [P, NT])
        wr, wrh, wrl = sb("wr", [P, KC, E]), sb("wrh", [P, KC, E], F16), sb("wrl", [P, KC, E], F16)
        brb = sb("brb", [P, E])
        b2 = sb("b2", [E, D])
        bias = sb("bias", [1, D])
        b1r = sb("b1r", [E * FT, P])
        b1 = sb("b1", [P, E, FT])
        b1e = sb("b1e", [P, 2, FT])
        ones, upper = sb("ones", [P, P]), sb("upper", [P, P])
        zero = sb("zero", [P, D])
        revi, iexp, thr = sb("revi", [P, E]), sb("iexp", [P, E]), sb("thr", [P, MAXC])
        lg, ex, sc, sc2, eq, cand, oh1, oh2, wgt, off, tot = (
            sb(n, [P, NT, E]) for n in ("lg", "ex", "sc", "sc2", "eq", "cand", "oh1", "oh2", "wgt", "off", "tot"))
        m1, m2, f1, sm, rs = (sb(n, [P, NT]) for n in ("m1", "m2", "f1", "sm", "rs"))
        pos, wk = sb("pos", [P, 2, NT]), sb("wk", [P, 2, NT])
        vd, dump = sb("vd", [P, 2, NT]), sb("dump", [P, 2, NT])
        dumpi = sb("dumpi", [P, 2, NT], I32)
        sidx, gidx = sb("sidx", [P, 2, NT], U32), sb("gidx", [P, 2, NT], U32)
        nch, cb, base = sb("nch", [P, E]), sb("cb", [P, E]), sb("base", [P, E])
        cmpc = sb("cmpc", [P, E, MAXC])
        ci, ciE = sb("ci", [1, NC], I32), sb("ciE", [1, NC, E])
        cf, tf = sb("cf", [1, NC]), sb("tf", [1, NC + 1])
        table = sb("table", [1, NC + 1], I32)
        tie_e = sb("tie_e", [1, T // CH * E + 1], I32)
        rest, restf, flag = sb("rest", [P, 1]), sb("restf", [1, 1]), sb("flag", [1, 1], I32)

        xrows = nc.dram_tensor(tag + "xrows", (ROWS + 2 * T, D), F32, kind="Internal").ap()
        yrows = nc.dram_tensor(tag + "yrows", (NC * CH, D), F32, kind="Internal").ap()
        xall = nc.dram_tensor(tag + "xall", (T + CH, D), F32, kind="Internal").ap()

        psH = [ctx.enter_context(nc.psum_tensor(tag + f"psH{i}", [P, 512], F32)) for i in range(3)]
        psX = ctx.enter_context(nc.psum_tensor(tag + "psX", [P, 512], F32))
        psY = [ctx.enter_context(nc.psum_tensor(tag + f"psY{i}", [P, 512], F32)) for i in range(2 * IT)]
        ring4 = psH + [psX]

        s_const = sem("const")
        s_z = sem("z")
        s_small = sem("small")
        s_w = [sem("w0"), sem("w1")]
        s_wh = sem("wh")
        s_wl = sem("wl")
        s_st = sem("st")
        s_mv = sem("mv")
        s_pool = sem("pool")
        s_rstd = sem("rstd")
        s_nt = sem("nt")
        s_tP = sem("tP")
        s_tH = sem("tH")
        s_tL = sem("tL")
        s_wr = sem("wr")
        s_lg = sem("lg")
        s_b1 = sem("b1")
        s_sh = sem("sh")
        s_ex = sem("ex")
        s_sel = sem("sel")
        s_rk = sem("rk")
        s_idx = sem("idx")
        s_rest = sem("rest")
        s_tab = sem("tab")
        s_sc = sem("sc")
        s_wtP = sem("wtP")
        s_wtF = sem("wtF")
        s_gy = [sem(f"gy{i}") for i in range(GR)]
        s_gu = sem("gu")

        class Loop:

            def __init__(self, name):
                self.xb = [sem(name + "xb0"), sem(name + "xb1")]
                self.ys = [sem(name + "ys0"), sem(name + "ys1")]
                self.xP = sem(name + "xP")
                self.xH = sem(name + "xH")
                self.xL = sem(name + "xL")
                self.b1 = sem(name + "b1")
                self.hP = sem(name + "hP")
                self.hH = sem(name + "hH")
                self.hF = sem(name + "hF")
                self.hL = sem(name + "hL")
                self.hU = sem(name + "hU")
                self.yF = sem(name + "yF")

        main = Loop("m")
        TC = T // CH
        NTIE = E * TC

        block = ctx.enter_context(nc.Block(no_gpsimd_drain=True))
        NSMALL = 4 if layer else 2
        NCONST = 5 + 2 * E + MAXC + 5
        PIECES, EARLY = FT, 2
        PH = PIECES // 2
        PS = KC * F // PH


        def load_rows(sp, L, m, p, src):
            sp.wait_ge(L.xP, m * 2 + p + 1)
            sp.dma_start(xb[:, p, :, :], src.rearrange("(u p) c -> p u c", p=P)).then_inc(L.xb[p], 16)

        def pe_turn(pe, L, m, p):
            n = m * 2 + p
            pe.wait_ge(L.xb[p], m * 16 + 16)
            pe.wait_ge(L.xL, n + 1)
            for k in range(KC):
                for u in range(IT):
                    ins = pe.transpose(psX[:, k * CH + u * P:k * CH + (u + 1) * P],
                                       xb[:, p, u, k * P:(k + 1) * P], identf[:, :])
            ins.then_inc(L.xP, 1)

        def pe_hidden(pe, L, n, p, e, f):
            dn, pf = before(HR, f)
            pe.wait_ge(L.hF, done(FT, n + dn, pf))
            ps = psH[HR[f]][:, 0:CH]
            for k in range(KC):
                ks = slice(k * F + f * P, k * F + (f + 1) * P)
                a, b_ = (w16[:, bass.ds(e, 1), part, ks].rearrange("p a f -> p (a f)") for part in (0, 1))
                pe.matmul(ps, a, xh[:, p, k, :], start=(k == 0), stop=False)
                pe.matmul(ps, a, xl[:, p, k, :], start=False, stop=False)
                ins = pe.matmul(ps, b_, xh[:, p, k, :], start=False, stop=(k == KC - 1))
            ins.then_inc(L.hP, 1)

        def pe_output(pe, L, n, p, e, f):
            ds = slice(f * D, (f + 1) * D)
            a, b_ = (w16[:, bass.ds(e, 1), part, ds].rearrange("p a d -> p (a d)") for part in (2, 3))
            if f == 0:
                pe.wait_ge(L.yF, n + 1)
            pe.wait_ge(L.hH, done(FT, n, f))
            for it in range(IT):
                y, h = psY[p * IT + it][:, 0:D], hh[:, PR[f], it * P:(it + 1) * P]
                pe.matmul(y, h, a, start=(f == 0), stop=False)
                pe.matmul(y, h, b_, start=False, stop=False)
            pe.wait_ge(L.hL, done(FT, n, f))
            for it in range(IT):
                y, h = psY[p * IT + it][:, 0:D], hl[:, PR[f], it * P:(it + 1) * P]
                ins = pe.matmul(y, h, a, start=False, stop=(f == FT - 1))
            ins.then_inc(L.hU, 1)

        def pe_chunk(pe, L, m, p, experts_of, c, splits):
            n = m * 2 + p
            e, e_next = (pe.value_load(experts_of[0:1, bass.ds(c + i, 1)], min_val=0, max_val=E - 1)
                         for i in range(2))
            for f in range(2, FT):
                pe_hidden(pe, L, n, p, e, f)
                pe_output(pe, L, n, p, e, f - 2)
                if f == 3:
                    pe_turn(pe, L, m + p, 1 - p)
            pe.wait_ge(L.xL, n + 3)
            if splits:
                pe.wait_ge(s_wl, (n + 3) * PIECES)
            for f in range(2):
                pe_hidden(pe, L, n + 1, 1 - p, e_next, f)
                pe_output(pe, L, n, p, e, FT - 2 + f)

        def split_high(act, e, q):
            half, cs = q // PH, slice(q % PH * PS, (q % PH + 1) * PS)
            act.wait_ge(s_w[half], e * 16 + 16)
            act.nop(nofuse=True)
            w = w16[:, bass.ds(e, 1), 2 * half, cs].rearrange("p a f -> p (a f)")
            act.activation(w, stage[:, half, cs], ACT.Copy, scale=WS).then_inc(s_wh, 1)

        def split_low(v, e, q):
            half, cs = q // PH, slice(q % PH * PS, (q % PH + 1) * PS)
            v.wait_ge(s_wh, e * PIECES + q + 1)
            w = [w16[:, bass.ds(e, 1), 2 * half + part, cs].rearrange("p a f -> p (a f)") for part in (0, 1)]
            v.scalar_tensor_tensor(w[1], stage[:, half, cs], WS, w[0], ALU.mult, ALU.subtract).then_inc(s_wl, 1)

        def act_turn(act, L, m, p):
            act.wait_ge(L.xP, m * 2 + p + 3)
            act.activation(xh[:, p, :, :].rearrange("p k t -> p (k t)"), psX[:, :], ACT.Copy).then_inc(L.xH, 1)

        def act_chunk(act, L, m, p, splits):
            n = m * 2 + p
            if layer:
                act.wait_ge(L.b1, n + 1)
                act.nop(nofuse=True)
            for f in range(FT):
                dn, pf = before(PR, f)
                bs = b1e[:, p, f:f + 1] if layer else 0.0
                ps = psH[HR[f]][:, 0:CH]
                act.wait_ge(L.hP, n * FT + f + 1)
                act.wait_ge(L.hU, done(FT, n + dn, pf))
                act.activation(hh[:, PR[f], :], ps, GELU, bias=bs, scale=1.0 / WS).then_inc(L.hH, 1)
                act.wait_ge(L.hL, done(FT, n + dn, pf))
                act.activation(hf[:, PR[f], :], ps, GELU, bias=bs, scale=1.0 / WS).then_inc(L.hF, 1)
                if f == 4:
                    act_turn(act, L, m + p, 1 - p)
                if splits:
                    split_high(act, n + EARLY, f)

        def dve_turn(v, L, m, p):
            v.wait_ge(L.xH, m * 2 + p + 1)
            v.tensor_tensor(xl[:, p, :, :].rearrange("p k t -> p (k t)"), psX[:, :],
                            xh[:, p, :, :].rearrange("p k t -> p (k t)"), ALU.subtract).then_inc(L.xL, 1)

        def dve_bias(v, L, m, p, e, wait=True):
            if wait:
                v.wait_ge(L.hF, done(FT, m * 2 + p - 1, -1))
                v.nop(nofuse=True)
            v.tensor_copy(b1e[:, p, :], b1[:, bass.ds(e, 1), :].rearrange("p a f -> p (a f)")).then_inc(L.b1, 1)

        def dve_chunk(v, L, m, p, take, splits, bias_next):
            n = m * 2 + p
            for f in range(FT):
                dn, pf = before(PR, f)
                v.wait_ge(L.hF, done(FT, n, f))
                v.wait_ge(L.hU, done(FT, n + dn, pf))
                v.tensor_tensor(hl[:, PR[f], :], hf[:, PR[f], :], hh[:, PR[f], :], ALU.subtract).then_inc(L.hL, 1)
                if f == 4:
                    dve_turn(v, L, m + p, 1 - p)
                if f == 5 and layer:
                    bias_next()
                if splits:
                    split_low(v, n + EARLY, f)
            v.wait_ge(L.hU, done(FT, n, FT - 1))
            take(n)

        @block.sync
        def _(sp):
            sp.dma_start(wr[:, :, :], io[names[0]].rearrange("(k p) e -> p k e", p=P)).then_inc(s_small, 16)
            if layer:
                sp.dma_start(brb[:, :], io["L1_ffn_br"].rearrange("(a e) -> a e", a=1).to_broadcast([P, E])
                             ).then_inc(s_small, 16)
                sp.dma_start(b2[:, :], io["L1_ffn_b2"]).then_inc(s_small, 16)
                sp.dma_start(b1r[:, :], io["L1_ffn_b1"].rearrange("e (f p) -> (e f) p", p=P)).then_inc(s_small, 16)
            else:
                sp.dma_start(bias[:, :], io["L0_ffn_bias"].rearrange("a b d -> (a b) d")).then_inc(s_small, 16)
            def load_weights(e, half):
                sp.wait_ge(s_wl, (e + 1) * PIECES - PIECES + (half + 1) * PH)
                if half == 0:
                    src = io[names[1]][bass.ds(e, 1)].rearrange("a (k p) f -> p (a k) f", p=P)
                    dst = stage[:, 0, :].rearrange("p (k f) -> p k f", k=KC)
                else:
                    src = io[names[2]][bass.ds(e, 1)].rearrange("a (f p) d -> p (a f) d", p=P)
                    dst = stage[:, 1, :].rearrange("p (f d) -> p f d", f=FT)
                sp.dma_start(dst, src).then_inc(s_w[half], 16)

            def load_chunk(m, p):
                load_rows(sp, main, m, p, xrows[bass.ds((m * 2 + p) * CH, CH), :])

            with sp.Fori(0, EARLY + 1) as e:
                for half in range(2):
                    load_weights(e, half)
            sp.wait_ge(s_z, 16)
            sp.wait_ge(s_sc, 16 * (2 * NT + 2 * layer))
            for c in range(EARLY + 1):
                load_chunk(c // 2, c % 2)
            def store(m, p):
                n = m * 2 + p
                sp.wait_ge(main.yF, n + 3)
                sp.dma_start(yrows[bass.ds(n * CH, CH), :].rearrange("(u p) c -> p u c", p=P),
                             yb[:, p, :, :]).then_inc(main.ys[p], 16)

            load_weights(3, 0)
            load_chunk(1, 1)
            load_weights(3, 1)
            store(0, 0)
            with sp.Fori(2, E // 2) as m:
                for p in range(2):
                    load_weights(m * 2 + p, 0)
                    load_chunk(m, p)
                    load_weights(m * 2 + p, 1)
                    store(m - 2 + p, 1 - p)
            with sp.Fori(E // 2, NC // 2) as m:
                for p in range(2):
                    load_chunk(m, p)
                    store(m - 2 + p, 1 - p)
            load_rows(sp, main, NC // 2, 0, xall[0:CH, :] if layer else xrows[NC * CH:(NC + 1) * CH, :])
            for n in range(NC - 3, NC):
                store(n // 2, n % 2)
            if layer:
                sp.wait_ge(s_tab, 1)
                found = sp.value_load(flag[0:1, 0:1], min_val=0, max_val=T * E)
                with sp.If(found > 0):
                    sp.wait_ge(s_gu, 2 * NT)
                    with sp.Fori(0, E) as e:
                        with sp.Fori(0, TC // 2) as c:
                            m = e * (TC // 2) + c + NC // 2
                            load_rows(sp, main, m, 1, xall[bass.ds((c * 2 + 1) * CH, CH), :])
                            load_rows(sp, main, m + 1, 0, xall[bass.ds((c * 2 + 2) * CH, CH), :])
                    sp.wait_ge(main.xb[0], 16 * ((NC + NTIE) // 2 + 1))
            sp.wait_ge(main.xb[0], 16 * (NC // 2 + 1))

        @block.gpsimd
        def _(g):
            k = [0]

            def const(ap, val):
                g.memset(ap, val).then_inc(s_const, 1)
                k[0] += 1

            for ap, val in ((mhalf[:, :], -0.5), (ones[:, :], 1.0), (upper[:, :], 0.0), (zero[:, :], 0.0)):
                const(ap, val)
            for e in range(E):
                const(revi[:, e:e + 1], float(E - e))
                const(iexp[:, e:e + 1], float(e))
            for c in range(MAXC):
                const(thr[:, c:c + 1], float(c * CH) if c else -1.0)
            g.wait_ge(s_const, k[0])
            g.affine_select(out=upper[:, :], in_=upper[:, :], compare_op=ALU.is_ge, fill=1.0, base=0,
                            pattern=[[-1, P]], channel_multiplier=1).then_inc(s_const, 1)
            g.iota(dumpi[:, :, :], pattern=[[T, 2], [P, NT]], base=ROWS, channel_multiplier=1).then_inc(s_const, 1)
            if layer:
                g.iota(ci[:, :], pattern=[[1, NC]], base=0, channel_multiplier=0).then_inc(s_const, 1)
                g.iota(tie_e[:, 0:NTIE], pattern=[[1, E], [0, TC]], base=0, channel_multiplier=0).then_inc(s_const, 1)
                g.iota(tie_e[:, NTIE:NTIE + 1], pattern=[[1, 1]], base=0, channel_multiplier=0).then_inc(s_const, 1)
            else:
                g.iota(table[:, 0:NC], pattern=[[1, E], [0, NC // E]], base=0, channel_multiplier=0
                       ).then_inc(s_const, 1)
                g.iota(table[:, NC:NC + 1], pattern=[[1, 1]], base=0, channel_multiplier=0).then_inc(s_const, 1)
                g.sem_inc(s_const, 1)
            g.sem_inc(s_const, 1)
            g.wait_ge(s_const, NCONST)
            g.dma_start(xrows[0:ROWS, :].rearrange("(t p) c -> p t c", p=P),
                        zero[:, :].unsqueeze(1).broadcast_to([P, ROWS // P, D])).then_inc(s_z, 16)
            g.wait_ge(s_mv, 1)
            g.tensor_scalar(ve[:, :], mv[:, :, 1], EPS, None, ALU.add).then_inc(s_pool, 1)
            g.wait_ge(s_pool, 1)
            g.tensor_tensor(rstd[:, :], ve[:, :], mhalf[:, :], ALU.pow).then_inc(s_rstd, 1)
            if layer:
                g.wait_ge(s_nt, NT)
                g.dma_start(xall[0:T, :].rearrange("(t p) c -> p t c", p=P), xn[:, :, :]).then_inc(s_sc, 16)
                g.dma_start(xall[T:T + CH, :].rearrange("(t p) c -> p t c", p=P), xn[:, 0:IT, :]).then_inc(s_sc, 16)
            g.wait_ge(s_z, 16)
            g.wait_ge(s_idx, 1)
            for t in range(NT):
                for q in range(2):
                    g.indirect_dma_start(xrows, bass.IndirectOffsetOnAxis(ap=sidx[:, q, t:t + 1], axis=0),
                                         xn[:, t, :], None).then_inc(s_sc, 16)
            g.wait_ge(main.yF, NC + 2)
            g.wait_ge(main.xb[0], 16 * (NC // 2 + 1))
            for p in range(2):
                g.wait_ge(main.ys[p], 16 * (NC // 2 + 1))
            for i in range(2 * NT):
                t, q = i // 2, i % 2
                if i >= GR:
                    g.wait_ge(s_gu, i - GR + 1)
                g.indirect_dma_start(gy[:, i % GR, :], None, yrows,
                                     bass.IndirectOffsetOnAxis(ap=gidx[:, q, t:t + 1], axis=0)
                                     ).then_inc(s_gy[i % GR], 16)

        @block.scalar
        def _(act):
            act.sem_inc(main.hF, FT)
            act.sem_inc(main.hH, FT)
            act.wait_ge(s_small, 16 * NSMALL)
            act.activation(wrh[:, :, :], wr[:, :, :], ACT.Copy, scale=WS).then_inc(s_wr, 1)
            for i in range(GI):
                kk, q = i % KC, i // KC
                act.wait_ge(s_tP, i + 1)
                act.activation(xth[:, kk, q * 512:q * 512 + 512], ring4[i % 4][:, :], ACT.Copy).then_inc(s_tH, 1)
            act.wait_ge(s_sh, 1)
            act.activation(ex[:, :, :], sc2[:, :, :], ACT.Exp).then_inc(s_ex, 1)
            act.wait_ge(s_lg, 1)
            with act.Fori(0, EARLY) as e:
                for q in range(PIECES):
                    split_high(act, e, q)
            act_turn(act, main, 0, 0)
            for first, last, splits in ((0, (E - EARLY) // 2, True), ((E - EARLY) // 2, NC // 2, False)):
                with act.Fori(first, last) as m:
                    for p in range(2):
                        act_chunk(act, main, m, p, splits)
            for p in range(2):
                act.wait_ge(main.ys[p], 16 * (NC // 2 + 1))
            if layer:
                act.wait_ge(s_tab, 1)
                found = act.value_load(flag[0:1, 0:1], min_val=0, max_val=T * E)
                with act.If(found > 0):
                    act.wait_ge(s_gu, 2 * NT)
                    with act.Fori(NC // 2, (NC + NTIE) // 2) as m:
                        for p in range(2):
                            act_chunk(act, main, m, p, False)

        @block.tensor
        def _(pe):
            pe.sem_inc(main.xP, 2)
            pe.sem_inc(main.hU, FT)
            pe.wait_ge(s_const, NCONST)
            pe.wait_ge(s_small, 16 * NSMALL)
            for i in range(GI):
                kk, q = i % KC, i // KC
                pe.wait_ge(s_nt, 4 * q + 4)
                if i >= 4:
                    pe.wait_ge(s_tL, i - 3)
                for u in range(4):
                    ins = pe.transpose(ring4[i % 4][:, u * P:(u + 1) * P], xn[:, 4 * q + u, kk * P:(kk + 1) * P],
                                       identf[:, :])
                ins.then_inc(s_tP, 1)
            if layer:
                pe.transpose(psY[1][:, 0:E * FT], b1r[:, :], identf[0:E * FT, 0:E * FT]).then_inc(s_b1, 1)
            pe.wait_ge(s_tL, GI)
            pe.wait_ge(s_wr, 2)
            for t in range(NT):
                ts = slice(t * P, (t + 1) * P)
                for kk in range(KC):
                    for j, (a, w) in enumerate(((xth, wrh), (xth, wrl), (xtl, wrh))):
                        ins = pe.matmul(psY[0][:, t * E:(t + 1) * E], a[:, kk, ts], w[:, kk, :],
                                        start=(kk == 0 and j == 0), stop=(kk == KC - 1 and j == 2))
            ins.then_inc(s_lg, 1)
            pe.wait_ge(s_sel, 1)
            sel = cand[:, :, :].rearrange("p t e -> p (t e)")
            pe.matmul(psY[2][:, 0:NT * E], upper[:, :], sel, start=True, stop=True)
            pe.matmul(psY[3][:, 0:NT * E], ones[:, :], sel, start=True, stop=True).then_inc(s_rk, 1)
            if layer:
                pe.wait_ge(s_rest, 1)
                pe.matmul(psY[1][0:1, 0:1], ones[:, 0:1], rest[:, :], start=True, stop=True).then_inc(s_rk, 1)
                pe.wait_ge(s_tab, 1)

            pe.wait_ge(s_idx, 1)
            nq = NT // 4 if layer else 0
            for q in range(nq):
                if q >= 2:
                    pe.wait_ge(s_wtF, q - 1)
                for u in range(4):
                    ins = pe.transpose(psH[q % 2][0:E, u * P:(u + 1) * P], wgt[:, 4 * q + u, :], identf[:, :])
                ins.then_inc(s_wtP, 1)
            for t in range(NT):
                if layer:
                    pe.wait_ge(s_wtF, nq + max(0, t - 3))
                    ins = pe.matmul(psY[t % 4][:, 0:D], wt[:, t, :], b2[:, :], start=True, stop=True)
                else:
                    if t >= 4:
                        pe.wait_ge(s_wtF, t - 3)
                    ins = pe.matmul(psY[t % 4][:, 0:D], ones[0:1, :], bias[:, :], start=True, stop=True)
                ins.then_inc(s_wtP, 1)
            pe.wait_ge(s_wtF, nq + NT)

            pe_turn(pe, main, 0, 0)
            pe.wait_ge(main.xL, 2)
            pe.wait_ge(s_wl, 2 * PIECES)
            for f in range(2):
                pe_hidden(pe, main, 0, 0, 0, f)
            for first, last, splits in ((0, (E - EARLY) // 2, True), ((E - EARLY) // 2, NC // 2, False)):
                with pe.Fori(first, last) as m:
                    for p in range(2):
                        pe_chunk(pe, main, m, p, table, m * 2 + p, splits)
                if splits:
                    pe.wait_ge(s_wl, (E + 1) * PIECES)
            if layer:
                found = pe.value_load(flag[0:1, 0:1], min_val=0, max_val=T * E)
                with pe.If(found > 0):
                    pe.wait_ge(s_gu, 2 * NT)
                    with pe.Fori(0, NTIE // 2) as m:
                        for p in range(2):
                            pe_chunk(pe, main, m + NC // 2, p, tie_e, m * 2 + p, False)

        @block.vector
        def _(v):
            v.sem_inc(s_wl, PIECES)
            v.sem_inc(main.xL, 1)
            v.sem_inc(main.hL, FT)
            v.sem_inc(main.yF, 2)
            v.sem_inc(main.ys[0], 16)
            v.sem_inc(main.ys[1], 16)
            ch = Chain(v, s_st)
            for t in range(NT):
                ch.step(v.bn_stats(st[:, t, :], X[:, t, :]))
            ch.wait()
            for t in range(NT):
                ch.step(v.bn_aggr(mv[:, t, :], st[:, t, :]))
            ch.wait()
            v.sem_inc(s_mv, 1)
            v.wait_ge(s_const, NCONST)
            v.wait_ge(s_small, 16 * NSMALL)
            v.wait_ge(s_wr, 1)
            v.scalar_tensor_tensor(wrl[:, :, :], wr[:, :, :], WS, wrh[:, :, :], ALU.mult,
                                   ALU.subtract).then_inc(s_wr, 1)
            ch.step(v.tensor_copy(dump[:, :, :], dumpi[:, :, :]))
            if layer:
                ch.step(v.tensor_copy(cf[:, :], ci[:, :]))
            v.wait_ge(s_rstd, 1)
            for t in range(NT):
                v.tensor_scalar(xn[:, t, :], X[:, t, :], mv[:, t, 0:1], rstd[:, t:t + 1], ALU.subtract,
                                ALU.mult).then_inc(s_nt, 1)
            for i in range(GI):
                kk, q = i % KC, i // KC
                cs = slice(q * 512, q * 512 + 512)
                v.wait_ge(s_tH, i + 1)
                v.tensor_tensor(xtl[:, kk, cs], ring4[i % 4][:, :], xth[:, kk, cs], ALU.subtract).then_inc(s_tL, 1)
            if layer:
                v.wait_ge(s_b1, 1)
                ch.step(v.tensor_copy(b1[:, :, :].rearrange("p e f -> p (e f)"), psY[1][:, 0:E * FT]))

            def wide(t):
                return t[:, :].unsqueeze(2).broadcast_to([P, NT, E])

            def along(t):
                return t[:, :].unsqueeze(1).broadcast_to([P, NT, E])

            def op(ins):
                ch.step(ins)
                ch.wait()

            def first_max(src, mval, onehot):
                op(v.tensor_reduce(mval[:, :], src, AX.X, ALU.max))
                op(v.tensor_tensor(eq[:, :, :], src, wide(mval), ALU.is_ge))
                op(v.tensor_tensor(cand[:, :, :], eq[:, :, :], along(revi), ALU.mult))
                op(v.tensor_reduce(f1[:, :], cand[:, :, :], AX.X, ALU.max))
                op(v.tensor_tensor(onehot[:, :, :], along(revi), wide(f1), ALU.is_equal))

            def tiles(ps):
                return ps[:, 0:NT * E].rearrange("p (t e) -> p t e", e=E)

            v.wait_ge(s_lg, 1)
            op(v.tensor_scalar(lg[:, :, :], tiles(psY[0]), 1.0 / WS, None, ALU.mult))
            if layer:
                op(v.tensor_tensor(lg[:, :, :], lg[:, :, :], along(brb), ALU.add))
            op(v.tensor_reduce(m1[:, :], lg[:, :, :], AX.X, ALU.max))
            v.tensor_tensor(sc2[:, :, :], lg[:, :, :], wide(m1), ALU.subtract).then_inc(s_sh, 1)
            v.wait_ge(s_ex, 1)
            if not layer:
                op(v.tensor_reduce(sm[:, :], ex[:, :, :], AX.X, ALU.add))
                op(v.reciprocal(rs[:, :], sm[:, :]))
                op(v.tensor_tensor(sc[:, :, :], ex[:, :, :], wide(rs), ALU.mult))
                first_max(sc[:, :, :], m1, oh1)
                op(v.scalar_tensor_tensor(sc2[:, :, :], oh1[:, :, :], -2.0, sc[:, :, :], ALU.mult, ALU.add))
                first_max(sc2[:, :, :], m2, oh2)
                op(v.tensor_copy(wgt[:, :, :], sc[:, :, :]))
            else:
                first_max(lg[:, :, :], m2, oh1)
                op(v.scalar_tensor_tensor(sc2[:, :, :], oh1[:, :, :], -3.0e38, lg[:, :, :], ALU.mult, ALU.add))
                first_max(sc2[:, :, :], m2, oh2)
                op(v.tensor_tensor(eq[:, :, :], lg[:, :, :], wide(m2), ALU.is_ge))
                op(v.tensor_tensor(sc[:, :, :], eq[:, :, :], ex[:, :, :], ALU.mult))
                op(v.tensor_reduce(sm[:, :], sc[:, :, :], AX.X, ALU.add))
                op(v.reciprocal(rs[:, :], sm[:, :]))
                op(v.tensor_tensor(wgt[:, :, :], sc[:, :, :], wide(rs), ALU.mult))
            op(v.tensor_tensor(cand[:, :, :], oh1[:, :, :], oh2[:, :, :], ALU.add))
            v.sem_inc(s_sel, 1)
            if layer:
                op(v.tensor_tensor(sc2[:, :, :], eq[:, :, :], cand[:, :, :], ALU.subtract))
                op(v.tensor_reduce(rest[:, :], sc2[:, :, :].rearrange("p t e -> p (t e)"), AX.X, ALU.add))
                v.sem_inc(s_rest, 1)
                op(v.tensor_tensor(sc[:, :, :], sc2[:, :, :], wgt[:, :, :], ALU.mult))
                op(v.tensor_scalar(sc[:, :, :], sc[:, :, :], 1.0 / WS, None, ALU.mult))
            v.wait_ge(s_rk, 1)
            op(v.tensor_copy(tot[:, :, :], tiles(psY[3])))
            op(v.memset(off[:, 0, :], 0.0))
            for t in range(1, NT):
                op(v.tensor_tensor(off[:, t, :], off[:, t - 1, :], tot[:, t - 1, :], ALU.add))
            if layer:
                op(v.tensor_tensor(nch[:, :], off[:, NT - 1, :], tot[:, NT - 1, :], ALU.add))
            op(v.tensor_tensor(off[:, :, :], tiles(psY[2]), off[:, :, :], ALU.add))
            if layer:
                op(v.tensor_tensor(cmpc[:, :, :], nch[:, :].unsqueeze(2).broadcast_to([P, E, MAXC]),
                                   thr[:, :].unsqueeze(1).broadcast_to([P, E, MAXC]), ALU.is_gt))
                op(v.tensor_reduce(nch[:, :], cmpc[:, :, :], AX.X, ALU.add))
                op(v.memset(cb[:, 0:1], 0.0))
                for e in range(1, E):
                    op(v.tensor_tensor(cb[:, e:e + 1], cb[:, e - 1:e], nch[:, e - 1:e], ALU.add))
                op(v.tensor_scalar(base[:, :], cb[:, :], float(CH), None, ALU.mult))
                op(v.tensor_tensor(ciE[:, :, :], cf[:, :].unsqueeze(2).broadcast_to([1, NC, E]),
                                   cb[0:1, :].unsqueeze(1).broadcast_to([1, NC, E]), ALU.is_ge))
                op(v.tensor_reduce(tf[:, 0:NC], ciE[:, :, 1:E], AX.X, ALU.add))
                op(v.memset(tf[:, NC:NC + 1], 0.0))
                op(v.tensor_copy(table[:, :], tf[:, :]))
                v.wait_ge(s_rk, 2)
                op(v.tensor_copy(flag[:, :], psY[1][0:1, 0:1]))
                v.sem_inc(s_tab, 1)
            else:
                op(v.tensor_scalar(base[:, :], iexp[:, :], float(CAP), None, ALU.mult))
            op(v.tensor_tensor(tot[:, :, :], off[:, :, :], along(base), ALU.add))
            for q, oh in enumerate((oh1, oh2)):
                op(v.tensor_tensor(eq[:, :, :], oh[:, :, :], tot[:, :, :], ALU.mult))
                op(v.tensor_reduce(pos[:, q, :], eq[:, :, :], AX.X, ALU.add))
                op(v.tensor_tensor(eq[:, :, :], oh[:, :, :], wgt[:, :, :], ALU.mult))
                op(v.tensor_reduce(wk[:, q, :], eq[:, :, :], AX.X, ALU.add))
                if not layer:
                    op(v.tensor_tensor(eq[:, :, :], oh[:, :, :], off[:, :, :], ALU.mult))
                    op(v.tensor_reduce(f1[:, :], eq[:, :, :], AX.X, ALU.add))
                    op(v.tensor_scalar(vd[:, q, :], f1[:, :], float(CAP), None, ALU.is_lt))
            if not layer:
                op(v.tensor_tensor(wk[:, :, :], wk[:, :, :], vd[:, :, :], ALU.mult))
                op(v.tensor_tensor(pos[:, :, :], pos[:, :, :], vd[:, :, :], ALU.mult))
                op(v.tensor_copy(gidx[:, :, :], pos[:, :, :]))
                op(v.tensor_scalar(vd[:, :, :], vd[:, :, :], -1.0, 1.0, ALU.mult, ALU.add))
                op(v.tensor_tensor(dump[:, :, :], dump[:, :, :], vd[:, :, :], ALU.mult))
                op(v.tensor_tensor(pos[:, :, :], pos[:, :, :], dump[:, :, :], ALU.add))
                op(v.tensor_copy(sidx[:, :, :], pos[:, :, :]))
            else:
                op(v.tensor_copy(gidx[:, :, :], pos[:, :, :]))
                op(v.tensor_copy(sidx[:, :, :], pos[:, :, :]))
            v.sem_inc(s_idx, 1)
            with v.Fori(0, EARLY) as e:
                for q in range(PIECES):
                    split_low(v, e, q)
            nq = NT // 4 if layer else 0
            for q in range(nq):
                v.wait_ge(s_wtP, q + 1)
                v.tensor_copy(wt[:, 4 * q:4 * q + 4, :].rearrange("e t p -> e (t p)"),
                              psH[q % 2][0:E, :]).then_inc(s_wtF, 1)
            for t in range(NT):
                v.wait_ge(s_wtP, nq + t + 1)
                v.tensor_tensor(X[:, t, :], X[:, t, :], psY[t % 4][:, 0:D], ALU.add).then_inc(s_wtF, 1)

            def take_rows(m, p):
                def take(n):
                    v.wait_ge(main.ys[p], m * 16 + 16)
                    for it in range(IT):
                        ins = v.tensor_scalar(yb[:, p, it, :], psY[p * IT + it][:, 0:D], 1.0 / WS, None, ALU.mult)
                    ins.then_inc(main.yF, 1)
                return take

            def bias_of(experts_of, c, m, p):
                def load():
                    e = v.value_load(experts_of[0:1, bass.ds(c, 1)], min_val=0, max_val=E - 1)
                    dve_bias(v, main, m, p, e)
                return load

            dve_turn(v, main, 0, 0)
            if layer:
                dve_bias(v, main, 0, 0, 0, wait=False)
            for first, last, splits in ((0, (E - EARLY) // 2, True), ((E - EARLY) // 2, NC // 2, False)):
                with v.Fori(first, last) as m:
                    for p in range(2):
                        dve_chunk(v, main, m, p, take_rows(m, p), splits, bias_of(table, m * 2 + p + 1, m + p, 1 - p))
            for i in range(2 * NT):
                t, q = i // 2, i % 2
                v.wait_ge(s_gy[i % GR], 16 * (i // GR + 1))
                v.wait_ge(s_wtF, nq + NT) if i == 0 else v.wait_ge(s_gu, i)
                v.scalar_tensor_tensor(X[:, t, :], gy[:, i % GR, :], wk[:, q, t:t + 1], X[:, t, :], ALU.mult,
                                       ALU.add).then_inc(s_gu, 1)
            v.wait_ge(s_gu, 2 * NT)
            if layer:
                def take_ties(e, c, p):
                    def take(n):
                        v.wait_ge(main.yF, n + 2)
                        for it in range(IT):
                            t = (c * 2 + p) * IT + it
                            xs = X[:, bass.ds(t, 1), :].rearrange("p a c -> p (a c)")
                            w = sc[:, bass.ds(t, 1), :].rearrange("p a e -> p (a e)")[:, bass.ds(e, 1)]
                            ins = v.scalar_tensor_tensor(xs, psY[p * IT + it][:, 0:D], w, xs, ALU.mult, ALU.add)
                        ins.then_inc(main.yF, 1)
                    return take

                found = v.value_load(flag[0:1, 0:1], min_val=0, max_val=T * E)
                with v.If(found > 0):
                    with v.Fori(0, E) as e:
                        with v.Fori(0, TC // 2) as c:
                            for p in range(2):
                                m = e * (TC // 2) + c
                                dve_chunk(v, main, m + NC // 2, p, take_ties(e, c, p), False,
                                          bias_of(tie_e, m * 2 + p + 1, m + p + NC // 2, 1 - p))
                    v.wait_ge(main.yF, NC + NTIE + 2)


def attention1(nc, X, identf, io):
    H, DH = 8, 32
    G = H * DH // P
    HG = H // G
    JT, JR = MT, MR
    KCH = chunks(M)
    NCK = len(KCH)
    NQ = KC * NT // 4 + G * B
    NGC = KC * -(-JT // 4)
    NV0 = NGC + G * NCK
    NW = NV0 + JT
    NA = 1 + ST * (NCK - 1)
    SCALE = DH ** -0.5
    KR = 3 * DH + 1
    VC = 2 * DH + 1
    LAG = 5
    PR = ring(JT, 7)
    SR = ring(JT, 4)
    R, NS = max(PR) + 1, max(SR) + 1
    VT = [2, 6, 10]
    GT = [j for j in range(JT) if j not in VT]

    with ExitStack() as ctx:
        def sb(name, shape, dt=F32):
            return ctx.enter_context(nc.sbuf_tensor("c_" + name, shape, dt))

        def sem(name):
            return ctx.enter_context(nc.semaphore("c_" + name))

        wf = sb("wf", [P, 3, G, D])
        wth, wtl = sb("wth", [P, 3, KC, D], F16), sb("wtl", [P, 3, KC, D], F16)
        st, mv = sb("st", [P, NT, 6]), sb("mv", [P, NT, 2])
        ve, mhalf, rstd = sb("ve", [P, NT]), sb("mhalf", [P, NT]), sb("rstd", [P, NT])
        qhs, qls = sb("qhs", [P, G, B * S], F16), sb("qls", [P, G, B * S], F16)
        qst = sb("qst", [P, H, B * S], F16)
        ltn = qst[:, 0:H // 2, :].rearrange("p h n -> p (h n)").bitcast(F32).rearrange("p (t c) -> p t c", c=D)
        lth = qst[:, H // 2:H // 2 + KC, :]
        ltl = qst[:, H // 2 + KC:H, :]
        kst = sb("kst", [P, H, M], F16)
        khs, kls = sb("khs", [P, G, M], F16), sb("kls", [P, G, M], F16)
        vst = sb("vst", [P, JT, H, VC], F16)
        cx = sb("cx", [P, JT, D])
        cth, ctl = sb("cth", [P, KC, M], F16), sb("ctl", [P, KC, M], F16)
        mx, mc = sb("mx", [P, ST, NCK]), sb("mc", [P, ST])
        pf = sb("pf", [P, R, S])
        ph, pl = sb("ph", [P, R, S], F16), sb("pl", [P, R, S], F16)
        of = sb("of", [VC, S])
        fold = sb("fold", [VC, DH + 1])
        rl = sb("rl", [P, ST])

        psA = [ctx.enter_context(nc.psum_tensor(f"c_psA{i}", [P, 512], F32)) for i in range(2)]
        psS = [ctx.enter_context(nc.psum_tensor(f"c_psS{i}", [P, 512], F32)) for i in range(NS)]
        psO = ctx.enter_context(nc.psum_tensor("c_psO", [P, 512], F32))
        psM = ctx.enter_context(nc.psum_tensor("c_psM", [P, 512], F32))
        ring4 = psA + psS[0:2]

        s_const = sem("const")
        s_w = sem("w")
        s_cx = sem("cx")
        s_st = sem("st")
        s_mv = sem("mv")
        s_pool = sem("pool")
        s_rstd = sem("rstd")
        s_nt = sem("nt")
        s_uP = sem("uP")
        s_uH = sem("uH")
        s_uL = sem("uL")
        s_q = sem("q")
        s_wP = sem("wP")
        s_wH = sem("wH")
        s_wL = sem("wL")
        s_k = [sem(f"k{g}") for g in range(G)]
        s_aP = sem("aP")
        s_aF = sem("aF")
        s_mc = sem("mc")
        s_mT = sem("mT")
        s_mr = sem("mr")
        s_sP = sem("sP")
        s_pF = sem("pF")
        s_pH = sem("pH")
        s_pL = sem("pL")
        s_pG = sem("pG")
        s_pv = sem("pv")
        s_oF = sem("oF")
        s_tP = sem("tP")
        s_rl = sem("rl")
        s_tF = sem("tF")

        block = ctx.enter_context(nc.Block(no_gpsimd_drain=True))
        NCONST = 6
        names = ("L1_xattn_Wq", "L1_xattn_Wk", "L1_xattn_Wv")

        def wait_low(eng, n, j):
            if j in VT:
                eng.wait_ge(s_pL, done(len(VT), n, VT.index(j)))
            else:
                eng.wait_ge(s_pG, done(len(GT), n, GT.index(j)))

        SLOTS = [[] for _ in range(JT)]
        for a in range(NA):
            SLOTS[a * 10 // NA].append(a)
        SLOTS[10].append("mc")
        SLOTS[11].append("mT")
        NEXT = [[] for _ in range(JT)]
        for i in range(NV0):
            NEXT[i * JT // NV0].append(f"W{i}")
        NONE = [[] for _ in range(JT)]

        @block.sync
        def _(sp):
            for i, name in enumerate(names):
                sp.dma_start(wf[:, i, :, :], io[name].rearrange("(g p) c -> p g c", p=P)).then_inc(s_w, 16)
            def load_context(b):
                src = io["ctx_1024"][bass.ds(b, 1), :, :].rearrange("a m c -> (a m) c")
                sp.dma_start(cx[:, 0:MT - 1, :],
                             src[0:(MT - 1) * P, :].rearrange("(t p) c -> p t c", p=P)).then_inc(s_cx, 16)
                sp.dma_start(cx[0:MR, MT - 1, :], src[(MT - 1) * P:M, :]).then_inc(s_cx, 16)

            load_context(0)
            sp.wait_ge(s_uL, 3 + NQ)
            for h in range(H):
                r0 = (h % HG) * DH
                for piece, src in enumerate((qhs, qhs, qls)):
                    sp.dma_start(qst[piece * DH:(piece + 1) * DH, h, :], src[r0:r0 + DH, h // HG, :]).then_inc(s_q, 16)
            def stack_keys(b):
                sp.wait_ge(s_sP, (b * H) * JT + JT)
                for g in range(G):
                    sp.wait_ge(s_wL, done(NW, b, NGC + (g + 1) * NCK - 1))
                    for u in range(HG):
                        for piece, src in enumerate((khs, kls, khs)):
                            sp.dma_start(kst[piece * DH:(piece + 1) * DH, g * HG + u, :],
                                         src[u * DH:(u + 1) * DH, g, :]).then_inc(s_k[g], 16)

            with sp.Fori(0, B - 1) as b:
                stack_keys(b)
                sp.wait_ge(s_wP, done(NW, b, NGC - 1))
                load_context(b + 1)
            stack_keys(B - 1)

        @block.gpsimd
        def _(g):
            g.memset(mhalf[:, :], -0.5).then_inc(s_const, 1)
            g.wait_ge(s_const, 1)
            g.wait_ge(s_mv, 1)
            g.tensor_scalar(ve[:, :], mv[:, :, 1], EPS, None, ALU.add).then_inc(s_pool, 1)
            g.wait_ge(s_pool, 1)
            g.tensor_tensor(rstd[:, :], ve[:, :], mhalf[:, :], ALU.pow).then_inc(s_rstd, 1)
            g.wait_ge(s_rstd, 1)
            for i, (t, val) in enumerate(((kst[3 * DH:KR, :, :], 1.0), (vst[:, :, :, 2 * DH:VC], WS),
                                          (fold[:, :], 0.0), (fold[2 * DH:VC, DH:DH + 1], 1.0))):
                g.memset(t, val).then_inc(s_const, 1)
                g.wait_ge(s_const, i + 2)
            g.affine_select(out=fold[0:2 * DH, 0:DH], in_=fold[0:2 * DH, 0:DH], compare_op=ALU.not_equal, fill=1.0,
                            base=0, pattern=[[-1, DH]], channel_multiplier=1).then_inc(s_pool, 1)
            g.wait_ge(s_pool, 2)
            g.affine_select(out=fold[0:2 * DH, 0:DH], in_=fold[0:2 * DH, 0:DH], compare_op=ALU.not_equal, fill=1.0,
                            base=-DH, pattern=[[-1, DH]], channel_multiplier=1).then_inc(s_pool, 1)
            g.wait_ge(s_pool, 3)
            g.sem_inc(s_const, 1)
            g.sem_inc(s_pG, len(GT))
            with g.Fori(0, B * H) as n:
                for j in GT:
                    r = rows(j, JT, JR)
                    dn, pj = before(PR, j)
                    g.wait_ge(s_pH, done(JT, n, j))
                    g.wait_ge(s_pv, done(JT, n + dn, pj))
                    g.tensor_tensor(pl[0:r, PR[j], :], pf[0:r, PR[j], :], ph[0:r, PR[j], :],
                                    ALU.subtract).then_inc(s_pG, 1)

        @block.scalar
        def _(act):
            act.sem_inc(s_wH, NW)
            act.sem_inc(s_pF, JT)
            act.sem_inc(s_pH, JT)
            act.sem_inc(s_oF, 1)
            for i in range(3 + NQ):
                act.wait_ge(s_uP, i + 1)
                ps = ring4[i % 4]
                if i < 3:
                    act.activation(wth[:, i, :, :].rearrange("p k n -> p (k n)"), ps[:, :], ACT.Copy,
                                   scale=WS).then_inc(s_uH, 1)
                elif i < 3 + KC * NT // 4:
                    k, q = (i - 3) % KC, (i - 3) // KC
                    act.activation(lth[:, k, q * 512:q * 512 + 512], ps[:, :], ACT.Copy).then_inc(s_uH, 1)
                else:
                    u = i - 3 - KC * NT // 4
                    g, b = u % G, u // G
                    act.activation(qhs[:, g, b * S:(b + 1) * S], ps[:, :], ACT.Copy, scale=1.0 / WS).then_inc(s_uH, 1)
            def event(b, i):
                act.wait_ge(s_wP, done(NW, b, i))
                if i < NGC:
                    k, q = i % KC, i // KC
                    n = min(512, M - q * 512)
                    act.activation(cth[:, k, q * 512:q * 512 + n], psA[i % 2][:, 0:n], ACT.Copy).then_inc(s_wH, 1)
                elif i < NV0:
                    g, c = divmod(i - NGC, NCK)
                    c0, cn = KCH[c]
                    act.activation(khs[:, g, c0:c0 + cn], psA[i % 2][:, 0:cn], ACT.Copy,
                                   scale=1.0 / WS).then_inc(s_wH, 1)
                else:
                    j = i - NV0
                    r = rows(j, JT, JR)
                    act.activation(vst[0:r, j, :, 0:DH], ring4[i % 4][0:r, 0:D].rearrange("p (h d) -> p h d", d=DH),
                                   ACT.Copy).then_inc(s_wH, 1)

            def batch(b, last):
                for i in range(NV0, NW):
                    event(b, i)

                def out_copy(n):
                    act.wait_ge(s_pv, done(JT, n, JT - 1))
                    act.wait_ge(s_tP, done(1, n, 0) - 1)
                    act.activation(of[:, :], psO[0:VC, :], ACT.Copy).then_inc(s_oF, 1)

                def main(h, with_tail, slots=NONE):
                    n = b * H + h
                    for j in range(JT):
                        r = rows(j, JT, JR)
                        dn, pj = before(PR, j)
                        if with_tail and j == LAG:
                            out_copy(n - 1)
                        act.wait_ge(s_sP, done(JT, n, j))
                        wait_low(act, n + dn, pj)
                        act.activation(pf[0:r, PR[j], :], psS[SR[j]][0:r, :], ACT.Exp, scale=SCALE).then_inc(s_pF, 1)
                        act.wait_ge(s_pv, done(JT, n + dn, pj))
                        act.activation(ph[0:r, PR[j], :], psS[SR[j]][0:r, :], ACT.Exp, scale=SCALE).then_inc(s_pH, 1)
                        for what in slots[j]:
                            event(b + 1, int(what[1:]))

                main(0, False)
                with act.Fori(1, H - 1) as h:
                    main(h, True)
                main(H - 1, True, NONE if last else NEXT)
                out_copy(b * H + (H - 1))

            for i in range(NV0):
                event(0, i)
            with act.Fori(0, B - 1) as b:
                batch(b, False)
            batch(B - 1, True)

        @block.tensor
        def _(pe):
            pe.sem_inc(s_wP, NW)
            pe.sem_inc(s_aP, NA)
            pe.sem_inc(s_mT, 1)
            pe.sem_inc(s_sP, JT)
            pe.sem_inc(s_pv, JT)
            pe.sem_inc(s_tP, 1)

            def triple(out, hi, lo, xh_, xl_, first=True, last=True):
                pe.matmul(out, hi, xh_, start=first, stop=False)
                pe.matmul(out, hi, xl_, start=False, stop=False)
                return pe.matmul(out, lo, xh_, start=False, stop=last)

            pe.wait_ge(s_w, 48)
            for i in range(3 + NQ):
                ps = ring4[i % 4]
                if i >= 4:
                    pe.wait_ge(s_uL, i - 3)
                if i < 3:
                    for k in range(KC):
                        for g in range(G):
                            o = (k * G + g) * P
                            ins = pe.transpose(ps[:, o:o + P], wf[:, i, g, k * P:(k + 1) * P], identf[:, :])
                elif i < 3 + KC * NT // 4:
                    k, q = (i - 3) % KC, (i - 3) // KC
                    pe.wait_ge(s_nt, 4 * q + 4)
                    for u in range(4):
                        ins = pe.transpose(ps[:, u * P:(u + 1) * P], ltn[:, 4 * q + u, k * P:(k + 1) * P],
                                           identf[:, :])
                else:
                    u = i - 3 - KC * NT // 4
                    g, b = u % G, u // G
                    if u == 0:
                        pe.wait_ge(s_uL, 3 + KC * NT // 4)
                    ts = slice(b * S, (b + 1) * S)
                    for k in range(KC):
                        ws = slice(g * P, (g + 1) * P)
                        ins = triple(ps[:, :], wth[:, 0, k, ws], wtl[:, 0, k, ws], lth[:, k, ts], ltl[:, k, ts],
                                     k == 0, k == KC - 1)
                ins.then_inc(s_uP, 1)
            pe.wait_ge(s_uL, 3 + NQ)
            pe.wait_ge(s_const, NCONST)

            def event(b, i):
                if i == 0:
                    pe.wait_ge(s_aF, (b * H) * NA + NA)
                    pe.wait_ge(s_cx, b * 32 + 32)
                elif i == NV0:
                    pe.wait_ge(s_wL, done(NW, b, NV0 - 1))
                    pe.wait_ge(s_pH, (b * H) * JT + JT)
                elif i == NGC:
                    pe.wait_ge(s_wL, done(NW, b, NGC - 1))
                elif i < NV0 and i >= 2:
                    pe.wait_ge(s_wL, done(NW, b, i - 2))
                elif i >= NV0 + 4:
                    pe.wait_ge(s_wL, done(NW, b, i - 4))
                if i < NGC:
                    k, q = i % KC, i // KC
                    for u in range(4):
                        tl = q * 4 + u
                        if tl >= JT:
                            break
                        r = rows(tl, JT, JR)
                        ins = pe.transpose(psA[i % 2][:, u * P:u * P + r], cx[0:r, tl, k * P:(k + 1) * P],
                                           identf[0:r, 0:r])
                elif i < NV0:
                    g, c = divmod(i - NGC, NCK)
                    c0, cn = KCH[c]
                    for k in range(KC):
                        ws = slice(g * P, (g + 1) * P)
                        ins = triple(psA[i % 2][:, 0:cn], wth[:, 1, k, ws], wtl[:, 1, k, ws], cth[:, k, c0:c0 + cn],
                                     ctl[:, k, c0:c0 + cn], k == 0, k == KC - 1)
                else:
                    j = i - NV0
                    r = rows(j, JT, JR)
                    js = slice(j * P, j * P + r)
                    for k in range(KC):
                        ins = triple(ring4[i % 4][0:r, 0:D], cth[:, k, js], ctl[:, k, js], wth[:, 2, k, :],
                                     wtl[:, 2, k, :], k == 0, k == KC - 1)
                ins.then_inc(s_wP, 1)

            def batch(b, last):
                for i in range(NV0, NW):
                    event(b, i)

                def head(t, h, cs, r=P):
                    return t[0:r, bass.ds(h, 1), cs].rearrange("p a n -> p (a n)")

                def pre(n, h, what, first=False):
                    if what == "mc":
                        return
                    if what == "mT":
                        pe.wait_ge(s_mc, done(1, n, 0))
                        pe.wait_ge(s_tF, done(1, n, 0) - (0 if first else 1))
                        for it in range(ST):
                            ins = pe.transpose(psM[0:1, it * P:(it + 1) * P], mc[:, it:it + 1], identf[:, :])
                        ins.then_inc(s_mT, 1)
                        return
                    a = what
                    pe.wait_ge(s_aF, done(NA, n, a - 2 if a != 0 else -1))
                    if a == 0:
                        for it in range(ST):
                            c0, cn = KCH[-1]
                            ins = pe.matmul(psA[0][:, it * cn:(it + 1) * cn],
                                            head(qst, h, bass.ds(b * S + it * P, P), KR - 1),
                                            head(kst, h, slice(c0, c0 + cn), KR - 1), start=True, stop=True)
                        ins.then_inc(s_aP, 1)
                        return
                    it, c = divmod(a - 1, NCK - 1)
                    c0, cn = KCH[c]
                    pe.matmul(psA[a % 2][:, 0:cn], head(qst, h, bass.ds(b * S + it * P, P), KR - 1),
                              head(kst, h, slice(c0, c0 + cn), KR - 1), start=True, stop=True).then_inc(s_aP, 1)

                def pv(n, h, j):
                    r = rows(j, JT, JR)
                    w = vst[0:r, j, bass.ds(h, 1), :].rearrange("p a n -> p (a n)")
                    pe.wait_ge(s_pH, done(JT, n, j))
                    if j == 0:
                        pe.wait_ge(s_oF, done(1, n, 0) - 1)
                    pe.matmul(psO[0:VC, :], w, ph[0:r, PR[j], :], start=(j == 0), stop=False)
                    wait_low(pe, n, j)
                    pe.matmul(psO[0:VC, :], w, pl[0:r, PR[j], :], start=False, stop=(j == JT - 1)).then_inc(s_pv, 1)

                def tail(n, last=False):
                    pe.wait_ge(s_oF, done(1, n, 0))
                    if last:
                        pe.wait_ge(s_tF, done(1, n, 0))
                    else:
                        pe.wait_ge(s_mr, done(1, n, 0) + 1)
                    for it in range(ST):
                        ins = pe.matmul(psM[:, it * (DH + 1):(it + 1) * (DH + 1)], of[:, it * P:(it + 1) * P],
                                        fold[:, :], start=True, stop=True)
                    ins.then_inc(s_tP, 1)

                def main(h, slots, with_tail):
                    n = b * H + h
                    for j in range(JT):
                        r = rows(j, JT, JR)
                        dn, pj = before(SR, j)
                        pe.wait_ge(s_pH, done(JT, n + dn, pj))
                        if j == 0:
                            pe.wait_ge(s_mr, done(1, n, 0))
                        pe.matmul(psS[SR[j]][0:r, :], head(kst, h, slice(j * P, j * P + r), KR),
                                  head(qst, h, bass.ds(b * S, S), KR), start=True, stop=True).then_inc(s_sP, 1)
                        for what in slots[j]:
                            if slots is NEXT:
                                event(b + 1, int(what[1:]))
                            else:
                                pre(n + 1, h + 1, what)
                        if j >= LAG:
                            pv(n, h, j - LAG)
                        elif with_tail:
                            pv(n - 1, h - 1, JT - LAG + j)
                        if with_tail and j == LAG + 1:
                            tail(n - 1)

                pe.wait_ge(s_wL, done(NW, b, NW - 1))
                pe.wait_ge(s_k[0], (b + 1) * (3 * HG * 16))
                pe.wait_ge(s_q, 3 * H * 16)
                for what in sum(SLOTS, []):
                    pre(b * H, 0, what, True)
                pe.wait_ge(s_k[1], (b + 1) * (3 * HG * 16))
                main(0, SLOTS, False)
                with pe.Fori(1, H - 1) as h:
                    main(h, SLOTS, True)
                main(H - 1, NONE if last else NEXT, True)
                for j in range(JT - LAG, JT):
                    pv(b * H + (H - 1), H - 1, j)
                tail(b * H + (H - 1), True)

            for i in range(NV0):
                event(0, i)
            with pe.Fori(0, B - 1) as b:
                batch(b, False)
            batch(B - 1, True)

        @block.vector
        def _(v):
            v.sem_inc(s_wL, NW)
            v.sem_inc(s_aF, NA)
            v.sem_inc(s_mc, 1)
            v.sem_inc(s_mr, 1)
            v.sem_inc(s_pL, len(VT))
            v.sem_inc(s_rl, 1)
            v.sem_inc(s_tF, 2)
            ch = Chain(v, s_st)
            for t in range(NT):
                ch.step(v.bn_stats(st[:, t, :], X[:, t, :]))
            ch.wait()
            for t in range(NT):
                ch.step(v.bn_aggr(mv[:, t, :], st[:, t, :]))
            ch.wait()
            v.sem_inc(s_mv, 1)
            v.wait_ge(s_rstd, 1)
            for t in range(NT):
                v.tensor_scalar(ltn[:, t, :], X[:, t, :], mv[:, t, 0:1], rstd[:, t:t + 1], ALU.subtract,
                                ALU.mult).then_inc(s_nt, 1)
            for i in range(3 + NQ):
                ps = ring4[i % 4]
                v.wait_ge(s_uH, i + 1)
                if i < 3:
                    v.scalar_tensor_tensor(wtl[:, i, :, :].rearrange("p k n -> p (k n)"), ps[:, :], WS,
                                           wth[:, i, :, :].rearrange("p k n -> p (k n)"), ALU.mult,
                                           ALU.subtract).then_inc(s_uL, 1)
                elif i < 3 + KC * NT // 4:
                    k, q = (i - 3) % KC, (i - 3) // KC
                    cs = slice(q * 512, q * 512 + 512)
                    v.tensor_tensor(ltl[:, k, cs], ps[:, :], lth[:, k, cs], ALU.subtract).then_inc(s_uL, 1)
                else:
                    u = i - 3 - KC * NT // 4
                    g, b = u % G, u // G
                    cs = slice(b * S, (b + 1) * S)
                    v.scalar_tensor_tensor(qls[:, g, cs], ps[:, :], 1.0 / WS, qhs[:, g, cs], ALU.mult,
                                           ALU.subtract).then_inc(s_uL, 1)
            def event(b, i):
                v.wait_ge(s_wH, done(NW, b, i))
                if i < NGC:
                    k, q = i % KC, i // KC
                    n = min(512, M - q * 512)
                    cs = slice(q * 512, q * 512 + n)
                    v.tensor_tensor(ctl[:, k, cs], psA[i % 2][:, 0:n], cth[:, k, cs], ALU.subtract).then_inc(s_wL, 1)
                elif i < NV0:
                    g, c = divmod(i - NGC, NCK)
                    c0, cn = KCH[c]
                    v.scalar_tensor_tensor(kls[:, g, c0:c0 + cn], psA[i % 2][:, 0:cn], 1.0 / WS,
                                           khs[:, g, c0:c0 + cn], ALU.mult, ALU.subtract).then_inc(s_wL, 1)
                else:
                    j = i - NV0
                    r = rows(j, JT, JR)
                    v.tensor_tensor(vst[0:r, j, :, DH:2 * DH],
                                    ring4[i % 4][0:r, 0:D].rearrange("p (h d) -> p h d", d=DH),
                                    vst[0:r, j, :, 0:DH], ALU.subtract).then_inc(s_wL, 1)

            def batch(b, last):
                for i in range(NV0, NW):
                    event(b, i)

                def pre(n, h, what):
                    if what == "mc":
                        v.wait_ge(s_aF, done(NA, n, NA - 1))
                        v.tensor_reduce(mc[:, :], mx[:, :, :], AX.X, ALU.max).then_inc(s_mc, 1)
                        return
                    if what == "mT":
                        v.wait_ge(s_mT, done(1, n, 0))
                        v.tensor_scalar(qst[KR - 1:KR, bass.ds(h, 1), bass.ds(b * S, S)].rearrange("p a n -> p (a n)"),
                                        psM[0:1, :], -1.0, None, ALU.mult).then_inc(s_mr, 1)
                        return
                    v.wait_ge(s_aP, done(NA, n, what))
                    if what == 0:
                        cn = KCH[-1][1]
                        v.tensor_reduce(mx[:, :, NCK - 1], psA[0][:, 0:ST * cn].rearrange("p (t n) -> p t n", n=cn), AX.X,
                                        ALU.max).then_inc(s_aF, 1)
                        return
                    it, c = divmod(what - 1, NCK - 1)
                    c0, cn = KCH[c]
                    v.tensor_reduce(mx[:, it, c:c + 1], psA[what % 2][:, 0:cn], AX.X, ALU.max).then_inc(s_aF, 1)

                def tail(n, h):
                    v.wait_ge(s_tP, done(1, n, 0))
                    pt = psM[:, 0:ST * (DH + 1)].rearrange("p (t n) -> p t n", n=DH + 1)
                    v.reciprocal(rl[:, :], pt[:, :, DH]).then_inc(s_rl, 1)
                    v.wait_ge(s_rl, done(1, n, 0))
                    for it in range(ST):
                        xs = X[:, bass.ds(b * ST + it, 1), bass.ds(h * DH, DH)].rearrange("p a c -> p (a c)")
                        ins = v.scalar_tensor_tensor(xs, pt[:, it, 0:DH], rl[:, it:it + 1], xs, ALU.mult, ALU.add)
                    ins.then_inc(s_tF, 1)

                def main(h, slots, with_tail):
                    n = b * H + h
                    for slot in range(JT):
                        j = slot - 2
                        if j in VT:
                            r = rows(j, JT, JR)
                            dn, pj = before(PR, j)
                            v.wait_ge(s_pH, done(JT, n, j))
                            v.wait_ge(s_pv, done(JT, n + dn, pj))
                            v.tensor_tensor(pl[0:r, PR[j], :], pf[0:r, PR[j], :], ph[0:r, PR[j], :],
                                            ALU.subtract).then_inc(s_pL, 1)
                        for what in slots[slot]:
                            if slots is NEXT:
                                event(b + 1, int(what[1:]))
                            else:
                                pre(n + 1, h + 1, what)
                        if with_tail and slot == LAG + 2:
                            tail(n - 1, h - 1)

                for what in sum(SLOTS, []):
                    pre(b * H, 0, what)
                main(0, SLOTS, False)
                with v.Fori(1, H - 1) as h:
                    main(h, SLOTS, True)
                main(H - 1, NONE if last else NEXT, True)
                tail(b * H + (H - 1), H - 1)

            for i in range(NV0):
                event(0, i)
            with v.Fori(0, B - 1) as b:
                batch(b, False)
            batch(B - 1, True)
            v.wait_ge(s_tF, B * H + 2)


def build(nc, io, out, phases):
    with ExitStack() as ctx:
        X = ctx.enter_context(nc.sbuf_tensor("X", [P, NT, D], F32))
        identf = ctx.enter_context(nc.sbuf_tensor("identf", [P, P], F32))
        s_id = ctx.enter_context(nc.semaphore("s_id"))
        s_out = ctx.enter_context(nc.semaphore("s_out"))
        s_x = ctx.enter_context(nc.semaphore("s_x"))
        with nc.Block(no_gpsimd_drain=True) as block:
            @block.sync
            def _(sp):
                sp.dma_start(X[:, :, :], io["x"].rearrange("b (t p) c -> p (b t) c", p=P)).then_inc(s_x, 16)
                sp.wait_ge(s_x, 16)

            @block.gpsimd
            def _(g):
                g.memset(identf[:, :], 0.0).then_inc(s_id, 1)
                g.wait_ge(s_id, 1)
                g.affine_select(out=identf[:, :], in_=identf[:, :], compare_op=ALU.not_equal, fill=1.0, base=0,
                                pattern=[[-1, P]], channel_multiplier=1).then_inc(s_id, 1)
                g.wait_ge(s_id, 2)
        if "A" in phases:
            attention0(nc, X, identf, io)
        if "B" in phases:
            experts(nc, X, identf, io, 0)
        if "C" in phases:
            attention1(nc, X, identf, io)
        if "D" in phases:
            experts(nc, X, identf, io, 1)
        with nc.Block(no_gpsimd_drain=True) as block:
            @block.sync
            def _(sp):
                sp.dma_start(out.rearrange("b (t p) c -> p (b t) c", p=P), X[:, :, :]).then_inc(s_out, 16)
                sp.wait_ge(s_out, 16)


PHASES = "ABCD"
_INS = ['x', 'ctx_1024', 'L0_xattn_gamma_media', 'L0_xattn_beta_media', 'L0_xattn_gamma_lat', 'L0_xattn_beta_lat',
        'L0_xattn_Wq', 'L0_xattn_bq', 'L0_xattn_Wkv', 'L0_xattn_bkv', 'L0_xattn_Wo', 'L0_xattn_bo',
        'L0_ffn_w_router', 'L0_ffn_w1', 'L0_ffn_w2', 'L0_ffn_bias', 'L1_xattn_Wq', 'L1_xattn_Wk', 'L1_xattn_Wv',
        'L1_ffn_W1', 'L1_ffn_b1', 'L1_ffn_W2', 'L1_ffn_b2', 'L1_ffn_Wr', 'L1_ffn_br']


def kernel(**inputs):
    import numpy as np
    import concourse.bacc as bacc
    from concourse.bass_utils import run_bass_kernel_spmd

    nc = bacc.Bacc("TRN2", target_bir_lowering=False, num_devices=1)
    arrays, io = {}, {}
    for name in _INS:
        a = np.ascontiguousarray(inputs[name])
        arrays[f"in_{name}"] = a
        io[name] = nc.dram_tensor(f"in_{name}", a.shape, F32, kind="ExternalInput").ap()
    out = nc.dram_tensor("out_0", (B, S, D), F32, kind="ExternalOutput").ap()
    build(nc, io, out, PHASES)
    r = run_bass_kernel_spmd(nc, [arrays], core_ids=[0])
    return r.results[0]["out_0"]
```
